# Optimizing a Trainium2 kernel written in Bass

```python
import numpy as np
import jax
import jax.numpy as jnp

def _softmax(x, axis=-1):
    return jax.nn.softmax(x, axis=axis)

def _gelu(x):
    return jax.nn.gelu(x, approximate=True)

def _silu(x):
    return jax.nn.silu(x)

def _sigmoid(x):
    return jax.nn.sigmoid(x)

def _layernorm(x, axis=-1, eps=1e-05):
    m = jnp.mean(x, axis=axis, keepdims=True)
    v = jnp.var(x, axis=axis, keepdims=True)
    return (x - m) / jnp.sqrt(v + eps)

def _scatter_add(tgt, idx, src, axis=0):
    return tgt.at[idx].add(src)

def _segment_sum(src, seg, n):
    return jax.ops.segment_sum(src, seg, n)
kernel_name = 'mk_prb_d2_jaxref_r4_fe1814'

def setup_inputs(seed: int=0):
    np.random.seed(seed)
    _w = jnp.asarray

    def _L0_attn_setup():
        import jax, jax.numpy as jnp
        import numpy as np
        import math
        D_MODEL = 256
        EXPAND = 2
        D_INNER = EXPAND * D_MODEL
        HEADDIM = 64
        NHEADS = D_INNER // HEADDIM
        D_STATE = 128
        D_CONV = 4
        CHUNK = 128
        SEQLEN = 1024
        BATCH = 1
        CONV_DIM = D_INNER + 2 * (2 * D_STATE)
        D_IN_PROJ = 2 * D_INNER + 2 * (2 * D_STATE) + 2 * NHEADS
        EPS = 1e-05

        def silu(x):
            return x * jax.nn.sigmoid(x)

        def segsum_exp(a):
            T = a.shape[-1]
            m1 = jnp.tril(jnp.ones((T, T), bool), -1)
            s = jnp.cumsum(jnp.where(m1, a[..., :, None], 0.0), axis=-2)
            m0 = jnp.tril(jnp.ones((T, T), bool))
            return jnp.where(m0, jnp.exp(jnp.where(m0, s, 0.0)), 0.0)

        def ssd(x, A, B, C, chunk):
            b, L, h, p = x.shape
            c = L // chunk
            x = x.reshape(b, c, chunk, h, p)
            A = A.reshape(b, c, chunk, h).transpose(0, 3, 1, 2)
            B = B.reshape(b, c, chunk, -1)
            C = C.reshape(b, c, chunk, -1)
            A_cs = jnp.cumsum(A, axis=-1)
            Lmat = segsum_exp(A)
            Y_diag = jnp.einsum('bcln,bcsn,bhcls,bcshp->bclhp', C, B, Lmat, x)
            decay_states = jnp.exp(A_cs[..., -1:] - A_cs)
            states = jnp.einsum('bcln,bhcl,bclhp->bchpn', B, decay_states, x)
            states = jnp.concatenate([jnp.zeros_like(states[:, :1]), states], axis=1)
            decay_chunk = segsum_exp(jnp.pad(A_cs[..., -1], ((0, 0), (0, 0), (1, 0))))
            new_states = jnp.einsum('bhzc,bchpn->bzhpn', decay_chunk, states)
            states, final_state = (new_states[:, :-1], new_states[:, -1])
            Y_off = jnp.einsum('bcln,bchpn,bhcl->bclhp', C, states, jnp.exp(A_cs))
            Y = (Y_diag + Y_off).reshape(b, L, h, p)
            return (Y, final_state)
        key = jax.random.key(seed)
        ks = jax.random.split(key, 8)
        s = 0.02
        u = jax.random.normal(ks[0], (BATCH, SEQLEN, D_MODEL), jnp.float32)
        in_proj_w = jax.random.normal(ks[1], (D_IN_PROJ, D_MODEL), jnp.float32) * s
        conv_w = jax.random.normal(ks[2], (CONV_DIM, 1, D_CONV), jnp.float32) * (1.0 / math.sqrt(D_CONV))
        conv_b = jnp.zeros((CONV_DIM,), jnp.float32)
        dt = jnp.exp(jax.random.uniform(ks[3], (NHEADS,)) * (math.log(0.1) - math.log(0.001)) + math.log(0.001))
        dt = jnp.clip(dt, 0.0001)
        dt_bias = dt + jnp.log(-jnp.expm1(-dt))
        A_log = jnp.log(jax.random.uniform(ks[4], (NHEADS,), minval=1.0, maxval=16.0))
        D = jnp.ones((NHEADS,), jnp.float32)
        fc_D_w = jax.random.normal(ks[5], (NHEADS, D_INNER), jnp.float32) * s
        norm_w = jnp.ones((D_INNER,), jnp.float32)
        out_proj_w = jax.random.normal(ks[6], (D_MODEL, D_INNER), jnp.float32) * s
        return dict(u=u, in_proj_w=in_proj_w, conv_w=conv_w, conv_b=conv_b, dt_bias=dt_bias, A_log=A_log, D=D, fc_D_w=fc_D_w, norm_w=norm_w, out_proj_w=out_proj_w)
    _L0_attn_in = _L0_attn_setup()

    def _L0_ffn_setup():
        import jax, jax.numpy as jnp
        import numpy as np
        H, E, DFF = (256, 8, 1024)
        key = jax.random.key(seed)
        ks = jax.random.split(key, 7)
        s = lambda *shape: 1.0 / np.sqrt(shape[-2] if len(shape) > 1 else shape[-1])
        x = jax.random.normal(ks[0], (2, 512, H), dtype=jnp.float32)
        Wr = jax.random.normal(ks[1], (H, E), dtype=jnp.float32) * (1.0 / np.sqrt(H))
        br = jnp.zeros((E,), dtype=jnp.float32)
        W1 = jax.random.normal(ks[2], (E, H, DFF), dtype=jnp.float32) * (1.0 / np.sqrt(H))
        b1 = jnp.zeros((E, DFF), dtype=jnp.float32)
        W2 = jax.random.normal(ks[3], (E, DFF, H), dtype=jnp.float32) * (1.0 / np.sqrt(DFF))
        b2 = jnp.zeros((E, H), dtype=jnp.float32)
        return {'x': x, 'Wr': Wr, 'br': br, 'W1': W1, 'b1': b1, 'W2': W2, 'b2': b2}
    _L0_ffn_in = _L0_ffn_setup()

    def _L1_attn_setup():
        import jax, jax.numpy as jnp
        import numpy as np
        D_MODEL = 256
        N_HEADS = 16
        HEAD_DIM = D_MODEL // N_HEADS
        D_LATENT = 64
        LAMBDA_DECAY = 0.01
        TIME_STEP = 0.01
        CLAMP = 10000.0

        def _reference_tuple_inner(x, Wq, Wk, Wv, Wo, W_down_kv, W_up_k, W_up_v):
            B, S, _ = x.shape
            q = x @ Wq
            k = x @ Wk
            v = x @ Wv
            latent_kv = (k + v) @ W_down_kv
            k_rec = latent_kv @ W_up_k
            v_rec = latent_kv @ W_up_v

            def heads(t):
                return t.reshape(B, S, N_HEADS, HEAD_DIM).transpose(0, 2, 1, 3)
            qh, kh, vh = (heads(q), heads(k_rec), heads(v_rec))
            scale = 1.0 / (jnp.sqrt(jnp.float32(D_MODEL)) + 1e-08)
            scores = jnp.einsum('bhqd,bhkd->bhqk', qh, kh) * scale
            scores = jnp.clip(jnp.nan_to_num(scores, nan=-1000000000.0), -CLAMP, CLAMP)
            idx = jnp.arange(S, dtype=jnp.float32)
            decay = jnp.exp(-LAMBDA_DECAY * TIME_STEP * jnp.abs(idx[:, None] - idx[None, :]))
            scores = scores * decay[None, None, :, :]
            scores = jnp.clip(jnp.nan_to_num(scores, nan=-1000000000.0), -CLAMP, CLAMP)
            attn = jax.nn.softmax(scores, axis=-1)
            out = jnp.einsum('bhqk,bhkd->bhqd', attn, vh)
            out = out.transpose(0, 2, 1, 3).reshape(B, S, D_MODEL)
            return (out @ Wo, latent_kv)
        key = jax.random.key(seed)
        ks = jax.random.split(key, 8)
        B, S = (2, 512)

        def w(k, i, o):
            return jax.random.normal(k, (i, o), dtype=jnp.float32) * 0.02
        return {'x': jax.random.normal(ks[0], (B, S, D_MODEL), dtype=jnp.float32), 'Wq': w(ks[1], D_MODEL, D_MODEL), 'Wk': w(ks[2], D_MODEL, D_MODEL), 'Wv': w(ks[3], D_MODEL, D_MODEL), 'Wo': w(ks[4], D_MODEL, D_MODEL), 'W_down_kv': w(ks[5], D_MODEL, D_LATENT), 'W_up_k': w(ks[6], D_LATENT, D_MODEL), 'W_up_v': w(ks[7], D_LATENT, D_MODEL)}
    _L1_attn_in = _L1_attn_setup()

    def _L1_ffn_setup():
        import math
        import jax, jax.numpy as jnp
        import numpy as np
        NUM_EXPERTS = 8
        TOP_K = 2
        CAPACITY_FACTOR = 1.0
        B, S, H, I = (4, 512, 256, 1024)
        key = jax.random.key(seed)
        k_x, k_rw, k_wi, k_wo = jax.random.split(key, 4)
        x = jax.random.normal(k_x, (B, S, H), dtype=jnp.float32)
        lim = math.sqrt(6.0 / (H + NUM_EXPERTS))
        router_w = jax.random.uniform(k_rw, (NUM_EXPERTS, H), minval=-lim, maxval=lim, dtype=jnp.float32)
        router_b = jnp.zeros((NUM_EXPERTS,), dtype=jnp.float32)
        experts_inter = jax.random.normal(k_wi, (NUM_EXPERTS - 1, H, I), dtype=jnp.float32) / math.sqrt(H)
        experts_out = jax.random.normal(k_wo, (NUM_EXPERTS - 1, I, H), dtype=jnp.float32) / math.sqrt(I)
        return {'x': x, 'router_w': router_w, 'router_b': router_b, 'experts_inter': experts_inter, 'experts_out': experts_out}
    _L1_ffn_in = _L1_ffn_setup()
    _d = {'L0_attn_u': _L0_attn_in['u'], 'L0_attn_in_proj_w': _L0_attn_in['in_proj_w'], 'L0_attn_conv_w': _L0_attn_in['conv_w'], 'L0_attn_conv_b': _L0_attn_in['conv_b'], 'L0_attn_dt_bias': _L0_attn_in['dt_bias'], 'L0_attn_A_log': _L0_attn_in['A_log'], 'L0_attn_D': _L0_attn_in['D'], 'L0_attn_fc_D_w': _L0_attn_in['fc_D_w'], 'L0_attn_norm_w': _L0_attn_in['norm_w'], 'L0_attn_out_proj_w': _L0_attn_in['out_proj_w'], 'L0_ffn_Wr': _L0_ffn_in['Wr'], 'L0_ffn_br': _L0_ffn_in['br'], 'L0_ffn_W1': _L0_ffn_in['W1'], 'L0_ffn_b1': _L0_ffn_in['b1'], 'L0_ffn_W2': _L0_ffn_in['W2'], 'L0_ffn_b2': _L0_ffn_in['b2'], 'L1_attn_Wq': _L1_attn_in['Wq'], 'L1_attn_Wk': _L1_attn_in['Wk'], 'L1_attn_Wv': _L1_attn_in['Wv'], 'L1_attn_Wo': _L1_attn_in['Wo'], 'L1_attn_W_down_kv': _L1_attn_in['W_down_kv'], 'L1_attn_W_up_k': _L1_attn_in['W_up_k'], 'L1_attn_W_up_v': _L1_attn_in['W_up_v'], 'L1_ffn_router_w': _L1_ffn_in['router_w'], 'L1_ffn_router_b': _L1_ffn_in['router_b'], 'L1_ffn_experts_inter': _L1_ffn_in['experts_inter'], 'L1_ffn_experts_out': _L1_ffn_in['experts_out']}
    _x0 = _d['L0_attn_u']
    _d['L0_attn_u'] = jax.random.normal(jax.random.fold_in(jax.random.key(seed), 1), (8, 512, 256), dtype=_x0.dtype)
    del _x0
    return _d

def reference(L0_attn_u, L0_attn_in_proj_w, L0_attn_conv_w, L0_attn_conv_b, L0_attn_dt_bias, L0_attn_A_log, L0_attn_D, L0_attn_fc_D_w, L0_attn_norm_w, L0_attn_out_proj_w, L0_ffn_Wr, L0_ffn_br, L0_ffn_W1, L0_ffn_b1, L0_ffn_W2, L0_ffn_b2, L1_attn_Wq, L1_attn_Wk, L1_attn_Wv, L1_attn_Wo, L1_attn_W_down_kv, L1_attn_W_up_k, L1_attn_W_up_v, L1_ffn_router_w, L1_ffn_router_b, L1_ffn_experts_inter, L1_ffn_experts_out):

    def _L0_attn_ref(u, in_proj_w, conv_w, conv_b, dt_bias, A_log, D, fc_D_w, norm_w, out_proj_w):
        import jax, jax.numpy as jnp
        import numpy as np
        import math
        D_MODEL = 256
        EXPAND = 2
        D_INNER = EXPAND * D_MODEL
        HEADDIM = 64
        NHEADS = D_INNER // HEADDIM
        D_STATE = 128
        D_CONV = 4
        CHUNK = 128
        SEQLEN = 1024
        BATCH = 1
        CONV_DIM = D_INNER + 2 * (2 * D_STATE)
        D_IN_PROJ = 2 * D_INNER + 2 * (2 * D_STATE) + 2 * NHEADS
        EPS = 1e-05

        def silu(x):
            return x * jax.nn.sigmoid(x)

        def segsum_exp(a):
            T = a.shape[-1]
            m1 = jnp.tril(jnp.ones((T, T), bool), -1)
            s = jnp.cumsum(jnp.where(m1, a[..., :, None], 0.0), axis=-2)
            m0 = jnp.tril(jnp.ones((T, T), bool))
            return jnp.where(m0, jnp.exp(jnp.where(m0, s, 0.0)), 0.0)

        def ssd(x, A, B, C, chunk):
            b, L, h, p = x.shape
            c = L // chunk
            x = x.reshape(b, c, chunk, h, p)
            A = A.reshape(b, c, chunk, h).transpose(0, 3, 1, 2)
            B = B.reshape(b, c, chunk, -1)
            C = C.reshape(b, c, chunk, -1)
            A_cs = jnp.cumsum(A, axis=-1)
            Lmat = segsum_exp(A)
            Y_diag = jnp.einsum('bcln,bcsn,bhcls,bcshp->bclhp', C, B, Lmat, x)
            decay_states = jnp.exp(A_cs[..., -1:] - A_cs)
            states = jnp.einsum('bcln,bhcl,bclhp->bchpn', B, decay_states, x)
            states = jnp.concatenate([jnp.zeros_like(states[:, :1]), states], axis=1)
            decay_chunk = segsum_exp(jnp.pad(A_cs[..., -1], ((0, 0), (0, 0), (1, 0))))
            new_states = jnp.einsum('bhzc,bchpn->bzhpn', decay_chunk, states)
            states, final_state = (new_states[:, :-1], new_states[:, -1])
            Y_off = jnp.einsum('bcln,bchpn,bhcl->bclhp', C, states, jnp.exp(A_cs))
            Y = (Y_diag + Y_off).reshape(b, L, h, p)
            return (Y, final_state)
        b, l, _ = u.shape
        zxbcdt = u @ in_proj_w.T
        z = zxbcdt[..., :D_INNER]
        xBC = zxbcdt[..., D_INNER:D_INNER + CONV_DIM]
        dt = zxbcdt[..., D_INNER + CONV_DIM:]
        dt = jnp.concatenate([dt[..., :NHEADS], jnp.flip(dt[..., NHEADS:], axis=1)], axis=0)
        dt = jax.nn.softplus(dt + dt_bias)
        xc = jnp.transpose(xBC, (0, 2, 1))
        xc = jax.lax.conv_general_dilated(xc, conv_w, (1,), [(D_CONV - 1, 0)], feature_group_count=CONV_DIM, dimension_numbers=('NCH', 'OIH', 'NCH'))
        xc = xc + conv_b[None, :, None]
        xBC = silu(jnp.transpose(xc, (0, 2, 1)))
        x = xBC[..., :D_INNER]
        BC = xBC[..., D_INNER:]
        x_og = x
        x2 = jnp.concatenate([x, jnp.flip(x, 1)], axis=0)
        BC = jnp.concatenate([BC[..., :2 * D_STATE], jnp.flip(BC[..., 2 * D_STATE:], 1)], axis=0)
        B = BC[..., :D_STATE]
        C = BC[..., D_STATE:]
        xh = x2.reshape(2 * b, l, NHEADS, HEADDIM)
        A = -jnp.exp(A_log)
        Y, final_state = ssd(xh * dt[..., None], A * dt, B, C, CHUNK)
        y = Y + xh * D[:, None]
        y = y.reshape(2 * b, l, D_INNER)
        y = jnp.concatenate([jnp.zeros_like(y[:, :1]), y[:, :-1]], axis=1)
        y_fw, y_bw = (y[:b], jnp.flip(y[b:], 1))
        fd = x_og @ fc_D_w.T + D
        y = y_fw + y_bw + x_og * jnp.repeat(fd, HEADDIM, axis=-1)
        yg = y * silu(z)
        yn = yg * jax.lax.rsqrt(jnp.mean(yg * yg, axis=-1, keepdims=True) + EPS) * norm_w
        return yn @ out_proj_w.T

    def _L0_ffn_ref(x, Wr, br, W1, b1, W2, b2):
        import jax, jax.numpy as jnp
        import numpy as np
        H, E, DFF = (256, 8, 1024)
        B, S, Hd = x.shape
        n_exp = W1.shape[0]
        xt = x.reshape(-1, Hd)
        logits = xt @ Wr + br
        probs = jax.nn.softmax(logits, axis=-1)
        gate = jnp.max(probs, axis=-1)
        idx = jnp.argmax(probs, axis=-1)
        h1 = jnp.maximum(jnp.einsum('th,ehf->etf', xt, W1) + b1[:, None, :], 0.0)
        ye = jnp.einsum('etf,efh->eth', h1, W2) + b2[:, None, :]
        onehot = jax.nn.one_hot(idx, n_exp, dtype=xt.dtype)
        y = jnp.einsum('te,eth->th', onehot, ye) * gate[:, None]
        return y.reshape(B, S, Hd)

    def _L1_attn_ref(x, Wq, Wk, Wv, Wo, W_down_kv, W_up_k, W_up_v):
        import jax, jax.numpy as jnp
        import numpy as np
        D_MODEL = 256
        N_HEADS = 16
        HEAD_DIM = D_MODEL // N_HEADS
        D_LATENT = 64
        LAMBDA_DECAY = 0.01
        TIME_STEP = 0.01
        CLAMP = 10000.0

        def _reference_tuple_inner(x, Wq, Wk, Wv, Wo, W_down_kv, W_up_k, W_up_v):
            B, S, _ = x.shape
            q = x @ Wq
            k = x @ Wk
            v = x @ Wv
            latent_kv = (k + v) @ W_down_kv
            k_rec = latent_kv @ W_up_k
            v_rec = latent_kv @ W_up_v

            def heads(t):
                return t.reshape(B, S, N_HEADS, HEAD_DIM).transpose(0, 2, 1, 3)
            qh, kh, vh = (heads(q), heads(k_rec), heads(v_rec))
            scale = 1.0 / (jnp.sqrt(jnp.float32(D_MODEL)) + 1e-08)
            scores = jnp.einsum('bhqd,bhkd->bhqk', qh, kh) * scale
            scores = jnp.clip(jnp.nan_to_num(scores, nan=-1000000000.0), -CLAMP, CLAMP)
            idx = jnp.arange(S, dtype=jnp.float32)
            decay = jnp.exp(-LAMBDA_DECAY * TIME_STEP * jnp.abs(idx[:, None] - idx[None, :]))
            scores = scores * decay[None, None, :, :]
            scores = jnp.clip(jnp.nan_to_num(scores, nan=-1000000000.0), -CLAMP, CLAMP)
            attn = jax.nn.softmax(scores, axis=-1)
            out = jnp.einsum('bhqk,bhkd->bhqd', attn, vh)
            out = out.transpose(0, 2, 1, 3).reshape(B, S, D_MODEL)
            return (out @ Wo, latent_kv)
        return _reference_tuple_inner(x, Wq, Wk, Wv, Wo, W_down_kv, W_up_k, W_up_v)[0]

    def _L1_ffn_ref(x, router_w, router_b, experts_inter, experts_out):
        import math
        import jax, jax.numpy as jnp
        import numpy as np
        NUM_EXPERTS = 8
        TOP_K = 2
        CAPACITY_FACTOR = 1.0
        B, S, H, I = (4, 512, 256, 1024)
        batch, seq, hidden = x.shape
        n_exp = router_w.shape[0]
        n_tok = batch * seq
        cap = math.ceil(n_tok / n_exp * CAPACITY_FACTOR)
        logits = jnp.einsum('bsh,eh->bse', x, router_w) + router_b
        weights_flat = jax.nn.softmax(logits, axis=-1).reshape(n_tok, n_exp)
        x_flat = x.reshape(n_tok, hidden)
        topk_vals, topk_idx = jax.lax.top_k(weights_flat, TOP_K)
        rows = jnp.arange(n_tok)[:, None]
        topk_flat = jnp.zeros_like(weights_flat).at[rows, topk_idx].set(topk_vals)
        routing_mask = (topk_flat > 0).astype(jnp.int32)
        noop_w = topk_flat[:, -1]
        noop_mask = routing_mask[:, -1].astype(x.dtype)
        expert_w = topk_flat[:, :-1]
        expert_mask = routing_mask[:, :-1]
        sorted_indices = jnp.argsort(-expert_mask, axis=0)[:cap]
        sorted_mask = jnp.take_along_axis(expert_mask, sorted_indices, axis=0)
        used_idx = (sorted_indices * sorted_mask).reshape(-1)
        inputs = x_flat[used_idx] * sorted_mask.reshape(-1).astype(x.dtype)[:, None]
        inputs = inputs.reshape(cap, n_exp - 1, hidden)
        in_w = jnp.take_along_axis(expert_w, sorted_indices, axis=0)
        h = jax.nn.relu(jnp.einsum('ceh,ehi->cei', inputs, experts_inter))
        out = jnp.einsum('cei,eih->ceh', h, experts_out) * in_w[..., None]
        combined = jnp.zeros_like(x_flat).at[used_idx].add(out.reshape(-1, hidden))
        combined = combined + x_flat * (noop_w * noop_mask)[:, None]
        return combined.reshape(batch, seq, hidden)
    x = L0_attn_u
    xn = _layernorm(x, axis=-1)
    x = x + _L0_attn_ref(xn, L0_attn_in_proj_w, L0_attn_conv_w, L0_attn_conv_b, L0_attn_dt_bias, L0_attn_A_log, L0_attn_D, L0_attn_fc_D_w, L0_attn_norm_w, L0_attn_out_proj_w) + _L0_ffn_ref(xn, L0_ffn_Wr, L0_ffn_br, L0_ffn_W1, L0_ffn_b1, L0_ffn_W2, L0_ffn_b2)
    xn = _layernorm(x, axis=-1)
    x = x + _L1_attn_ref(xn, L1_attn_Wq, L1_attn_Wk, L1_attn_Wv, L1_attn_Wo, L1_attn_W_down_kv, L1_attn_W_up_k, L1_attn_W_up_v) + _L1_ffn_ref(xn, L1_ffn_router_w, L1_ffn_router_b, L1_ffn_experts_inter, L1_ffn_experts_out)
    return x

_drawn_inputs = setup_inputs


def setup_inputs(seed=0):
    import zlib

    import numpy as np

    out = dict(_drawn_inputs(seed))
    spreads = {'L0_attn_conv_b': (0.0, 0.1),
     'L0_attn_D': (1.0, 0.2),
     'L0_attn_norm_w': (1.0, 0.2),
     'L0_ffn_br': (0.0, 0.1),
     'L0_ffn_b1': (0.0, 0.1),
     'L0_ffn_b2': (0.0, 0.1),
     'L1_ffn_router_b': (0.0, 0.8)}
    factors = {'L0_attn_dt_bias': 34.112,
     'L0_attn_A_log': 29.728,
     'L1_attn_Wq': 8.0,
     'L1_attn_Wk': 8.0,
     'L1_attn_Wv': 8.0,
     'L1_attn_Wo': 8.0,
     'L1_attn_W_down_kv': 8.0,
     'L1_attn_W_up_k': 8.0,
     'L1_attn_W_up_v': 8.0,
     'L1_ffn_router_w': 5.301,
     'L1_ffn_experts_inter': 7.176,
     'L1_ffn_experts_out': 5.936}
    for name, (base, spread) in spreads.items():
        noise = np.random.default_rng([zlib.crc32(name.encode()), seed]).standard_normal(out[name].shape)
        drawn = base * np.exp(spread * noise) if base else spread * noise
        out[name] = jnp.asarray(drawn.astype(out[name].dtype))
    for name, factor in factors.items():
        out[name] = (out[name] * factor).astype(out[name].dtype)
    return out
```

```python
from contextlib import ExitStack

import concourse.bass as bass
from concourse import mybir

F32 = mybir.dt.float32
I32 = mybir.dt.int32
BF16 = mybir.dt.bfloat16
ALU = mybir.AluOpType
ACT = mybir.ActivationFunctionType
AX_X = mybir.AxisListType.X

P = 128
D = 256
KD = D // P
BATCH, SEQ = 8, 512
TOK = BATCH * SEQ
NT = TOK // P
CPB = SEQ // P
EPS = 1e-5
LEAST_NORMAL = 2.0 ** -126

NE = 8
DFF = 1024
FT = DFF // P

DI = 512
DS = 128
NH = 8
HD = DI // NH
CONV = DI + 4 * DS
CT = CONV // P
TAPS = 4

L0_TILES = (TOK + NE * (P - 1)) // P

L0_ROWS = L0_TILES * P
L1_EXPERTS = NE - 1
CAP = TOK // NE
L1_ROWS = L1_EXPERTS * CAP

AH = 16
HW = D // AH
LAT = 64
CLAMP = 10000.0
DECAY = 0.01 * 0.01


class Space:

    def __init__(self, nc, name):
        self.nc, self.name = nc, name
        self.mem = ExitStack()
        self.sems = []

    def __enter__(self):
        return self

    def __exit__(self, failed, *a):
        self.mem.close()
        if failed is None:
            self.nc.clear_and_free_semaphores(self.sems)
            self.nc.all_engine_barrier()
        return False

    def sb(self, name, shape, dt=F32):
        return self.mem.enter_context(self.nc.sbuf_tensor(f"{self.name}_{name}", shape, dt))

    def psum(self, name, shape, dt=F32):
        return self.mem.enter_context(self.nc.psum_tensor(f"{self.name}_{name}", shape, dt))

    def sem(self, name):
        self.sems.append(self.nc.alloc_semaphore(name=f"{self.name}_{name}"))
        return self.sems[-1]


class Chain:

    def __init__(self, eng, sem, turn=0, per_turn=0, start=0):
        self.eng, self.sem, self.base, self.n, self.per_turn = eng, sem, turn * per_turn + start, 0, per_turn

    def link(self, ins):
        self.n += 1
        ins.then_inc(self.sem, 1)

    def wait(self):
        self.eng.wait_ge(self.sem, self.base + self.n)

    def step(self, ins):
        self.link(ins)
        self.wait()

    def end(self):
        assert self.n == self.per_turn, self.n


class Constants:
    pass


class Choice:
    pass


def constants(nc, kept, C):
    C.ident = kept.enter_context(nc.sbuf_tensor("ident", [P, P], F32))
    C.before = kept.enter_context(nc.sbuf_tensor("before", [P, P], F32))
    C.after = kept.enter_context(nc.sbuf_tensor("after", [P, P], F32))
    C.ones = kept.enter_context(nc.sbuf_tensor("ones", [P, P], F32))
    C.half = kept.enter_context(nc.sbuf_tensor("minus_half", [P, NT], F32))
    with Space(nc, "const") as s, nc.Block() as block:
        filled = s.sem("filled")

        @block.gpsimd
        def _(pool):
            nc.gpsimd.memset(C.ident[:], 0.0).then_inc(filled, 1)
            nc.gpsimd.memset(C.before[:], 1.0).then_inc(filled, 1)
            nc.gpsimd.memset(C.after[:], 1.0).then_inc(filled, 1)
            nc.gpsimd.memset(C.ones[:], 1.0)
            nc.gpsimd.memset(C.half[:], -0.5)
            pool.wait_ge(filled, 3)
            nc.gpsimd.affine_select(out=C.ident[:], in_=C.ident[:], compare_op=ALU.not_equal, fill=1.0,
                                    base=0, pattern=[[-1, P]], channel_multiplier=1)
            nc.gpsimd.affine_select(out=C.before[:], in_=C.before[:], compare_op=ALU.is_gt, fill=0.0,
                                    base=0, pattern=[[1, P]], channel_multiplier=-1)
            nc.gpsimd.affine_select(out=C.after[:], in_=C.after[:], compare_op=ALU.is_gt, fill=0.0,
                                    base=0, pattern=[[-1, P]], channel_multiplier=1)


def normalise(nc, C, name, x_d, w_d, width, logits, xn_all, xT_d, merge=None):
    G = 2
    TURNS = BATCH // G
    with Space(nc, name) as s:
        x = s.sb("x", [P, G, CPB, D])
        xn = s.sb("xn", [P, G, CPB, D])
        xT = s.sb("xT", [P, G, KD, SEQ])
        w = s.sb("w", [P, KD, width])
        stats = s.sb("stats", [P, G, CPB, 6])
        mean = s.sb("mean", [P, G, CPB])
        diff = s.sb("diff", [P, G, CPB])
        spread = s.sb("spread", [P, G, CPB])
        var = s.sb("var", [P, G, CPB])
        rstd = s.sb("rstd", [P, G, CPB])
        psT = [s.psum(f"psT{g}{k}", [P, SEQ]) for g in range(G) for k in range(KD)]
        psL = [s.psum(f"psL{g}", [P, CPB, width]) for g in range(G)]
        w_in = s.sem("w_in")
        x_in = [s.sem(f"x_in{g}") for g in range(G)]
        x_out = [s.sem(f"x_out{g}") for g in range(G)]
        merged = s.sem("merged")
        chain = s.sem("chain")
        var_ready = s.sem("var_ready")
        rstd_ready = s.sem("rstd_ready")
        xn_ready = s.sem("xn_ready")
        xn_kept = [s.sem(f"xn_kept{g}") for g in range(G)]
        turned = s.sem("turned")
        xT_ready = s.sem("xT_ready")
        xT_kept = [s.sem(f"xT_kept{g}") for g in range(G)]
        logits_ready = s.sem("logits_ready")
        logits_kept = s.sem("logits_kept")

        def rows(dram, i, g):
            return dram[bass.ds((i * G + g) * SEQ, SEQ), :].rearrange("(c p) d -> p c d", p=P)

        with nc.Block() as block:
            @block.sync
            def _(sp):
                sp.dma_start(w[:], w_d.rearrange("(k p) n -> p k n", p=P)).then_inc(w_in, 16)
                for i in range(TURNS):
                    for g in range(G):
                        if i:
                            sp.wait_ge(xn_ready, ((i - 1) * G + g + 1) * CPB)
                        if i and merge:
                            sp.wait_ge(x_out[g], i * 16)
                        sp.dma_start(x[:, g], rows(x_d, i, g)).then_inc(x_in[g], 16)
                    for g in range(G):
                        if merge:
                            sp.wait_ge(merged, (i * G + g + 1) * CPB)
                            sp.dma_start(rows(merge[2], i, g), x[:, g]).then_inc(x_out[g], 16)
                        sp.wait_ge(xn_ready, (i * G + g + 1) * CPB)
                        sp.dma_start(xn_all[:, bass.ds((i * G + g) * CPB, CPB), :], xn[:, g]).then_inc(xn_kept[g], 16)
                        sp.wait_ge(xT_ready, (i * G + g + 1) * KD)
                        sp.dma_start(xT_d[:, bass.ds((i * G + g) * SEQ, SEQ)].rearrange("(k p) t -> p k t", p=P),
                                     xT[:, g]).then_inc(xT_kept[g], 16)
                for g in range(G):
                    if merge:
                        sp.wait_ge(x_out[g], TURNS * 16)
                    sp.wait_ge(xn_kept[g], TURNS * 16)
                    sp.wait_ge(xT_kept[g], TURNS * 16)

            @block.vector
            def _(dve):
                n_links = CPB + 5
                with dve.Fori(0, TURNS) as i:
                    c = Chain(dve, chain, i, G * n_links)
                    for g in range(G):
                        dve.wait_ge(x_in[g], (i + 1) * 16)
                        if merge:
                            for t in range(CPB):
                                at = (i * G + g) * CPB + t
                                nc.vector.scalar_tensor_tensor(
                                    out=x[:, g, t], in0=merge[0][:, bass.ds(at, 1), :].rearrange("p a d -> p (a d)"),
                                    scalar=merge[1][:, bass.ds(at, 1)], in1=x[:, g, t],
                                    op0=ALU.mult, op1=ALU.add).then_inc(merged, 1)
                            dve.wait_ge(merged, (i * G + g + 1) * CPB)
                        for t in range(CPB):
                            c.link(nc.vector.bn_stats(stats[:, g, t], x[:, g, t]))
                        c.wait()
                        even, odd = stats[:, g, :, 1], stats[:, g, :, 4]
                        c.link(nc.vector.tensor_tensor(mean[:, g], even, odd, ALU.add))
                        c.link(nc.vector.tensor_tensor(diff[:, g], even, odd, ALU.subtract))
                        c.link(nc.vector.scalar_tensor_tensor(
                            out=spread[:, g], in0=stats[:, g, :, 2], scalar=D * EPS, in1=stats[:, g, :, 5],
                            op0=ALU.add, op1=ALU.add))
                        c.wait()
                        c.link(nc.vector.tensor_scalar(mean[:, g], mean[:, g], 0.5, None, ALU.mult))
                        c.link(nc.vector.scalar_tensor_tensor(
                            out=diff[:, g], in0=diff[:, g], scalar=0.25, in1=diff[:, g], op0=ALU.mult, op1=ALU.mult))
                        c.wait()
                        nc.vector.scalar_tensor_tensor(
                            out=var[:, g], in0=spread[:, g], scalar=1.0 / D, in1=diff[:, g],
                            op0=ALU.mult, op1=ALU.add).then_inc(var_ready, 1)
                        dve.wait_ge(rstd_ready, i * G + g + 1)
                        dve.wait_ge(xn_kept[g], i * 16)
                        dve.wait_ge(turned, i * G * KD)
                        for t in range(CPB):
                            nc.vector.tensor_scalar(xn[:, g, t], x[:, g, t], mean[:, g, t:t + 1], rstd[:, g, t:t + 1],
                                                    ALU.subtract, ALU.mult).then_inc(xn_ready, 1)
                    for g in range(G):
                        dve.wait_ge(logits_ready, i * G + g + 1)
                        nc.vector.tensor_copy(logits[:, bass.ds((i * G + g) * CPB, CPB), :], psL[g][:]).then_inc(logits_kept, 1)
                    c.end()
                dve.wait_ge(logits_kept, BATCH)

            @block.gpsimd
            def _(pool):
                with pool.Fori(0, TURNS) as i:
                    for g in range(G):
                        pool.wait_ge(xn_ready, i * G * CPB)
                        pool.wait_ge(var_ready, i * G + g + 1)
                        nc.gpsimd.tensor_tensor(rstd[:, g], var[:, g], C.half[:, 0:CPB], ALU.pow).then_inc(rstd_ready, 1)

            @block.tensor
            def _(pe):
                pe.wait_ge(w_in, 16)
                with pe.Fori(0, TURNS) as i:
                    for g in range(G):
                        pe.wait_ge(xn_ready, (i * G + g + 1) * CPB)
                        pe.wait_ge(xT_ready, i * G * KD)
                        for k in range(KD):
                            for t in range(CPB):
                                mm = nc.tensor.transpose(psT[g * KD + k][:, t * P:(t + 1) * P],
                                                         xn[:, g, t, k * P:(k + 1) * P], C.ident[:])
                            mm.then_inc(turned, 1)
                    for g in range(G):
                        pe.wait_ge(xT_ready, (i * G + g + 1) * KD)
                        pe.wait_ge(logits_kept, i * G)
                        for t in range(CPB):
                            for k in range(KD):
                                mm = nc.tensor.matmul(psL[g][:, t], xT[:, g, k, t * P:(t + 1) * P], w[:, k],
                                                      start=(k == 0), stop=(k == KD - 1))
                        mm.then_inc(logits_ready, 1)

            @block.scalar
            def _(act):
                with act.Fori(0, TURNS) as i:
                    for g in range(G):
                        act.wait_ge(xT_kept[g], i * 16)
                        act.wait_ge(logits_ready, i * G)
                        for k in range(KD):
                            act.wait_ge(turned, (i * G + g) * KD + k + 1)
                            nc.scalar.copy(xT[:, g, k], psT[g * KD + k][:]).then_inc(xT_ready, 1)


def route(nc, C, name, logits, bias_bc, xn_all, xs_d, first_layer, out):
    rows = L0_ROWS if first_layer else L1_ROWS
    picks = 1 if first_layer else 2
    per_p = rows // P * D
    ZW = per_p // 4
    with Space(nc, name) as s:
        zeros = s.sb("zeros", [P, ZW])
        lb = s.sb("lb", [P, NT, NE])
        red = s.sb("red", [P, NT])
        total = s.sb("total", [P, NT])
        prob = s.sb("prob", [P, NT, NE])
        weight_i = s.sb("order_i", [P, NE], I32)
        order = s.sb("order", [P, NE])
        rowbase_i = s.sb("rowbase_i", [P, NE], I32)
        rowbase = s.sb("rowbase", [P, NE])
        tile_i = s.sb("tile_i", [P, L0_TILES], I32)
        tiles = s.sb("tiles", [P, L0_TILES])
        tmp = s.sb("tmp", [P, NT, NE])
        tmp2 = s.sb("tmp2", [P, NT, NE])
        hot = [s.sb(f"hot{k}", [P, NT, NE]) for k in range(picks)]
        mask = s.sb("mask", [P, NT, NE])
        best = [s.sb(f"best{k}", [P, NT]) for k in range(picks)]
        some = s.sb("some", [P, NT])
        rank = s.sb("rank", [P, NT, NE])
        per_tile = s.sb("per_tile", [P, NT, NE])
        upto = s.sb("upto", [P, NT, NE])
        over = s.sb("over", [P, NE, NT])
        n_tiles = s.sb("n_tiles", [P, NE])
        end_tile = s.sb("end_tile", [P, NE])
        start_row = s.sb("start_row", [P, NE])
        by_tile = s.sb("by_tile", [P, L0_TILES, NE])
        tile_expert = s.sb("tile_expert", [P, L0_TILES])
        slot = s.sb("slot", [P, NT])
        ps_rank = s.psum("ps_rank", [P, NT, NE])
        ps_tile = s.psum("ps_tile", [P, NT, NE])
        bias_in = s.sem("bias_in")
        bias = s.sb("bias", [P, NE])
        zeroed = s.sem("zeroed")
        filled = [s.sem(f"filled{q}") for q in range(4)]
        counted = s.sem("counted")
        shifted = s.sem("shifted")
        exped = s.sem("exped")
        chosen = s.sem("chosen")
        ranked = s.sem("ranked")
        chain = s.sem("chain")
        placed = s.sem("placed")
        scattered = s.sem("scattered")
        xs_flat = xs_d.rearrange("(p r) d -> p (r d)", p=P)

        with nc.Block() as block:
            @block.sync
            def _(sp):
                sp.dma_start(bias[:], bias_bc).then_inc(bias_in, 16)
                sp.wait_ge(zeroed, 1)
                for q in range(4):
                    sp.dma_start(xs_flat[:, q * ZW:(q + 1) * ZW], zeros[:]).then_inc(filled[q], 16)

            @block.gpsimd
            def _(pool):
                nc.gpsimd.memset(zeros[:], 0.0).then_inc(zeroed, 1)
                nc.gpsimd.iota(weight_i[:], pattern=[[-1, NE]], base=NE, channel_multiplier=0).then_inc(counted, 1)
                nc.gpsimd.iota(rowbase_i[:], pattern=[[CAP, NE]], base=-L1_ROWS, channel_multiplier=0).then_inc(counted, 1)
                nc.gpsimd.iota(tile_i[:], pattern=[[1, L0_TILES]], base=0, channel_multiplier=0).then_inc(counted, 1)
                for q in range(4):
                    pool.wait_ge(filled[q], 16)
                for t in range(NT):
                    for k in range(picks):
                        if t == 0:
                            pool.wait_ge(placed, k + 1)
                        nc.gpsimd.indirect_dma_start(
                            out=xs_d, out_offset=bass.IndirectOffsetOnAxis(ap=out.slot[k][:, t:t + 1], axis=0),
                            in_=xn_all[:, t, :], in_offset=None,
                            bounds_check=rows - 1, oob_is_err=first_layer).then_inc(scattered, 16)
                pool.wait_ge(scattered, NT * picks * 16)

            @block.scalar
            def _(act):
                act.wait_ge(shifted, 1)
                nc.scalar.activation(prob[:], lb[:], ACT.Exp).then_inc(exped, 1)

            @block.tensor
            def _(pe):
                pe.wait_ge(chosen, 1)
                nc.tensor.matmul(ps_rank[:], C.before[:], mask[:], start=True, stop=True)
                nc.tensor.matmul(ps_tile[:], C.ones[:], mask[:], start=True, stop=True).then_inc(ranked, 1)

            @block.vector
            def _(dve):
                c = Chain(dve, chain)
                v = nc.vector

                def wide(ap):
                    return ap.unsqueeze(2).to_broadcast([P, NT, NE])

                def per_expert(ap):
                    return ap.unsqueeze(1).to_broadcast([P, NT, NE])

                dve.wait_ge(bias_in, 16)
                dve.wait_ge(counted, 3)
                c.step(v.tensor_copy(order[:], weight_i[:]))
                c.step(v.tensor_copy(rowbase[:], rowbase_i[:]))
                c.step(v.tensor_copy(tiles[:], tile_i[:]))
                c.step(v.tensor_tensor(lb[:], logits[:, :, 0:NE], per_expert(bias[:]), ALU.add))
                c.step(v.tensor_reduce(red[:], lb[:], AX_X, ALU.max))
                v.tensor_tensor(lb[:], lb[:], wide(red[:]), ALU.subtract).then_inc(shifted, 1)
                dve.wait_ge(exped, 1)
                c.step(v.tensor_reduce(total[:], prob[:], AX_X, ALU.add))
                c.step(v.reciprocal(total[:], total[:]))
                c.step(v.tensor_tensor(prob[:], prob[:], wide(total[:]), ALU.mult))
                for k in range(picks):
                    c.step(v.tensor_reduce(best[k][:], prob[:], AX_X, ALU.max))
                    c.step(v.tensor_tensor(tmp[:], prob[:], wide(best[k][:]), ALU.is_equal))
                    c.step(v.tensor_tensor(tmp[:], tmp[:], per_expert(order[:]), ALU.mult))
                    c.step(v.tensor_reduce(red[:], tmp[:], AX_X, ALU.max))
                    c.step(v.tensor_tensor(hot[k][:], tmp[:], wide(red[:]), ALU.is_equal))
                    if k + 1 < picks:
                        c.step(v.scalar_tensor_tensor(out=prob[:], in0=hot[k][:], scalar=-2.0, in1=prob[:],
                                                      op0=ALU.mult, op1=ALU.add))
                if first_layer:
                    v.tensor_copy(mask[:], hot[0][:]).then_inc(chosen, 1)
                    c.step(v.tensor_copy(out.gate[:], best[0][:]))
                else:
                    for k in range(picks):
                        c.step(v.tensor_scalar(some[:], best[k][:], LEAST_NORMAL, None, ALU.is_ge))
                        c.step(v.tensor_tensor(hot[k][:], hot[k][:], wide(some[:]), ALU.mult))
                    v.tensor_tensor(mask[:], hot[0][:], hot[1][:], ALU.add).then_inc(chosen, 1)
                dve.wait_ge(ranked, 1)
                c.step(v.tensor_copy(per_tile[:], ps_tile[:]))
                for e in range(NE):
                    c.link(v.tensor_tensor_scan(upto[:, :, e], C.ones[:, 0:NT], per_tile[:, :, e], 0.0, ALU.mult, ALU.add))
                c.wait()
                c.step(v.tensor_tensor(tmp[:], upto[:], per_tile[:], ALU.subtract))
                c.step(v.tensor_tensor(rank[:], ps_rank[:], tmp[:], ALU.add))
                if first_layer:
                    c.step(v.tensor_scalar(per_tile[:, :, 0], tiles[:, 0:NT], float(P), None, ALU.mult))
                    c.step(v.tensor_tensor(over[:], upto[:, NT - 1, :].unsqueeze(2).to_broadcast([P, NE, NT]),
                                           per_tile[:, :, 0].unsqueeze(1).to_broadcast([P, NE, NT]), ALU.is_gt))
                    c.step(v.tensor_reduce(n_tiles[:], over[:], AX_X, ALU.add))
                    c.step(v.tensor_tensor_scan(end_tile[:], C.ones[:, 0:NE], n_tiles[:], 0.0, ALU.mult, ALU.add))
                    c.step(v.tensor_tensor(start_row[:], end_tile[:], n_tiles[:], ALU.subtract))
                    c.step(v.tensor_scalar(start_row[:], start_row[:], float(P), None, ALU.mult))
                    c.step(v.tensor_tensor(rank[:], rank[:], per_expert(start_row[:]), ALU.add))
                    c.step(v.tensor_tensor(by_tile[:], tiles[:].unsqueeze(2).to_broadcast([P, L0_TILES, NE]),
                                           end_tile[:].unsqueeze(1).to_broadcast([P, L0_TILES, NE]), ALU.is_ge))
                    c.step(v.tensor_reduce(tile_expert[:], by_tile[:], AX_X, ALU.add))
                    c.step(v.tensor_scalar(tile_expert[:], tile_expert[:], float(NE - 1), None, ALU.min))
                    c.step(v.tensor_copy(out.tile_expert[:], tile_expert[:]))
                    c.step(v.tensor_tensor(tmp[:], hot[0][:], rank[:], ALU.mult))
                    c.step(v.tensor_reduce(slot[:], tmp[:], AX_X, ALU.add))
                    v.tensor_copy(out.slot[0][:], slot[:]).then_inc(placed, 1)
                else:
                    c.step(v.tensor_tensor(tmp2[:, :, 0], hot[0][:, :, NE - 1], best[0][:], ALU.mult))
                    c.step(v.tensor_tensor(tmp2[:, :, 1], hot[1][:, :, NE - 1], best[1][:], ALU.mult))
                    c.step(v.tensor_tensor(out.passed[:], tmp2[:, :, 0], tmp2[:, :, 1], ALU.add))
                    c.step(v.tensor_scalar(mask[:], rank[:], float(CAP), None, ALU.is_lt))
                    c.step(v.memset(mask[:, :, NE - 1], 0.0))
                    c.step(v.tensor_tensor(rank[:], rank[:], per_expert(rowbase[:]), ALU.add))
                    for k in range(picks):
                        c.step(v.tensor_tensor(hot[k][:], hot[k][:], mask[:], ALU.mult))
                        c.step(v.tensor_reduce(some[:], hot[k][:], AX_X, ALU.add))
                        c.step(v.tensor_tensor(out.weight[k][:], some[:], best[k][:], ALU.mult))
                        c.step(v.tensor_tensor(tmp[:], hot[k][:], rank[:], ALU.mult))
                        c.step(v.tensor_reduce(slot[:], tmp[:], AX_X, ALU.add))
                        c.step(v.tensor_scalar(slot[:], slot[:], float(L1_ROWS), None, ALU.add))
                        v.tensor_copy(out.slot[k][:], slot[:]).then_inc(placed, 1)
                        dve.wait_ge(placed, k + 1)


def time_steps(nc, C, logits, dt_bias_bc, a_log_bc, dt, a):
    N2 = 2 * NH
    with Space(nc, "steps") as s:
        bias = s.sb("bias", [P, N2])
        neg_a = s.sb("neg_a", [P, N2])
        raw = s.sb("raw", [P, NT, N2])
        mag = s.sb("mag", [P, NT, N2])
        u = s.sb("u", [P, NT, N2])
        w = s.sb("w", [P, NT, N2])
        d = s.sb("d", [P, NT, N2])
        flat = s.sb("flat", [P, NT, N2])
        lw = s.sb("lw", [P, NT, N2])
        loaded = s.sem("loaded")
        mag_ready = s.sem("mag_ready")
        exped = s.sem("exped")
        w_ready = s.sem("w_ready")
        logged = s.sem("logged")
        chain = s.sem("chain")
        with nc.Block() as block:
            @block.sync
            def _(sp):
                sp.dma_start(bias[:], dt_bias_bc).then_inc(loaded, 16)
                sp.dma_start(neg_a[:], a_log_bc).then_inc(loaded, 16)

            @block.scalar
            def _(act):
                act.wait_ge(loaded, 32)
                nc.scalar.activation(neg_a[:], neg_a[:], ACT.Exp).then_inc(exped, 1)
                act.wait_ge(mag_ready, 1)
                nc.scalar.activation(u[:], mag[:], ACT.Exp, scale=-1.0).then_inc(exped, 1)
                act.wait_ge(w_ready, 1)
                nc.scalar.activation(lw[:], w[:], ACT.Ln).then_inc(logged, 1)

            @block.vector
            def _(dve):
                c = Chain(dve, chain)
                v = nc.vector
                dve.wait_ge(loaded, 32)
                c.step(v.tensor_tensor(raw[:], logits[:, :, NE:NE + N2],
                                       bias[:].unsqueeze(1).to_broadcast([P, NT, N2]), ALU.add))
                v.scalar_tensor_tensor(out=mag[:], in0=raw[:], scalar=-1.0, in1=raw[:],
                                       op0=ALU.mult, op1=ALU.max).then_inc(mag_ready, 1)
                dve.wait_ge(exped, 2)
                v.tensor_scalar(w[:], u[:], 1.0, None, ALU.add).then_inc(w_ready, 1)
                dve.wait_ge(w_ready, 1)
                c.step(v.tensor_scalar(d[:], w[:], -1.0, None, ALU.add))
                c.step(v.tensor_scalar(flat[:], d[:], 0.0, None, ALU.is_equal))
                c.step(v.tensor_tensor(d[:], d[:], flat[:], ALU.add))
                c.step(v.reciprocal(d[:], d[:]))
                c.step(v.tensor_tensor(d[:], d[:], u[:], ALU.mult))
                dve.wait_ge(logged, 1)
                c.step(v.tensor_tensor(d[:], d[:], lw[:], ALU.mult))
                c.step(v.tensor_tensor(flat[:], flat[:], u[:], ALU.mult))
                c.step(v.tensor_tensor(d[:], d[:], flat[:], ALU.add))
                c.step(v.scalar_tensor_tensor(out=dt[:], in0=raw[:], scalar=0.0, in1=d[:], op0=ALU.max, op1=ALU.add))
                c.step(v.scalar_tensor_tensor(out=a[:], in0=dt[:], scalar=-1.0,
                                              in1=neg_a[:].unsqueeze(1).to_broadcast([P, NT, N2]),
                                              op0=ALU.mult, op1=ALU.mult))


def mamba(nc, C, xT_d, x_d, w, dt, a, out_d):
    CONV_AT, Z_AT = 0, CT
    BT_AT = Z_AT + CPB
    XT_AT = BT_AT + 2
    TAIL_AT = XT_AT + CPB
    USES = TAIL_AT + 2 * CPB
    ORDER = [4, 5, 6, 7, 0, 1, 2, 3]
    XW = SEQ + 2
    U = 2 * CPB

    with Space(nc, "mamba") as s:
        w_in = s.sb("w_in", [P, KD, DI + CONV])
        w_out = s.sb("w_out", [P, DI // P, D])
        norm_w = s.sb("norm_w", [P, DI // P])
        w_fcd = s.sb("w_fcd", [P, DI // P, NH])
        taps = s.sb("taps", [P, CT, TAPS])
        conv_b = s.sb("conv_b", [P, CT])
        d_bc = s.sb("d_bc", [P, NH])
        d_col = s.sb("d_col", [P, DI // P])
        d_diag = s.sb("d_diag", [P, DI // P, P])
        xT = s.sb("xT", [P, KD, SEQ])
        acc = s.sb("acc", [P, 4, SEQ])
        xc = s.sb("xc", [P, CT, XW])
        near = s.sb("near", [P, DI // P, SEQ])
        zs = s.sb("zs", [P, CPB, DI])
        Bl = s.sb("Bl", [P, 2, CPB, DS])
        xl = s.sb("xl", [P, CPB, DI])
        ab = s.sb("ab", [P, 2, CPB, NH])
        dtb = s.sb("dtb", [P, 2, CPB, NH])
        fac = s.sb("fac", [P, 3, 2, CPB, NH])
        dtdec = s.sb("dtdec", [P, 2, CPB, NH])
        fd = s.sb("fd", [P, CPB, NH])
        xdd = s.sb("xdd", [P, 2, DI])
        state = s.sb("state", [P, 2, CPB, DI])
        scaled = s.sb("scaled", [P, 2, DI])
        am = s.sb("am", [P, 2, NH, P])
        L = s.sb("L", [P, 2, NH, P])
        Gm = s.sb("Gm", [P, 2, P])
        xdt = s.sb("xdt", [P, 2, DI])
        xfd = s.sb("xfd", [P, DI])
        yo = s.sb("yo", [P, 2, DI])
        y = s.sb("y", [P, 2, DI])
        sq = s.sb("sq", [P, DI])
        ssum = s.sb("ssum", [P, CPB])
        var = s.sb("var", [P, CPB])
        rstd = s.sb("rstd", [P, CPB])
        yT = s.sb("yT", [P, 2, DI // P, P])
        x = s.sb("x", [P, CPB, D])
        o = s.sb("o", [P, CPB, D])
        psA = [s.psum(f"psA{j}", [P, 512]) for j in range(2)]
        psS = [s.psum(f"psS{j}", [P, 4, P]) for j in range(2)]
        psG = s.psum("psG", [P, 512])
        psY = s.psum("psY", [P, DI])
        psO = [s.psum(f"psO{d}", [P, DI]) for d in range(2)]
        gT = psG[:, 0:2 * P].rearrange("p (d t) -> p d t", d=2)
        sums = psG[:, 256:448]
        fd_ps = psG[:, 448:480].rearrange("p (c h) -> p c h", c=CPB)
        tri = [C.before, C.after]

        weights_in = s.sem("weights_in")
        xT_in = s.sem("xT_in")
        x_in = s.sem("x_in")
        out_stored = s.sem("out_stored")
        padded = s.sem("padded")
        diag_ready = s.sem("diag_ready")
        wout_ready = s.sem("wout_ready")
        bank_ready = s.sem("bank_ready")
        tap0 = s.sem("tap0")
        conv_done = s.sem("conv_done")
        xc_ready = s.sem("xc_ready")
        z_ready = s.sem("z_ready")
        tok_ready = s.sem("tok_ready")
        ab_ready = s.sem("ab_ready")
        sums_ready = s.sem("sums_ready")
        fac_ready = s.sem("fac_ready")
        dtdec_ready = s.sem("dtdec_ready")
        fd_done = s.sem("fd_done")
        fd_ready = s.sem("fd_ready")
        near_ready = s.sem("near_ready")
        xdd_ready = s.sem("xdd_ready")
        grown = s.sem("grown")
        state_ready = s.sem("state_ready")
        am_ready = s.sem("am_ready")
        seg_ready = s.sem("seg_ready")
        seg_exped = s.sem("seg_exped")
        g_ready = s.sem("g_ready")
        gm_ready = s.sem("gm_ready")
        L_ready = s.sem("L_ready")
        xdt_ready = s.sem("xdt_ready")
        diag_used = s.sem("diag_used")
        off_ready = s.sem("off_ready")
        off_scaled = s.sem("off_scaled")
        xfd_ready = s.sem("xfd_ready")
        y_read = s.sem("y_read")
        summed = s.sem("summed")
        gated = s.sem("gated")
        squared = s.sem("squared")
        var_ready = s.sem("var_ready")
        rstd_ready = s.sem("rstd_ready")
        yT_ready = s.sem("yT_ready")
        o_ready = s.sem("o_ready")
        chain = s.sem("chain")

        def drained(eng, i, use):
            last = use - 2
            if last < 0:
                eng.wait_ge(o_ready, i * CPB)
                eng.wait_ge(yT_ready, i * CPB)
            elif last < Z_AT:
                eng.wait_ge(conv_done, i * CT + last - CONV_AT + 1)
            elif last < BT_AT:
                eng.wait_ge(z_ready, i * CPB + last - Z_AT + 1)
            elif last < TAIL_AT:
                eng.wait_ge(tok_ready, i * (2 + CPB) + last - BT_AT + 1)
            elif (last - TAIL_AT) % 2 == 0:
                eng.wait_ge(yT_ready, i * CPB + (last - TAIL_AT) // 2 + 1)
            else:
                eng.wait_ge(o_ready, i * CPB + (last - TAIL_AT) // 2 + 1)

        def heads(ap):
            return ap.unsqueeze(2).to_broadcast([P, NH, HD])

        def by_head(ap):
            return ap.rearrange("p (h e) -> p h e", h=NH)

        with nc.Block() as block:
            @block.sync
            def _(sp):
                sp.dma_start(w_in[:], w["in_T"].rearrange("(k p) n -> p k n", p=P)[:, :, 0:DI + CONV]).then_inc(weights_in, 16)
                sp.dma_start(w_out[:], w["out_T"].rearrange("(k p) n -> p k n", p=P)).then_inc(weights_in, 16)
                sp.dma_start(norm_w[:], w["norm_col"]).then_inc(weights_in, 16)
                sp.dma_start(w_fcd[:], w["fcd_T"].rearrange("(k p) n -> p k n", p=P)).then_inc(weights_in, 16)
                sp.dma_start(taps[:], w["taps"]).then_inc(weights_in, 16)
                sp.dma_start(conv_b[:], w["conv_b"]).then_inc(weights_in, 16)
                sp.dma_start(d_bc[:], w["d_bc"]).then_inc(weights_in, 16)
                sp.dma_start(d_col[:], w["d_col"]).then_inc(weights_in, 16)
                for i in range(BATCH):
                    if i:
                        sp.wait_ge(bank_ready, (i - 1) * USES + BT_AT)
                    sp.dma_start(xT[:], xT_d[:, i * SEQ:(i + 1) * SEQ].rearrange("(k p) t -> p k t", p=P)).then_inc(xT_in, 16)
                    if i:
                        sp.wait_ge(o_ready, i * CPB)
                        sp.dma_start(out_d[(i - 1) * SEQ:i * SEQ, :].rearrange("(c p) d -> p c d", p=P), o[:]).then_inc(out_stored, 16)
                    sp.dma_start(x[:], x_d[i * SEQ:(i + 1) * SEQ, :].rearrange("(c p) d -> p c d", p=P)).then_inc(x_in, 16)
                sp.wait_ge(o_ready, BATCH * CPB)
                sp.dma_start(out_d[(BATCH - 1) * SEQ:BATCH * SEQ, :].rearrange("(c p) d -> p c d", p=P), o[:]).then_inc(out_stored, 16)
                sp.wait_ge(out_stored, BATCH * 16)

            @block.tensor
            def _(pe):
                pe.wait_ge(weights_in, 8 * 16)
                pe.wait_ge(padded, 1)
                pe.wait_ge(diag_ready, DI // P)
                pe.wait_ge(wout_ready, DI // P)
                with pe.Fori(0, BATCH) as i:
                    pe.wait_ge(xT_in, (i + 1) * 16)
                    for n, m in enumerate(ORDER):
                        drained(pe, i, CONV_AT + n)
                        for k in range(KD):
                            mm = nc.tensor.matmul(psA[n % 2][:], w_in[:, k, DI + m * P:DI + (m + 1) * P], xT[:, k],
                                                  start=(k == 0), stop=(k == KD - 1))
                        mm.then_inc(bank_ready, 1)
                    for t in range(CPB):
                        use = Z_AT + t
                        drained(pe, i, use)
                        for k in range(KD):
                            mm = nc.tensor.matmul(psA[use % 2][:], xT[:, k, t * P:(t + 1) * P], w_in[:, k, 0:DI],
                                                  start=(k == 0), stop=(k == KD - 1))
                        mm.then_inc(bank_ready, 1)
                    pe.wait_ge(ab_ready, i + 1)
                    pe.wait_ge(gm_ready, i * CPB)
                    for q in range(3):
                        for d in range(2):
                            lhs = C.ones if q == 2 else tri[d] if q == 0 else tri[1 - d]
                            at = (q * 2 + d) * CPB * NH
                            mm = nc.tensor.matmul(sums[:, at:at + CPB * NH], lhs[:], ab[:, d], start=True, stop=True)
                    mm.then_inc(sums_ready, 1)
                    pe.wait_ge(xc_ready, i * CT + 4)
                    for d in range(2):
                        use = BT_AT + d
                        drained(pe, i, use)
                        for t in range(CPB):
                            mm = nc.tensor.transpose(psA[use % 2][:, t * P:(t + 1) * P],
                                                     xc[:, 4 + 2 * d, 1 + t * P:1 + (t + 1) * P], C.ident[:])
                        mm.then_inc(bank_ready, 1)
                    pe.wait_ge(xc_ready, (i + 1) * CT)
                    for t in range(CPB):
                        use = XT_AT + t
                        drained(pe, i, use)
                        for m in range(DI // P):
                            mm = nc.tensor.transpose(psA[use % 2][:, m * P:(m + 1) * P],
                                                     xc[:, m, 1 + t * P:1 + (t + 1) * P], C.ident[:])
                        mm.then_inc(bank_ready, 1)
                    pe.wait_ge(fac_ready, i + 1)
                    for t in range(CPB):
                        for m in range(DI // P):
                            mm = nc.tensor.matmul(fd_ps[:, t], xc[:, m, 1 + t * P:1 + (t + 1) * P], w_fcd[:, m],
                                                  start=(m == 0), stop=(m == DI // P - 1))
                    mm.then_inc(fd_done, 1)
                    for k in range(CPB - 1):
                        for d in range(2):
                            n = 2 * k + d
                            t = k if d == 0 else CPB - 1 - k
                            pe.wait_ge(xdd_ready, i * 6 + n + 1)
                            if n >= 2:
                                pe.wait_ge(state_ready, i * 6 + n - 1)
                            else:
                                pe.wait_ge(off_scaled, i * 6)
                            nc.tensor.matmul(psO[d][:], Bl[:, d, t], xdd[:, d], start=True, stop=True).then_inc(grown, 1)

                    def segment(u):
                        t, d = u // 2, u % 2
                        if d == 0:
                            pe.wait_ge(fd_ready, i + 1)
                            pe.wait_ge(gm_ready, i * CPB + t)
                            for e in range(2):
                                lo = t * P + (0 if e == 0 else 2)
                                mm = nc.tensor.matmul(gT[:, e], xc[:, 4 + 2 * e, 1 + t * P:1 + (t + 1) * P],
                                                      xc[:, 5 + 2 * e, lo:lo + P], start=True, stop=True)
                            mm.then_inc(g_ready, 1)
                        pe.wait_ge(am_ready, i * U + u + 1)
                        pe.wait_ge(seg_exped, (i * U + u) * 2)
                        for hf in range(2):
                            nc.tensor.matmul(psS[hf][:], tri[1 - d][:], am[:, u % 2, 4 * hf:4 * hf + 4],
                                             start=True, stop=True).then_inc(seg_ready, 1)

                    def diagonal(u):
                        t, d = u // 2, u % 2
                        if d == 0:
                            pe.wait_ge(y_read, i * CPB + t)
                            pe.wait_ge(near_ready, i + 1)
                            for m in range(DI // P):
                                nc.tensor.matmul(psY[:, m * P:(m + 1) * P], near[:, m, t * P:(t + 1) * P], d_diag[:, m],
                                                 start=(m == 0), stop=False, skip_group_check=True)
                        pe.wait_ge(L_ready, i * U + u + 1)
                        pe.wait_ge(xdt_ready, i * U + u + 1)
                        for h in range(NH):
                            mm = nc.tensor.matmul(psY[:, h * HD:(h + 1) * HD], L[:, u % 2, h], xdt[:, u % 2, h * HD:(h + 1) * HD],
                                                  start=False, stop=(d == 1), skip_group_check=True)
                        mm.then_inc(diag_used, 1)
                        if (d == 0 and t > 0) or (d == 1 and t < CPB - 1):
                            pe.wait_ge(state_ready, (i + 1) * 6)
                            done = [2 * (t - 1) if t > 1 else 0, 2 * t][d]
                            pe.wait_ge(off_scaled, i * 6 + done)
                            lo = t * P + (0 if d == 0 else 2)
                            nc.tensor.matmul(psO[d][:], xc[:, 5 + 2 * d, lo:lo + P], state[:, d, t],
                                             start=True, stop=True).then_inc(off_ready, 1)

                    def tail(t):
                        use = TAIL_AT + 2 * t
                        drained(pe, i, use)
                        pe.wait_ge(gated, i * CPB + t + 1)
                        for m in range(DI // P):
                            mm = nc.tensor.transpose(psA[use % 2][:, m * P:(m + 1) * P], y[:, t % 2, m * P:(m + 1) * P], C.ident[:])
                        mm.then_inc(bank_ready, 1)
                        drained(pe, i, use + 1)
                        pe.wait_ge(yT_ready, i * CPB + t + 1)
                        for m in range(DI // P):
                            mm = nc.tensor.matmul(psA[(use + 1) % 2][:, 0:D], yT[:, t % 2, m], w_out[:, m],
                                                  start=(m == 0), stop=(m == DI // P - 1))
                        mm.then_inc(bank_ready, 1)

                    for u in range(U + 1):
                        if u < U:
                            segment(u)
                        if u >= 1:
                            diagonal(u - 1)
                        if u >= 4 and u % 2 == 0:
                            tail(u // 2 - 2)
                    tail(CPB - 1)

            @block.scalar
            def _(act):
                act.wait_ge(weights_in, 8 * 16)
                with act.Fori(0, BATCH) as i:
                    def silu(n):
                        act.wait_ge(conv_done, i * CT + n + 1)
                        if n == 0:
                            act.wait_ge(diag_used, i * U)
                            act.wait_ge(off_ready, i * 6)
                            act.wait_ge(near_ready, i)
                        nc.scalar.activation(xc[:, ORDER[n], 1:1 + SEQ], acc[:, n % 4], ACT.Silu).then_inc(xc_ready, 1)

                    for n in range(CT):
                        m = ORDER[n]
                        act.wait_ge(bank_ready, i * USES + CONV_AT + n + 1)
                        if n >= 4:
                            act.wait_ge(xc_ready, i * CT + n - 3)
                        else:
                            act.wait_ge(xc_ready, i * CT)
                        nc.scalar.activation(acc[:, n % 4], psA[n % 2][:], ACT.Identity, bias=conv_b[:, m:m + 1],
                                             scale=taps[:, m, TAPS - 1:TAPS]).then_inc(tap0, 1)
                        if n % 2 == 1 and n >= 3:
                            silu(n - 3)
                            silu(n - 2)
                    silu(CT - 2)
                    silu(CT - 1)
                    for t in range(CPB):
                        act.wait_ge(bank_ready, i * USES + Z_AT + t + 1)
                        if t == 0:
                            act.wait_ge(gated, i * CPB)
                        nc.scalar.activation(zs[:, t], psA[(Z_AT + t) % 2][:], ACT.Silu).then_inc(z_ready, 1)
                    for d in range(2):
                        act.wait_ge(bank_ready, i * USES + BT_AT + d + 1)
                        act.wait_ge(grown, i * 6)
                        nc.scalar.copy(Bl[:, d], psA[(BT_AT + d) % 2][:].rearrange("p (t n) -> p t n", t=CPB)).then_inc(tok_ready, 1)
                    for t in range(CPB):
                        act.wait_ge(bank_ready, i * USES + XT_AT + t + 1)
                        act.wait_ge(xdt_ready, i * U)
                        act.wait_ge(xfd_ready, i * CPB)
                        nc.scalar.copy(xl[:, t], psA[(XT_AT + t) % 2][:]).then_inc(tok_ready, 1)
                    act.wait_ge(sums_ready, i + 1)
                    act.wait_ge(off_scaled, i * 6)
                    nc.scalar.activation(fac[:].rearrange("p a b c h -> p (a b c h)"), sums, ACT.Exp).then_inc(fac_ready, 1)

                    def tail(t):
                        act.wait_ge(gated, i * CPB + t + 1)
                        if t == 0:
                            act.wait_ge(rstd_ready, i * CPB)
                        act.wait_ge(squared, i * CPB + t)
                        nc.scalar.activation(sq[:], y[:, t % 2], ACT.Square, accum_out=ssum[:, t:t + 1]).then_inc(squared, 1)
                        act.wait_ge(squared, i * CPB + t + 1)
                        nc.scalar.activation(var[:, t:t + 1], ssum[:, t:t + 1], ACT.Copy, bias=EPS, scale=1.0 / DI).then_inc(var_ready, 1)
                        act.wait_ge(bank_ready, i * USES + TAIL_AT + 2 * t + 1)
                        if t >= 2:
                            act.wait_ge(bank_ready, i * USES + TAIL_AT + 2 * (t - 2) + 2)
                        else:
                            act.wait_ge(bank_ready, i * USES)
                        nc.scalar.copy(yT[:, t % 2], psA[(TAIL_AT + 2 * t) % 2][:].rearrange("p (m t) -> p m t", m=DI // P)).then_inc(yT_ready, 1)

                    for u in range(U):
                        if u >= 2:
                            act.wait_ge(diag_used, i * U + u - 1)
                        else:
                            act.wait_ge(diag_used, i * U)
                        for hf in range(2):
                            act.wait_ge(seg_ready, (i * U + u) * 2 + hf + 1)
                            nc.scalar.activation(L[:, u % 2, 4 * hf:4 * hf + 4], psS[hf][:], ACT.Exp).then_inc(seg_exped, 1)
                        if u >= 4 and u % 2 == 0:
                            tail(u // 2 - 2)
                    tail(CPB - 2)
                    tail(CPB - 1)

            @block.gpsimd
            def _(pool):
                nc.gpsimd.memset(xc[:, :, 0:1], 0.0)
                nc.gpsimd.memset(xc[:, :, XW - 1:XW], 0.0).then_inc(padded, 1)
                with pool.Fori(0, BATCH) as i:
                    def masked_a(u):
                        t, d = u // 2, u % 2
                        if u == 0:
                            pool.wait_ge(ab_ready, i + 1)
                        if u >= 2:
                            pool.wait_ge(seg_ready, (i * U + u - 1) * 2)
                        else:
                            pool.wait_ge(seg_ready, i * U * 2)
                        nc.gpsimd.tensor_tensor(am[:, u % 2], tri[d][:].unsqueeze(1).to_broadcast([P, NH, P]),
                                                ab[:, d, t].unsqueeze(2).to_broadcast([P, NH, P]), ALU.mult).then_inc(am_ready, 1)

                    def rms(t):
                        pool.wait_ge(var_ready, i * CPB + t + 1)
                        nc.gpsimd.tensor_tensor(rstd[:, t:t + 1], var[:, t:t + 1], C.half[:, 0:1], ALU.pow).then_inc(rstd_ready, 1)

                    masked_a(0)
                    masked_a(1)
                    pool.wait_ge(dtdec_ready, i + 1)
                    pool.wait_ge(tok_ready, (i + 1) * (2 + CPB))
                    for k in range(CPB - 1):
                        for d in range(2):
                            n = 2 * k + d
                            t = k if d == 0 else CPB - 1 - k
                            if n >= 2:
                                pool.wait_ge(grown, i * 6 + n - 1)
                            else:
                                pool.wait_ge(grown, i * 6)
                            nc.gpsimd.tensor_tensor(by_head(xdd[:, d]), by_head(xl[:, t]), heads(dtdec[:, d, t]), ALU.mult).then_inc(xdd_ready, 1)
                    for u in range(U):
                        t, d = u // 2, u % 2
                        if u >= 2:
                            masked_a(u)
                            pool.wait_ge(diag_used, i * U + u - 1)
                        else:
                            pool.wait_ge(diag_used, i * U)
                        nc.gpsimd.tensor_tensor(by_head(xdt[:, u % 2]), by_head(xl[:, t]), heads(dtb[:, d, t]), ALU.mult).then_inc(xdt_ready, 1)
                        if d == 0:
                            if t == 0:
                                pool.wait_ge(fd_ready, i + 1)
                            pool.wait_ge(y_read, i * CPB + t)
                            nc.gpsimd.tensor_tensor(by_head(xfd[:]), by_head(xl[:, t]), heads(fd[:, t]), ALU.mult).then_inc(xfd_ready, 1)
                        if u >= 5 and d == 1:
                            rms((u - 5) // 2)
                    rms(CPB - 2)
                    rms(CPB - 1)

            @block.vector
            def _(dve):
                v = nc.vector
                dve.wait_ge(weights_in, 8 * 16)
                for m in range(DI // P):
                    v.tensor_scalar(d_diag[:, m], C.ident[:], d_col[:, m:m + 1], None, ALU.mult).then_inc(diag_ready, 1)
                    v.tensor_scalar(w_out[:, m], w_out[:, m], norm_w[:, m:m + 1], None, ALU.mult).then_inc(wout_ready, 1)
                LINKS = CT * 2 + 2 * (CPB - 2) + CPB - 2
                with dve.Fori(0, BATCH) as i:
                    c = Chain(dve, chain, i, LINKS)
                    dve.wait_ge(am_ready, i * U)
                    dve.wait_ge(xdt_ready, i * U)
                    for d in range(2):
                        v.tensor_copy(dtb[:, d], dt[:, bass.ds(i * CPB, CPB), d * NH:(d + 1) * NH])
                        cp = v.tensor_copy(ab[:, d], a[:, bass.ds(i * CPB, CPB), d * NH:(d + 1) * NH])
                    cp.then_inc(ab_ready, 1)
                    for n in range(0, CT, 2):
                        dve.wait_ge(tap0, i * CT + n + 2)
                        for j in range(1, TAPS):
                            for q in (n, n + 1):
                                ins = v.scalar_tensor_tensor(
                                    out=acc[:, q % 4, j:SEQ], in0=psA[q % 2][:, 0:SEQ - j],
                                    scalar=taps[:, ORDER[q], TAPS - 1 - j:TAPS - j], in1=acc[:, q % 4, j:SEQ],
                                    op0=ALU.mult, op1=ALU.add)
                                if j < TAPS - 1:
                                    c.link(ins)
                                else:
                                    ins.then_inc(conv_done, 1)
                            if j < TAPS - 1:
                                c.wait()
                    dve.wait_ge(ab_ready, i + 1)
                    dve.wait_ge(fac_ready, i + 1)
                    dve.wait_ge(xdd_ready, i * 6)
                    v.tensor_tensor(dtdec[:], dtb[:], fac[:, 1], ALU.mult).then_inc(dtdec_ready, 1)
                    dve.wait_ge(xc_ready, (i + 1) * CT)
                    dve.wait_ge(diag_used, i * U)
                    v.tensor_tensor(near[:], xc[:, 0:DI // P, 0:SEQ], xc[:, 0:DI // P, 2:2 + SEQ], ALU.add).then_inc(near_ready, 1)
                    dve.wait_ge(fd_done, i + 1)
                    dve.wait_ge(xfd_ready, i * CPB)
                    v.tensor_tensor(fd[:], fd_ps, d_bc[:].unsqueeze(1).to_broadcast([P, CPB, NH]), ALU.add).then_inc(fd_ready, 1)
                    for k in range(CPB - 1):
                        for d in range(2):
                            n = 2 * k + d
                            t = k if d == 0 else CPB - 1 - k
                            to = t + 1 if d == 0 else t - 1
                            if n == 0:
                                dve.wait_ge(off_ready, i * 6)
                            if k:
                                dve.wait_ge(state_ready, i * 6 + n - 1)
                                c.step(v.tensor_tensor(by_head(scaled[:, d]), by_head(state[:, d, t]), heads(fac[:, 2, d, t]), ALU.mult))
                            dve.wait_ge(grown, i * 6 + n + 1)
                            if k:
                                v.tensor_tensor(state[:, d, to], scaled[:, d], psO[d][:], ALU.add).then_inc(state_ready, 1)
                            else:
                                v.tensor_copy(state[:, d, to], psO[d][:]).then_inc(state_ready, 1)

                    def decays(u):
                        t, d = u // 2, u % 2
                        if d == 0:
                            dve.wait_ge(g_ready, i * CPB + t + 1)
                            dve.wait_ge(L_ready, i * U + u)
                            for e in range(2):
                                ins = v.tensor_tensor(Gm[:, e], gT[:, e], tri[e][:], ALU.mult)
                            ins.then_inc(gm_ready, 1)
                            dve.wait_ge(gm_ready, i * CPB + t + 1)
                        dve.wait_ge(seg_exped, (i * U + u + 1) * 2)
                        v.tensor_tensor(L[:, u % 2], L[:, u % 2], Gm[:, d].unsqueeze(1).to_broadcast([P, NH, P]), ALU.mult).then_inc(L_ready, 1)

                    def off(u, count):
                        t, d = u // 2, u % 2
                        if (d == 0 and t > 0) or (d == 1 and t < CPB - 1):
                            dve.wait_ge(off_ready, i * 6 + count + 1)
                            dve.wait_ge(summed, i * CPB + t)
                            v.tensor_tensor(by_head(yo[:, d]), by_head(psO[d][:]), heads(fac[:, 0, d, t]), ALU.mult).then_inc(off_scaled, 1)
                            return count + 1
                        return count

                    def finish(t):
                        b = t % 2
                        dve.wait_ge(diag_used, i * U + 2 * t + 2)
                        dve.wait_ge(xfd_ready, i * CPB + t + 1)
                        if t >= 2:
                            dve.wait_ge(bank_ready, i * USES + TAIL_AT + 2 * (t - 2) + 1)
                            dve.wait_ge(squared, i * CPB + t - 1)
                        else:
                            dve.wait_ge(bank_ready, i * USES)
                            dve.wait_ge(squared, i * CPB)
                        v.tensor_tensor(y[:, b], psY[:], xfd[:], ALU.add).then_inc(y_read, 1)
                        dve.wait_ge(y_read, i * CPB + t + 1)
                        dve.wait_ge(off_scaled, i * 6 + [1, 3, 5, 6][t])
                        if 0 < t < CPB - 1:
                            c.step(v.tensor_tensor(yo[:, 0], yo[:, 0], yo[:, 1], ALU.add))
                        v.tensor_tensor(y[:, b], y[:, b], yo[:, 1 if t == 0 else 0], ALU.add).then_inc(summed, 1)
                        dve.wait_ge(summed, i * CPB + t + 1)
                        v.tensor_tensor(y[:, b], y[:, b], zs[:, t], ALU.mult).then_inc(gated, 1)

                    def outputs(t):
                        dve.wait_ge(bank_ready, i * USES + TAIL_AT + 2 * t + 2)
                        dve.wait_ge(rstd_ready, i * CPB + t + 1)
                        if t == 0:
                            dve.wait_ge(x_in, (i + 1) * 16)
                            dve.wait_ge(out_stored, i * 16)
                        v.scalar_tensor_tensor(out=o[:, t], in0=psA[(TAIL_AT + 1) % 2][:, 0:D], scalar=rstd[:, t:t + 1],
                                               in1=x[:, t], op0=ALU.mult, op1=ALU.add).then_inc(o_ready, 1)

                    count = 0
                    for u in range(U + 1):
                        if u < U:
                            decays(u)
                        if u >= 1:
                            count = off(u - 1, count)
                        if u >= 2 and u % 2 == 0:
                            finish(u // 2 - 1)
                        if u >= 5 and u % 2 == 1:
                            outputs((u - 5) // 2)
                    outputs(CPB - 2)
                    outputs(CPB - 1)
                    c.end()


def one_expert_each(nc, C, w1_d, b1_bc, w2_d, b2_bc, tile_expert, xs_d, ys_d):
    N = L0_TILES
    W1N, W2N = KD * DFF, FT * D
    HALF = 512
    LAG = 3
    with Space(nc, "ffn0") as s:
        w1 = s.sb("w1", [P, NE * W1N])
        w2 = s.sb("w2", [P, NE * W2N])
        b1 = s.sb("b1", [P, NE * DFF])
        b2 = s.sb("b2", [P, NE * D])
        xs = s.sb("xs", [P, 2, D])
        xT = s.sb("xT", [P, 2, KD, P])
        h = s.sb("h", [P, 2, DFF])
        hT = s.sb("hT", [P, 2, FT, P])
        y = s.sb("y", [P, 2, D])
        psX = s.psum("psX", [P, KD, P])
        psH = [s.psum(f"psH{j}", [P, HALF]) for j in range(4)]
        psT = [s.psum(f"psT{j}", [P, 4, P]) for j in range(2)]
        psY = s.psum("psY", [P, D])
        w1_in = [s.sem(f"w1_in{e}") for e in range(2)]
        bias_in = s.sem("bias_in")
        xs_in = [s.sem(f"xs_in{b}") for b in range(2)]
        x_turned = s.sem("x_turned")
        xT_ready = s.sem("xT_ready")
        up_done = s.sem("up_done")
        h_ready = s.sem("h_ready")
        h_turned = s.sem("h_turned")
        hT_ready = s.sem("hT_ready")
        down_done = s.sem("down_done")
        y_ready = s.sem("y_ready")
        y_stored = [s.sem(f"y_stored{b}") for b in range(2)]

        def pairs(eng, first, last, step):
            n = (last - first) // 2
            with eng.Fori(0, n) as i:
                step(i * 2 + first, first % 2)
                step(i * 2 + first + 1, (first + 1) % 2)
            for j in range(first + 2 * n, last):
                step(j, j % 2)

        with nc.Block() as block:
            @block.sync
            def _(sp):
                sp.dma_start(w1[:].rearrange("p (e k n) -> p e k n", e=NE, k=KD),
                             w1_d.rearrange("e (k p) n -> p e k n", p=P)).then_inc(w1_in[0], 16)
                sp.dma_start(w2[:].rearrange("p (e k n) -> p e k n", e=NE, k=FT),
                             w2_d.rearrange("e (k p) n -> p e k n", p=P)).then_inc(w1_in[1], 16)
                sp.dma_start(b1[:], b1_bc).then_inc(bias_in, 16)
                sp.dma_start(b2[:], b2_bc).then_inc(bias_in, 16)
                for j in range(N + LAG):
                    if j < N:
                        if j >= 2:
                            sp.wait_ge(x_turned, j - 1)
                        sp.dma_start(xs[:, j % 2], xs_d[j * P:(j + 1) * P, :]).then_inc(xs_in[j % 2], 16)
                    done = j - LAG
                    if done >= 0:
                        sp.wait_ge(y_ready, done + 1)
                        sp.dma_start(ys_d[done * P:(done + 1) * P, :], y[:, done % 2]).then_inc(y_stored[done % 2], 16)
                sp.wait_ge(y_stored[0], (N + 1) // 2 * 16)
                sp.wait_ge(y_stored[1], N // 2 * 16)

            @block.tensor
            def _(pe):
                def turn_x(j, b):
                    pe.wait_ge(xs_in[b], ((j - b) // 2 + 1) * 16 if isinstance(j, int) else (j - b) * 8 + 16)
                    pe.wait_ge(xT_ready, j)
                    for k in range(KD):
                        mm = nc.tensor.transpose(psX[:, k], xs[:, b, k * P:(k + 1) * P], C.ident[:])
                    mm.then_inc(x_turned, 1)

                def up(j, b):
                    at = nc.tensor.value_load(tile_expert[0:1, bass.ds(j, 1)], min_val=0, max_val=NE - 1)
                    pe.wait_ge(xT_ready, j + 1)
                    if not isinstance(j, int) or j >= 2:
                        pe.wait_ge(h_ready, (j - 1) * 2)
                    for hf in range(2):
                        for k in range(KD):
                            mm = nc.tensor.matmul(psH[2 * b + hf][:], xT[:, b, k],
                                                  w1[:, bass.ds(at * W1N + (k * DFF + hf * HALF), HALF)],
                                                  start=(k == 0), stop=(k == KD - 1))
                        mm.then_inc(up_done, 1)

                def turn_h(j, b):
                    for hf in range(2):
                        pe.wait_ge(h_ready, j * 2 + hf + 1)
                        pe.wait_ge(hT_ready, j * 2)
                        for q in range(4):
                            mm = nc.tensor.transpose(psT[hf][:, q], h[:, b, hf * HALF + q * P:hf * HALF + (q + 1) * P], C.ident[:])
                        mm.then_inc(h_turned, 1)

                def down(j, b):
                    at = nc.tensor.value_load(tile_expert[0:1, bass.ds(j, 1)], min_val=0, max_val=NE - 1)
                    pe.wait_ge(hT_ready, j * 2 + 2)
                    pe.wait_ge(y_ready, j)
                    for f in range(FT):
                        mm = nc.tensor.matmul(psY[:], hT[:, b, f], w2[:, bass.ds(at * W2N + f * D, D)],
                                              start=(f == 0), stop=(f == FT - 1))
                    mm.then_inc(down_done, 1)

                turn_x(0, 0)
                turn_x(1, 1)
                pe.wait_ge(w1_in[0], 16)
                pe.wait_ge(w1_in[1], 16)
                up(0, 0)
                up(1, 1)
                turn_h(0, 0)

                def step(j, b):
                    turn_x(j + 1, 1 - b)
                    up(j + 1, 1 - b)
                    turn_h(j, b)
                    down(j - 1, 1 - b)

                pairs(pe, 1, N - 1, step)
                turn_h(N - 1, (N - 1) % 2)
                down(N - 2, N % 2)
                down(N - 1, (N - 1) % 2)

            @block.scalar
            def _(act):
                def x_out(j, b):
                    act.wait_ge(x_turned, j + 1)
                    if not isinstance(j, int) or j >= 2:
                        act.wait_ge(up_done, (j - 1) * 2)
                    nc.scalar.copy(xT[:, b], psX[:]).then_inc(xT_ready, 1)

                def relu(j, b):
                    if not isinstance(j, int) or j >= 2:
                        act.wait_ge(down_done, j - 1)
                    for hf in range(2):
                        act.wait_ge(h_turned, j * 2 + hf + 1)
                        nc.scalar.activation(hT[:, b, 4 * hf:4 * hf + 4], psT[hf][:], ACT.Relu).then_inc(hT_ready, 1)

                x_out(0, 0)
                x_out(1, 1)
                relu(0, 0)

                def step(j, b):
                    x_out(j + 1, 1 - b)
                    relu(j, b)

                pairs(act, 1, N - 1, step)
                relu(N - 1, (N - 1) % 2)

            @block.vector
            def _(dve):
                v = nc.vector

                def hidden(j, b):
                    at = v.value_load(tile_expert[0:1, bass.ds(j, 1)], min_val=0, max_val=NE - 1)
                    if not isinstance(j, int) or j >= 2:
                        dve.wait_ge(h_turned, (j - 1) * 2)
                    for hf in range(2):
                        dve.wait_ge(up_done, j * 2 + hf + 1)
                        v.tensor_tensor(h[:, b, hf * HALF:(hf + 1) * HALF], psH[2 * b + hf][:],
                                        b1[:, bass.ds(at * DFF + hf * HALF, HALF)], ALU.add).then_inc(h_ready, 1)

                def result(j, b):
                    at = v.value_load(tile_expert[0:1, bass.ds(j, 1)], min_val=0, max_val=NE - 1)
                    dve.wait_ge(down_done, j + 1)
                    if not isinstance(j, int) or j >= 2:
                        dve.wait_ge(y_stored[b], (j - b) * 8)
                    v.tensor_tensor(y[:, b], psY[:], b2[:, bass.ds(at * D, D)], ALU.add).then_inc(y_ready, 1)

                dve.wait_ge(bias_in, 32)
                hidden(0, 0)
                hidden(1, 1)

                def step(j, b):
                    hidden(j + 1, 1 - b)
                    result(j - 1, 1 - b)

                pairs(dve, 1, N - 1, step)
                result(N - 2, N % 2)
                result(N - 1, (N - 1) % 2)


def gather(nc, name, rows_d, slots, n_rows, got):
    picks = len(slots)
    with Space(nc, name) as s:
        cleared = s.sem("cleared")
        gathered = s.sem("gathered")
        with nc.Block() as block:
            @block.gpsimd
            def _(pool):
                if picks > 1:
                    pool.wait_ge(cleared, picks)
                for t in range(NT):
                    for k in range(picks):
                        nc.gpsimd.indirect_dma_start(
                            out=got[k][:, t, :], out_offset=None, in_=rows_d,
                            in_offset=bass.IndirectOffsetOnAxis(ap=slots[k][:, t:t + 1], axis=0),
                            bounds_check=n_rows - 1, oob_is_err=(picks == 1)).then_inc(gathered, 16)
                pool.wait_ge(gathered, NT * picks * 16)

            @block.vector
            def _(dve):
                if picks > 1:
                    for k in range(picks):
                        nc.vector.memset(got[k][:], 0.0).then_inc(cleared, 1)


def full_experts(nc, C, w1_d, w2_d, xs_d, ys_d):
    RT = CAP // P
    with Space(nc, "ffn1") as s:
        w1 = s.sb("w1", [P, 2, KD, DFF])
        w2 = s.sb("w2", [P, 2, FT, D])
        xs = s.sb("xs", [P, 2, RT, D])
        xT = s.sb("xT", [P, 2, KD, CAP])
        hT = s.sb("hT", [P, FT, CAP])
        y = s.sb("y", [P, RT, D])
        psX = [s.psum(f"psX{k}", [P, CAP]) for k in range(KD)]
        psH = [s.psum(f"psH{j}", [P, CAP]) for j in range(4)]
        psY = [s.psum(f"psY{j}", [P, D]) for j in range(2)]
        w_in = [s.sem(f"w_in{b}") for b in range(2)]
        xs_in = [s.sem(f"xs_in{b}") for b in range(2)]
        x_turned = s.sem("x_turned")
        xT_ready = s.sem("xT_ready")
        up_done = s.sem("up_done")
        hT_ready = s.sem("hT_ready")
        down_done = s.sem("down_done")
        y_ready = s.sem("y_ready")
        y_stored = s.sem("y_stored")
        N = L1_EXPERTS

        def all_experts(eng, step):
            with eng.Fori(0, N // 2) as i:
                step(i * 2, 0)
                step(i * 2 + 1, 1)
            step(N - 1, 0)

        with nc.Block() as block:
            @block.sync
            def _(sp):
                for e in range(N):
                    b = e % 2
                    if e >= 2:
                        sp.wait_ge(down_done, (e - 1) * RT)
                    sp.dma_start(xs[:, b], xs_d[e * CAP:(e + 1) * CAP, :].rearrange("(t p) d -> p t d", p=P)).then_inc(xs_in[b], 16)
                    sp.dma_start(w1[:, b], w1_d[e].rearrange("(k p) n -> p k n", p=P)).then_inc(w_in[b], 16)
                    sp.dma_start(w2[:, b], w2_d[e].rearrange("(k p) n -> p k n", p=P)).then_inc(w_in[b], 16)

            @block.tensor
            def _(pe):
                def step(e, b):
                    turn = (e - b) * 8 + 16
                    pe.wait_ge(xs_in[b], turn)
                    for k in range(KD):
                        pe.wait_ge(xT_ready, e * KD)
                        for t in range(RT):
                            mm = nc.tensor.transpose(psX[k][:, t * P:(t + 1) * P], xs[:, b, t, k * P:(k + 1) * P], C.ident[:])
                        mm.then_inc(x_turned, 1)
                    pe.wait_ge(w_in[b], turn * 2)
                    pe.wait_ge(xT_ready, (e + 1) * KD)
                    for f in range(FT):
                        pe.wait_ge(hT_ready, e * FT + max(f - 3, 0))
                        for k in range(KD):
                            mm = nc.tensor.matmul(psH[f % 4][:], w1[:, b, k, f * P:(f + 1) * P], xT[:, b, k],
                                                  start=(k == 0), stop=(k == KD - 1))
                        mm.then_inc(up_done, 1)
                    for t in range(RT):
                        pe.wait_ge(hT_ready, (e + 1) * FT)
                        pe.wait_ge(y_ready, e * RT + max(t - 1, 0))
                        for f in range(FT):
                            mm = nc.tensor.matmul(psY[t % 2][:], hT[:, f, t * P:(t + 1) * P], w2[:, b, f],
                                                  start=(f == 0), stop=(f == FT - 1))
                        mm.then_inc(down_done, 1)

                all_experts(pe, step)

            @block.scalar
            def _(act):
                def step(e, b):
                    for k in range(KD):
                        act.wait_ge(x_turned, e * KD + k + 1)
                        act.wait_ge(up_done, e * FT)
                        nc.scalar.copy(xT[:, b, k], psX[k][:]).then_inc(xT_ready, 1)
                    for f in range(FT):
                        act.wait_ge(up_done, e * FT + f + 1)
                        act.wait_ge(down_done, e * RT)
                        nc.scalar.activation(hT[:, f], psH[f % 4][:], ACT.Relu).then_inc(hT_ready, 1)

                all_experts(act, step)

            @block.vector
            def _(dve):
                def step(e, b):
                    for t in range(RT):
                        dve.wait_ge(down_done, e * RT + t + 1)
                        if t == 0:
                            dve.wait_ge(y_stored, e * 16)
                        nc.vector.tensor_copy(y[:, t], psY[t % 2][:]).then_inc(y_ready, 1)

                all_experts(dve, step)

            @block.gpsimd
            def _(pool):
                for e in range(N):
                    pool.wait_ge(y_ready, (e + 1) * RT)
                    pool.dma_start(ys_d[e * CAP:(e + 1) * CAP, :].rearrange("(t p) d -> p t d", p=P), y[:]).then_inc(y_stored, 16)
                pool.wait_ge(y_stored, N * 16)



PAIRS = [(0, 0), (0, 1), (1, 0), (1, 1), (0, 2), (2, 0), (1, 2), (2, 1)]


def project(nc, C, xT_d, w, qp_d, kp_d, v_all):
    with Space(nc, "proj") as s:
        wq = s.sb("wq", [P, KD, D])
        wk = s.sb("wk", [P, KD, D])
        wv = s.sb("wv", [P, KD, D])
        wd = s.sb("wd", [P, KD, LAT])
        wuk = s.sb("wuk", [LAT, D])
        wuv = s.sb("wuv", [LAT, D])
        xT = s.sb("xT", [P, 2, KD, SEQ])
        kvT = s.sb("kvT", [P, KD, SEQ])
        latT = s.sb("latT", [LAT, SEQ])
        qk = s.sb("qk", [P, 2, KD, SEQ])
        rest = s.sb("rest", [P, 2, KD, SEQ])
        parts = s.sb("parts", [P, 2, 3, KD, SEQ], BF16)
        psQ = [s.psum(f"psQ{m}", [P, SEQ]) for m in range(KD)]
        psK = [s.psum(f"psK{m}", [P, SEQ]) for m in range(KD)]
        psKV = [s.psum(f"psKV{m}", [P, SEQ]) for m in range(KD)]
        psL = s.psum("psL", [P, SEQ])
        psV = s.psum("psV", [P, 2, D])
        w_in = s.sem("w_in")
        wkv_ready = s.sem("wkv_ready")
        xT_in = [s.sem(f"xT_in{b}") for b in range(2)]
        q_done = s.sem("q_done")
        kv_done = s.sem("kv_done")
        kv_ready = s.sem("kv_ready")
        lat_done = s.sem("lat_done")
        lat_ready = s.sem("lat_ready")
        k_done = s.sem("k_done")
        v_done = s.sem("v_done")
        v_ready = s.sem("v_ready")
        taken = s.sem("taken")
        high = s.sem("high")
        rest_ready = s.sem("rest_ready")
        mid = s.sem("mid")
        low = s.sem("low")
        stored = [s.sem(f"stored{j}") for j in range(2)]

        def loop(eng, step):
            with eng.Fori(0, BATCH // 2) as i:
                step(i * 2, 0)
                step(i * 2 + 1, 1)

        with nc.Block() as block:
            @block.sync
            def _(sp):
                for dst, src in ((wq, w["wq"]), (wk, w["wk"]), (wv, w["wv"]), (wd, w["wd"])):
                    sp.dma_start(dst[:], src.rearrange("(k p) n -> p k n", p=P)).then_inc(w_in, 16)
                sp.dma_start(wuk[:], w["wuk"]).then_inc(w_in, 16)
                sp.dma_start(wuv[:], w["wuv"]).then_inc(w_in, 16)
                for b in range(BATCH + 1):
                    if b < BATCH:
                        if b >= 2:
                            sp.wait_ge(v_done, (b - 1) * 2)
                            sp.wait_ge(q_done, (b - 1) * KD)
                        sp.dma_start(xT[:, b % 2], xT_d[:, b * SEQ:(b + 1) * SEQ].rearrange("(k p) t -> p k t", p=P)).then_inc(xT_in[b % 2], 16)
                    if b:
                        for j, dst in enumerate((qp_d, kp_d)):
                            sp.wait_ge(low, (b - 1) * 2 + j + 1)
                            sp.dma_start(dst[b - 1].rearrange("a (m p) t -> p (a m) t", p=P),
                                         parts[:, j].rearrange("p a m t -> p (a m) t")).then_inc(stored[j], 16)
                for j in range(2):
                    sp.wait_ge(stored[j], BATCH * 16)

            @block.tensor
            def _(pe):
                pe.wait_ge(w_in, 6 * 16)

                def step(b, slot):
                    pe.wait_ge(xT_in[slot], (b - slot) * 8 + 16)
                    for m in range(KD):
                        pe.wait_ge(taken, b * 2)
                        for k in range(KD):
                            mm = nc.tensor.matmul(psQ[m][:], wq[:, k, m * P:(m + 1) * P], xT[:, slot, k],
                                                  start=(k == 0), stop=(k == KD - 1))
                        mm.then_inc(q_done, 1)
                    for m in range(KD):
                        pe.wait_ge(kv_ready, b * KD)
                        for n, ww in enumerate((wk, wv)):
                            for k in range(KD):
                                mm = nc.tensor.matmul(psKV[m][:], ww[:, k, m * P:(m + 1) * P], xT[:, slot, k],
                                                      start=(n == 0 and k == 0), stop=(n == 1 and k == KD - 1))
                        mm.then_inc(kv_done, 1)
                    pe.wait_ge(kv_ready, (b + 1) * KD)
                    pe.wait_ge(lat_ready, b)
                    for k in range(KD):
                        mm = nc.tensor.matmul(psL[0:LAT, :], wd[:, k], kvT[:, k], start=(k == 0), stop=(k == KD - 1))
                    mm.then_inc(lat_done, 1)
                    pe.wait_ge(lat_ready, b + 1)
                    for m in range(KD):
                        mm = nc.tensor.matmul(psK[m][:], wuk[:, m * P:(m + 1) * P], latT[:], start=True, stop=True)
                    mm.then_inc(k_done, 1)
                    for g in range(2):
                        pe.wait_ge(v_ready, b * 2 + g)
                        for t in range(2):
                            mm = nc.tensor.matmul(psV[:, t], latT[:, (2 * g + t) * P:(2 * g + t + 1) * P], wuv[:], start=True, stop=True)
                        mm.then_inc(v_done, 1)

                loop(pe, step)

            @block.scalar
            def _(act):
                def step(b, slot):
                    for m in range(KD):
                        act.wait_ge(kv_done, b * KD + m + 1)
                        act.wait_ge(lat_done, b)
                        nc.scalar.copy(kvT[:, m], psKV[m][:]).then_inc(kv_ready, 1)
                    act.wait_ge(lat_done, b + 1)
                    act.wait_ge(v_done, b * 2)
                    nc.scalar.copy(latT[:], psL[0:LAT, :]).then_inc(lat_ready, 1)
                    for j in range(2):
                        act.wait_ge(taken, b * 2 + j + 1)
                        act.wait_ge(stored[j], b * 16)
                        nc.scalar.copy(parts[:, j, 0], qk[:, j]).then_inc(high, 1)
                        act.wait_ge(rest_ready, b * 2 + j + 1)
                        nc.scalar.copy(parts[:, j, 1], rest[:, j]).then_inc(mid, 1)

                loop(act, step)

            @block.vector
            def _(dve):
                v = nc.vector

                def step(b, slot):
                    for j, (ps, done, scale) in enumerate(((psQ, q_done, 1.0 / 16.0), (psK, k_done, 1.0))):
                        dve.wait_ge(done, (b + 1) * (KD if j == 0 else 1))
                        dve.wait_ge(rest_ready, b * 2)
                        dve.wait_ge(high, b * 2)
                        for m in range(KD):
                            ins = v.tensor_scalar(qk[:, j, m], ps[m][:], scale, None, ALU.mult)
                        ins.then_inc(taken, 1)
                        dve.wait_ge(taken, b * 2 + j + 1)
                        dve.wait_ge(high, b * 2 + j + 1)
                        dve.wait_ge(low, b * 2 + j)
                        v.tensor_tensor(rest[:, j], qk[:, j], parts[:, j, 0], ALU.subtract).then_inc(rest_ready, 1)
                        dve.wait_ge(mid, b * 2 + j + 1)
                        v.tensor_tensor(parts[:, j, 2], rest[:, j], parts[:, j, 1], ALU.subtract).then_inc(low, 1)
                    for g in range(2):
                        dve.wait_ge(v_done, b * 2 + g + 1)
                        v.tensor_copy(v_all[:, bass.ds(b * CPB + 2 * g, 2), :], psV[:]).then_inc(v_ready, 1)

                loop(dve, step)


def attend(nc, C, qp_d, kp_d, v_all, wo_d, res_d, out_d):
    U = 2 * CPB
    TURNS = AH // 2
    with Space(nc, "att") as s:
        wo = s.sb("wo", [P, KD, D])
        decay = s.sb("decay", [P, CPB, SEQ])
        dist_i = s.sb("dist_i", [P, CPB, SEQ], I32)
        dist = s.sb("dist", [P, CPB, SEQ])
        qs = s.sb("qs", [P, 2, AH, SEQ], BF16)
        ks = s.sb("ks", [P, 2, AH, SEQ], BF16)
        clipped = s.sb("clipped", [P, 2, SEQ])
        scores = s.sb("scores", [P, U, SEQ])
        top = s.sb("top", [P, 2, CPB])
        shift = s.sb("shift", [P, 2, CPB])
        prob = s.sb("prob", [P, U, SEQ])
        total = s.sb("total", [P, 2, CPB])
        inv = s.sb("inv", [P, 2, CPB])
        pT = s.sb("pT", [P, 2, CPB, P])
        heads = s.sb("heads", [P, CPB, D])
        hT = s.sb("hT", [P, KD, SEQ])
        res = s.sb("res", [P, CPB, D])
        out = s.sb("out", [P, CPB, D])
        psS = [s.psum(f"psS{j}", [P, SEQ]) for j in range(2)]
        psT = [s.psum(f"psT{j}", [P, CPB, P]) for j in range(2)]
        psO = [s.psum(f"psO{j}", [P, CPB, HW]) for j in range(2)]
        psE = s.psum("psE", [P, SEQ])
        wo_in = s.sem("wo_in")
        counted = s.sem("counted")
        chain0 = s.sem("chain0")
        dist_ready = s.sem("dist_ready")
        decay_ready = s.sem("decay_ready")
        stacked = [s.sem(f"stacked{j}") for j in range(2)]
        res_in = s.sem("res_in")
        scored = s.sem("scored")
        clip_done = s.sem("clip_done")
        decayed = s.sem("decayed")
        shift_ready = s.sem("shift_ready")
        exped = s.sem("exped")
        turned = s.sem("turned")
        pT_ready = s.sem("pT_ready")
        mixed = s.sem("mixed")
        inv_ready = s.sem("inv_ready")
        heads_ready = s.sem("heads_ready")
        h_turned = s.sem("h_turned")
        hT_ready = s.sem("hT_ready")
        out_done = s.sem("out_done")
        out_ready = s.sem("out_ready")
        out_stored = s.sem("out_stored")

        with nc.Block() as block:
            @block.sync
            def _(sp):
                sp.dma_start(wo[:], wo_d.rearrange("(k p) n -> p k n", p=P)).then_inc(wo_in, 16)
                for b in range(BATCH + 1):
                    if b < BATCH:
                        if b >= 2:
                            sp.wait_ge(scored, (b - 1) * AH * CPB)
                        for j, (qa, kb) in enumerate(PAIRS):
                            for dst, src, part in ((qs, qp_d, qa), (ks, kp_d, kb)):
                                sp.dma_start(dst[HW * j:HW * (j + 1), b % 2],
                                             src[b, part].rearrange("(h e) t -> e h t", e=HW)).then_inc(stacked[b % 2], 16)
                    if b:
                        sp.wait_ge(out_ready, b * CPB)
                        sp.dma_start(out_d[(b - 1) * SEQ:b * SEQ, :].rearrange("(c p) d -> p c d", p=P), out[:]).then_inc(out_stored, 16)
                    if b < BATCH:
                        sp.dma_start(res[:], res_d[b * SEQ:(b + 1) * SEQ, :].rearrange("(c p) d -> p c d", p=P)).then_inc(res_in, 16)
                sp.wait_ge(out_stored, BATCH * 16)

            @block.gpsimd
            def _(pool):
                for t in range(CPB):
                    nc.gpsimd.iota(dist_i[:, t], pattern=[[-1, SEQ]], base=t * P, channel_multiplier=1).then_inc(counted, 1)

            @block.tensor
            def _(pe):
                def score(n, b, slot, hp, u):
                    g, t = u // CPB, u % CPB
                    pe.wait_ge(clip_done, n * U + (u - 1 if u else 0))
                    if not isinstance(hp, int) or hp == 0:
                        pe.wait_ge(stacked[slot], (b - slot) * (len(PAIRS) * 16) + 2 * len(PAIRS) * 16)
                    nc.tensor.matmul(psS[u % 2][:], qs[:, slot, bass.ds(hp * 2 + g, 1), t * P:(t + 1) * P].rearrange("p a t -> p (a t)"),
                                     ks[:, slot, bass.ds(hp * 2 + g, 1), :].rearrange("p a t -> p (a t)"),
                                     start=True, stop=True).then_inc(scored, 1)

                def turn(n, u):
                    pe.wait_ge(exped, n * U + u + 1)
                    pe.wait_ge(pT_ready, n * U + (u - 1 if u else 0))
                    for q in range(CPB):
                        mm = nc.tensor.transpose(psT[u % 2][:, q], prob[:, u, q * P:(q + 1) * P], C.ident[:])
                    mm.then_inc(turned, 1)

                def mix(b, hp, n, u):
                    g, t = u // CPB, u % CPB
                    pe.wait_ge(pT_ready, n * U + u + 1)
                    if t == 0:
                        pe.wait_ge(heads_ready, n * 2)
                    for q in range(CPB):
                        mm = nc.tensor.matmul(psO[g][:, t], pT[:, u % 2, q],
                                              v_all[:, bass.ds(b * CPB + q, 1), bass.ds((hp * 2 + g) * HW, HW)].rearrange("p a e -> p (a e)"),
                                              start=(q == 0), stop=(q == CPB - 1))
                    mm.then_inc(mixed, 1)

                def pair(b, hp, ahead):
                    n = b * TURNS + hp
                    for u in range(U + 1):
                        if u < U:
                            if ahead:
                                score(n + 2, *ahead, u)
                            turn(n, u)
                        if u >= 1:
                            mix(b, hp, n, u - 1)

                def batch(b, slot, last=False):
                    with pe.Fori(0, TURNS - 2) as hp:
                        pair(b, hp, (b, slot, hp + 2))
                    pair(b, TURNS - 2, None if last else (b + 1, 1 - slot, 0))
                    pair(b, TURNS - 1, None if last else (b + 1, 1 - slot, 1))
                    pe.wait_ge(heads_ready, (b + 1) * AH)
                    for k in range(KD):
                        pe.wait_ge(hT_ready, b * KD + k)
                        pe.wait_ge(out_ready, b * CPB)
                        for t in range(CPB):
                            mm = nc.tensor.transpose(psE[:, t * P:(t + 1) * P], heads[:, t, k * P:(k + 1) * P], C.ident[:])
                        mm.then_inc(h_turned, 1)
                    pe.wait_ge(hT_ready, (b + 1) * KD)
                    for t in range(CPB):
                        pe.wait_ge(out_ready, b * CPB + t)
                        for k in range(KD):
                            mm = nc.tensor.matmul(psE[:, 0:D], hT[:, k, t * P:(t + 1) * P], wo[:, k],
                                                  start=(k == 0), stop=(k == KD - 1))
                        mm.then_inc(out_done, 1)

                pe.wait_ge(wo_in, 16)
                for hp in range(2):
                    for u in range(U):
                        score(hp, 0, 0, hp, u)
                with pe.Fori(0, BATCH // 2 - 1) as i:
                    batch(i * 2, 0)
                    batch(i * 2 + 1, 1)
                batch(BATCH - 2, 0)
                batch(BATCH - 1, 1, last=True)

            @block.scalar
            def _(act):
                def exp(n, u):
                    g, t = u // CPB, u % CPB
                    if t == 0:
                        if not isinstance(n, int) or n > 0:
                            act.wait_ge(inv_ready, (n - 1) * 2 + g + 1)
                        act.wait_ge(shift_ready, n * 2 + g + 1)
                    if not isinstance(n, int) or n > 0:
                        act.wait_ge(turned, (n - 1) * U + u + 1)
                    nc.scalar.activation(prob[:, u], scores[:, u], ACT.Exp, bias=shift[:, g, t:t + 1],
                                         accum_out=total[:, g, t:t + 1]).then_inc(exped, 1)

                def copy(n, u):
                    act.wait_ge(turned, n * U + u + 1)
                    act.wait_ge(mixed, n * U + (u - 1 if u else 0))
                    nc.scalar.copy(pT[:, u % 2], psT[u % 2][:]).then_inc(pT_ready, 1)

                def pair(n, ahead=True):
                    for u in range(U):
                        copy(n, u)
                        if ahead:
                            exp(n + 1, u)

                def project_out(b):
                    for k in range(KD):
                        act.wait_ge(h_turned, b * KD + k + 1)
                        act.wait_ge(out_done, b * CPB)
                        nc.scalar.copy(hT[:, k], psE[:]).then_inc(hT_ready, 1)

                act.wait_ge(dist_ready, 1)
                nc.scalar.activation(decay[:], dist[:], ACT.Exp, scale=-DECAY).then_inc(decay_ready, 1)
                for u in range(U):
                    exp(0, u)
                with act.Fori(0, BATCH - 1) as b:
                    with act.Fori(0, TURNS) as hp:
                        pair(b * TURNS + hp)
                    project_out(b)
                with act.Fori(0, TURNS - 1) as hp:
                    pair((BATCH - 1) * TURNS + hp)
                pair(BATCH * TURNS - 1, ahead=False)
                project_out(BATCH - 1)

            @block.vector
            def _(dve):
                v = nc.vector

                def clip(n, u):
                    dve.wait_ge(scored, n * U + u + 1)
                    dve.wait_ge(decayed, n * U + (u - 1 if u else 0))
                    v.tensor_scalar(clipped[:, u % 2], psS[u % 2][:], -CLAMP, CLAMP, ALU.max, ALU.min).then_inc(clip_done, 1)

                def before_fade(n, u):
                    dve.wait_ge(clip_done, n * U + u + 1)
                    if not isinstance(n, int) or n > 0:
                        dve.wait_ge(exped, (n - 1) * U + u + 1)

                def fade(n, u):
                    g, t = u // CPB, u % CPB
                    v.tensor_tensor_reduce(scores[:, u], clipped[:, u % 2], decay[:, t], 1.0, -2.0 * CLAMP,
                                           ALU.mult, ALU.max, top[:, g, t:t + 1]).then_inc(decayed, 1)

                def negate(n, g):
                    dve.wait_ge(decayed, n * U + (g + 1) * CPB)
                    v.tensor_scalar(shift[:, g], top[:, g], -1.0, None, ALU.mult).then_inc(shift_ready, 1)

                def soften(n, between):
                    clip(n, 0)
                    for u in range(1, U):
                        before_fade(n, u - 1)
                        clip(n, u)
                        fade(n, u - 1)
                        if u == CPB:
                            negate(n, 0)
                    before_fade(n, U - 1)
                    between()
                    fade(n, U - 1)
                    negate(n, 1)

                def spare():
                    v.tensor_copy(top[:, 1, 0:1], top[:, 1, 0:1])

                def reciprocals(n):
                    for g in range(2):
                        dve.wait_ge(exped, n * U + (g + 1) * CPB)
                        dve.wait_ge(heads_ready, n * 2)
                        v.reciprocal(inv[:, g], total[:, g]).then_inc(inv_ready, 1)

                def normalise_heads(b, hp, n):
                    for g in range(2):
                        dve.wait_ge(inv_ready, n * 2 + g + 1)
                        dve.wait_ge(mixed, n * U + (g + 1) * CPB)
                        if g == 0:
                            dve.wait_ge(h_turned, b * KD)
                        v.tensor_tensor(heads[:, :, bass.ds((hp * 2 + g) * HW, HW)], psO[g][:],
                                        inv[:, g].unsqueeze(2).to_broadcast([P, CPB, HW]), ALU.mult).then_inc(heads_ready, 1)

                def pair(b, hp, ahead=True):
                    n = b * TURNS + hp
                    reciprocals(n)
                    if ahead:
                        soften(n + 2, lambda: normalise_heads(b, hp, n))
                    else:
                        normalise_heads(b, hp, n)

                def results(b):
                    dve.wait_ge(res_in, (b + 1) * 16)
                    dve.wait_ge(out_stored, b * 16)
                    for t in range(CPB):
                        dve.wait_ge(out_done, b * CPB + t + 1)
                        v.tensor_tensor(out[:, t], psE[:, 0:D], res[:, t], ALU.add).then_inc(out_ready, 1)

                c0 = Chain(dve, chain0)
                dve.wait_ge(counted, CPB)
                c0.step(v.tensor_copy(scores[:, 0:CPB], dist_i[:]))
                v.scalar_tensor_tensor(out=dist[:], in0=scores[:, 0:CPB], scalar=-1.0, in1=scores[:, 0:CPB],
                                       op0=ALU.mult, op1=ALU.max).then_inc(dist_ready, 1)
                dve.wait_ge(decay_ready, 1)
                dve.wait_ge(dist_ready, 1)
                soften(0, spare)
                soften(1, spare)
                with dve.Fori(0, BATCH - 1) as b:
                    with dve.Fori(0, TURNS) as hp:
                        pair(b, hp)
                    results(b)
                with dve.Fori(0, TURNS - 2) as hp:
                    pair(BATCH - 1, hp)
                pair(BATCH - 1, TURNS - 2, ahead=False)
                pair(BATCH - 1, TURNS - 1, ahead=False)
                results(BATCH - 1)


def combine(nc, C, base_d, xn_all, got, weight, passed, out_d):
    with Space(nc, "end") as s:
        x = s.sb("x", [P, 2, CPB, D])
        x_in = [s.sem(f"x_in{b}") for b in range(2)]
        added = s.sem("added")
        stored = [s.sem(f"stored{b}") for b in range(2)]
        terms = [(got[0], weight[0]), (got[1], weight[1]), (xn_all, passed)]

        def rows(dram, b):
            return dram[b * SEQ:(b + 1) * SEQ, :].rearrange("(c p) d -> p c d", p=P)

        PER = CPB * len(terms)
        with nc.Block() as block:
            @block.sync
            def _(sp):
                for b in range(BATCH + 1):
                    if b < BATCH:
                        if b >= 2:
                            sp.wait_ge(stored[b % 2], (b // 2) * 16)
                        sp.dma_start(x[:, b % 2], rows(base_d, b)).then_inc(x_in[b % 2], 16)
                    if b:
                        sp.wait_ge(added, b * PER)
                        sp.dma_start(rows(out_d, b - 1), x[:, (b - 1) % 2]).then_inc(stored[(b - 1) % 2], 16)
                for b in range(2):
                    sp.wait_ge(stored[b], BATCH // 2 * 16)

            @block.vector
            def _(dve):
                with dve.Fori(0, BATCH // 2) as i:
                    for slot in range(2):
                        dve.wait_ge(x_in[slot], (i + 1) * 16)
                        for n, (rows_of, factor) in enumerate(terms):
                            for t in range(CPB):
                                at = (i * 2 + slot) * CPB + t
                                if n:
                                    dve.wait_ge(added, (i * 2 + slot) * PER + (n - 1) * CPB + t + 1)
                                nc.vector.scalar_tensor_tensor(
                                    out=x[:, slot, t], in0=rows_of[:, bass.ds(at, 1), :].rearrange("p a d -> p (a d)"),
                                    scalar=factor[:, bass.ds(at, 1)], in1=x[:, slot, t],
                                    op0=ALU.mult, op1=ALU.add).then_inc(added, 1)


def build(nc, a, out_d):

    def dram(name, shape, dt=F32):
        return nc.dram_tensor(name, shape, dt).ap()

    xnT0_d, xnT1_d = dram("xnT0", (D, TOK)), dram("xnT1", (D, TOK))
    mixed_d, x1_d, base_d = dram("mixed", (TOK, D)), dram("x1", (TOK, D)), dram("base", (TOK, D))
    xs0_d, ys0_d = dram("xs0", (L0_ROWS, D)), dram("ys0", (L0_ROWS, D))
    xs1_d, ys1_d = dram("xs1", (L1_ROWS, D)), dram("ys1", (L1_ROWS, D))
    qp_d, kp_d = (dram(n, (BATCH, 3, D, SEQ), BF16) for n in ("q_parts", "k_parts"))
    N2 = 2 * NH

    with ExitStack() as kept:
        def keep(where, name, shape, dt=F32):
            return where.enter_context(nc.sbuf_tensor(name, shape, dt))

        C = Constants()
        constants(nc, kept, C)
        choice0 = Choice()
        choice0.slot = [keep(kept, "slot0", [P, NT], I32)]
        choice0.gate = keep(kept, "gate0", [P, NT])
        choice0.tile_expert = keep(kept, "tile_expert", [P, L0_TILES], I32)
        with ExitStack() as mem:
            dt, step_a = keep(mem, "dt", [P, NT, N2]), keep(mem, "step_a", [P, NT, N2])
            with ExitStack() as mem0:
                logits = keep(mem0, "logits0", [P, NT, NE + N2])
                xn_all = keep(mem0, "xn_all0", [P, NT, D])
                normalise(nc, C, "norm0", a["u"], a["router_dt"], NE + N2, logits, xn_all, xnT0_d)
                route(nc, C, "route0", logits, a["br_bc"], xn_all, xs0_d, True, choice0)
                time_steps(nc, C, logits, a["dt_bias_bc"], a["a_log_bc"], dt, step_a)
            mamba(nc, C, xnT0_d, a["u"], a, dt, step_a, mixed_d)
        one_expert_each(nc, C, a["w1"], a["b1_bc"], a["w2"], a["b2_bc"], choice0.tile_expert, xs0_d, ys0_d)
        with ExitStack() as mem:
            logits = keep(mem, "logits1", [P, NT, NE])
            xn_all = keep(mem, "xn_all1", [P, NT, D])
            choice1 = Choice()
            choice1.slot = [keep(mem, f"slot1{k}", [P, NT], I32) for k in range(2)]
            choice1.weight = [keep(mem, f"weight1{k}", [P, NT]) for k in range(2)]
            choice1.passed = keep(mem, "passed", [P, NT])
            with ExitStack() as mem0:
                got = [keep(mem0, "got", [P, NT, D])]
                gather(nc, "gather0", ys0_d, choice0.slot, L0_ROWS, got)
                normalise(nc, C, "norm1", mixed_d, a["router1"], NE, logits, xn_all, xnT1_d,
                          merge=(got[0], choice0.gate, x1_d))
            route(nc, C, "route1", logits, a["br1_bc"], xn_all, xs1_d, False, choice1)
            full_experts(nc, C, a["inter"], a["outer"], xs1_d, ys1_d)
            got = [keep(mem, f"got1{k}", [P, NT, D]) for k in range(2)]
            gather(nc, "gather1", ys1_d, choice1.slot, L1_ROWS, got)
            combine(nc, C, x1_d, xn_all, got, choice1.weight, choice1.passed, base_d)
        v_all = keep(kept, "v_all", [P, NT, D])
        project(nc, C, xnT1_d, a, qp_d, kp_d, v_all)
        attend(nc, C, qp_d, kp_d, v_all, a["wo"], base_d, out_d)


def kernel(**inputs):
    import concourse.bacc as bacc
    import numpy as np
    from concourse.bass_utils import run_bass_kernel_spmd

    g = {n: np.asarray(x) for n, x in inputs.items()}

    def rows(x):
        return np.ascontiguousarray(np.broadcast_to(x.reshape(1, -1), (P, x.size)))

    def column(x):
        return np.ascontiguousarray(x.reshape(-1, P).T)

    in_T = np.ascontiguousarray(g["L0_attn_in_proj_w"].T)
    arrays = {
        "u": g["L0_attn_u"].reshape(TOK, D),
        "router_dt": np.ascontiguousarray(np.concatenate([g["L0_ffn_Wr"], in_T[:, DI + CONV:]], axis=1)),
        "in_T": in_T,
        "out_T": np.ascontiguousarray(g["L0_attn_out_proj_w"].T),
        "norm_col": column(g["L0_attn_norm_w"]),
        "fcd_T": np.ascontiguousarray(g["L0_attn_fc_D_w"].T),
        "taps": np.ascontiguousarray(g["L0_attn_conv_w"].reshape(CT, P, TAPS).transpose(1, 0, 2)),
        "conv_b": column(g["L0_attn_conv_b"]),
        "d_bc": rows(g["L0_attn_D"]),
        "d_col": column(np.repeat(g["L0_attn_D"], HD)),
        "dt_bias_bc": rows(np.concatenate([g["L0_attn_dt_bias"]] * 2)),
        "a_log_bc": rows(np.concatenate([g["L0_attn_A_log"]] * 2)),
        "br_bc": rows(g["L0_ffn_br"]),
        "w1": g["L0_ffn_W1"], "b1_bc": rows(g["L0_ffn_b1"]),
        "w2": g["L0_ffn_W2"], "b2_bc": rows(g["L0_ffn_b2"]),
        "wq": g["L1_attn_Wq"], "wk": g["L1_attn_Wk"], "wv": g["L1_attn_Wv"], "wo": g["L1_attn_Wo"],
        "wd": g["L1_attn_W_down_kv"], "wuk": g["L1_attn_W_up_k"], "wuv": g["L1_attn_W_up_v"],
        "router1": np.ascontiguousarray(g["L1_ffn_router_w"].T),
        "br1_bc": rows(g["L1_ffn_router_b"]),
        "inter": g["L1_ffn_experts_inter"], "outer": g["L1_ffn_experts_out"],
    }
    nc = bacc.Bacc("TRN2", target_bir_lowering=False, num_devices=1)
    a = {n: nc.dram_tensor(f"in_{n}", x.shape, mybir.dt.from_np(x.dtype), kind="ExternalInput").ap()
         for n, x in arrays.items()}
    out_d = nc.dram_tensor("out", (TOK, D), F32, kind="ExternalOutput").ap()
    build(nc, a, out_d)
    done = run_bass_kernel_spmd(nc, [{f"in_{n}": x for n, x in arrays.items()}], core_ids=[0])
    return done.results[0]["out"].reshape(BATCH, SEQ, D)
```

```python
from contextlib import ExitStack

import concourse.bass as bass
from concourse import mybir

F32 = mybir.dt.float32
I32 = mybir.dt.int32
BF16 = mybir.dt.bfloat16
ALU = mybir.AluOpType
ACT = mybir.ActivationFunctionType
AX_X = mybir.AxisListType.X

P = 128
D = 256
KD = D // P
BATCH, SEQ = 8, 512
TOK = BATCH * SEQ
NT = TOK // P
CPB = SEQ // P
EPS = 1e-5
LEAST_NORMAL = 2.0 ** -126

NE = 8
DFF = 1024
FT = DFF // P

DI = 512
DS = 128
NH = 8
HD = DI // NH
CONV = DI + 4 * DS
CT = CONV // P
TAPS = 4

L0_TILES = (TOK + NE * (P - 1)) // P

L0_ROWS = L0_TILES * P
L1_EXPERTS = NE - 1
CAP = TOK // NE
L1_ROWS = L1_EXPERTS * CAP

AH = 16
HW = D // AH
LAT = 64
CLAMP = 10000.0
DECAY = 0.01 * 0.01


class Space:

    def __init__(self, nc, name):
        self.nc, self.name = nc, name
        self.mem = ExitStack()
        self.sems = []

    def __enter__(self):
        return self

    def __exit__(self, failed, *a):
        self.mem.close()
        if failed is None:
            self.nc.clear_and_free_semaphores(self.sems)
            self.nc.all_engine_barrier()
        return False

    def sb(self, name, shape, dt=F32):
        return self.mem.enter_context(self.nc.sbuf_tensor(f"{self.name}_{name}", shape, dt))

    def psum(self, name, shape, dt=F32):
        return self.mem.enter_context(self.nc.psum_tensor(f"{self.name}_{name}", shape, dt))

    def sem(self, name):
        self.sems.append(self.nc.alloc_semaphore(name=f"{self.name}_{name}"))
        return self.sems[-1]


class Chain:

    def __init__(self, eng, sem, turn=0, per_turn=0, start=0):
        self.eng, self.sem, self.base, self.n, self.per_turn = eng, sem, turn * per_turn + start, 0, per_turn

    def link(self, ins):
        self.n += 1
        ins.then_inc(self.sem, 1)

    def wait(self):
        self.eng.wait_ge(self.sem, self.base + self.n)

    def step(self, ins):
        self.link(ins)
        self.wait()

    def end(self):
        assert self.n == self.per_turn, self.n


class Constants:
    pass


class Choice:
    pass


def constants(nc, kept, C):
    C.ident = kept.enter_context(nc.sbuf_tensor("ident", [P, P], F32))
    C.before = kept.enter_context(nc.sbuf_tensor("before", [P, P], F32))
    C.after = kept.enter_context(nc.sbuf_tensor("after", [P, P], F32))
    C.ones = kept.enter_context(nc.sbuf_tensor("ones", [P, P], F32))
    C.half = kept.enter_context(nc.sbuf_tensor("minus_half", [P, NT], F32))
    with Space(nc, "const") as s, nc.Block() as block:
        filled = s.sem("filled")

        @block.gpsimd
        def _(pool):
            nc.gpsimd.memset(C.ident[:], 0.0).then_inc(filled, 1)
            nc.gpsimd.memset(C.before[:], 1.0).then_inc(filled, 1)
            nc.gpsimd.memset(C.after[:], 1.0).then_inc(filled, 1)
            nc.gpsimd.memset(C.ones[:], 1.0)
            nc.gpsimd.memset(C.half[:], -0.5)
            pool.wait_ge(filled, 3)
            nc.gpsimd.affine_select(out=C.ident[:], in_=C.ident[:], compare_op=ALU.not_equal, fill=1.0,
                                    base=0, pattern=[[-1, P]], channel_multiplier=1)
            nc.gpsimd.affine_select(out=C.before[:], in_=C.before[:], compare_op=ALU.is_gt, fill=0.0,
                                    base=0, pattern=[[1, P]], channel_multiplier=-1)
            nc.gpsimd.affine_select(out=C.after[:], in_=C.after[:], compare_op=ALU.is_gt, fill=0.0,
                                    base=0, pattern=[[-1, P]], channel_multiplier=1)


def normalise(nc, C, name, x_d, w_d, width, logits, xn_all, xT_d, merge=None):
    G = 2
    TURNS = BATCH // G
    KEEPS = 2 if merge else 1
    with Space(nc, name) as s:
        x = s.sb("x", [P, G, CPB, D])
        xn = s.sb("xn", [P, G, CPB, D])
        xT = s.sb("xT", [P, G, KD, SEQ])
        w = s.sb("w", [P, KD, width])
        stats = s.sb("stats", [P, G, CPB, 6])
        mean = s.sb("mean", [P, G, CPB])
        diff = s.sb("diff", [P, G, CPB])
        spread = s.sb("spread", [P, G, CPB])
        var = s.sb("var", [P, G, CPB])
        rstd = s.sb("rstd", [P, G, CPB])
        psT = [s.psum(f"psT{g}{k}", [P, SEQ]) for g in range(G) for k in range(KD)]
        psL = [s.psum(f"psL{g}", [P, CPB, width]) for g in range(G)]
        w_in = s.sem("w_in")
        x_in = [s.sem(f"x_in{g}") for g in range(G)]
        x_out = [s.sem(f"x_out{g}") for g in range(G)]
        got = s.sb("got", [P, G, CPB, D]) if merge else None
        gathered = [s.sem(f"gathered{g}") for g in range(G)]
        merged = s.sem("merged")
        chain = s.sem("chain")
        var_ready = s.sem("var_ready")
        rstd_ready = s.sem("rstd_ready")
        xn_ready = s.sem("xn_ready")
        xn_kept = [s.sem(f"xn_kept{g}") for g in range(G)]
        turned = s.sem("turned")
        xT_ready = s.sem("xT_ready")
        xT_kept = [s.sem(f"xT_kept{g}") for g in range(G)]
        logits_ready = s.sem("logits_ready")
        logits_kept = s.sem("logits_kept")

        def rows(dram, i, g):
            return dram[bass.ds((i * G + g) * SEQ, SEQ), :].rearrange("(c p) d -> p c d", p=P)

        with nc.Block() as block:
            @block.sync
            def _(sp):
                sp.dma_start(w[:], w_d.rearrange("(k p) n -> p k n", p=P)).then_inc(w_in, 16)
                for i in range(TURNS):
                    for g in range(G):
                        if i:
                            sp.wait_ge(xn_ready, ((i - 1) * G + g + 1) * CPB)
                        if i and merge:
                            sp.wait_ge(x_out[g], i * 16)
                        sp.dma_start(x[:, g], rows(x_d, i, g)).then_inc(x_in[g], 16)
                    for g in range(G):
                        if merge:
                            sp.wait_ge(merged, (i * G + g + 1) * CPB)
                            sp.dma_start(rows(merge[4], i, g), x[:, g]).then_inc(x_out[g], 16)
                        sp.wait_ge(xn_ready, (i * G + g + 1) * CPB)
                        sp.dma_start(xn_all[:, bass.ds((i * G + g) * CPB, CPB), :], xn[:, g]).then_inc(xn_kept[g], 16)
                        if merge:
                            sp.dma_start(rows(merge[5], i, g), xn[:, g]).then_inc(xn_kept[g], 16)
                        sp.wait_ge(xT_ready, (i * G + g + 1) * KD)
                        sp.dma_start(xT_d[:, bass.ds((i * G + g) * SEQ, SEQ)].rearrange("(k p) t -> p k t", p=P),
                                     xT[:, g]).then_inc(xT_kept[g], 16)
                for g in range(G):
                    if merge:
                        sp.wait_ge(x_out[g], TURNS * 16)
                    sp.wait_ge(xn_kept[g], TURNS * KEEPS * 16)
                    sp.wait_ge(xT_kept[g], TURNS * 16)

            @block.vector
            def _(dve):
                n_links = CPB + 5
                with dve.Fori(0, TURNS) as i:
                    c = Chain(dve, chain, i, G * n_links)
                    for g in range(G):
                        dve.wait_ge(x_in[g], (i + 1) * 16)
                        if merge:
                            dve.wait_ge(gathered[g], (i + 1) * CPB * 16)
                            for t in range(CPB):
                                at = (i * G + g) * CPB + t
                                nc.vector.scalar_tensor_tensor(
                                    out=x[:, g, t], in0=got[:, g, t],
                                    scalar=merge[3][:, bass.ds(at, 1)], in1=x[:, g, t],
                                    op0=ALU.mult, op1=ALU.add).then_inc(merged, 1)
                            dve.wait_ge(merged, (i * G + g + 1) * CPB)
                        for t in range(CPB):
                            c.link(nc.vector.bn_stats(stats[:, g, t], x[:, g, t]))
                        c.wait()
                        even, odd = stats[:, g, :, 1], stats[:, g, :, 4]
                        c.link(nc.vector.tensor_tensor(mean[:, g], even, odd, ALU.add))
                        c.link(nc.vector.tensor_tensor(diff[:, g], even, odd, ALU.subtract))
                        c.link(nc.vector.scalar_tensor_tensor(
                            out=spread[:, g], in0=stats[:, g, :, 2], scalar=D * EPS, in1=stats[:, g, :, 5],
                            op0=ALU.add, op1=ALU.add))
                        c.wait()
                        c.link(nc.vector.tensor_scalar(mean[:, g], mean[:, g], 0.5, None, ALU.mult))
                        c.link(nc.vector.scalar_tensor_tensor(
                            out=diff[:, g], in0=diff[:, g], scalar=0.25, in1=diff[:, g], op0=ALU.mult, op1=ALU.mult))
                        c.wait()
                        nc.vector.scalar_tensor_tensor(
                            out=var[:, g], in0=spread[:, g], scalar=1.0 / D, in1=diff[:, g],
                            op0=ALU.mult, op1=ALU.add).then_inc(var_ready, 1)
                        dve.wait_ge(rstd_ready, i * G + g + 1)
                        dve.wait_ge(xn_kept[g], i * KEEPS * 16)
                        dve.wait_ge(turned, i * G * KD)
                        for t in range(CPB):
                            nc.vector.tensor_scalar(xn[:, g, t], x[:, g, t], mean[:, g, t:t + 1], rstd[:, g, t:t + 1],
                                                    ALU.subtract, ALU.mult).then_inc(xn_ready, 1)
                    for g in range(G):
                        dve.wait_ge(logits_ready, i * G + g + 1)
                        nc.vector.tensor_copy(logits[:, bass.ds((i * G + g) * CPB, CPB), :], psL[g][:]).then_inc(logits_kept, 1)
                    c.end()
                dve.wait_ge(logits_kept, BATCH)

            @block.gpsimd
            def _(pool):
                def gather(i, g):
                    if i:
                        pool.wait_ge(merged, ((i - 1) * G + g + 1) * CPB)
                        pool.wait_ge(gathered[g], i * CPB * 16)
                    for t in range(CPB):
                        at = (i * G + g) * CPB + t
                        nc.gpsimd.indirect_dma_start(
                            out=got[:, g, t, :], out_offset=None, in_=merge[0],
                            in_offset=bass.IndirectOffsetOnAxis(ap=merge[1][:, at:at + 1], axis=0),
                            bounds_check=merge[2] - 1, oob_is_err=True).then_inc(gathered[g], 16)

                def roots(i, g):
                    pool.wait_ge(xn_ready, i * G * CPB)
                    pool.wait_ge(var_ready, i * G + g + 1)
                    nc.gpsimd.tensor_tensor(rstd[:, g], var[:, g], C.half[:, 0:CPB], ALU.pow).then_inc(rstd_ready, 1)

                if merge:
                    for g in range(G):
                        gather(0, g)
                    for i in range(TURNS):
                        for g in range(G):
                            roots(i, g)
                            if i + 1 < TURNS:
                                gather(i + 1, g)
                else:
                    with pool.Fori(0, TURNS) as i:
                        for g in range(G):
                            roots(i, g)

            @block.tensor
            def _(pe):
                pe.wait_ge(w_in, 16)
                with pe.Fori(0, TURNS) as i:
                    for g in range(G):
                        pe.wait_ge(xn_ready, (i * G + g + 1) * CPB)
                        pe.wait_ge(xT_ready, i * G * KD)
                        for k in range(KD):
                            for t in range(CPB):
                                mm = nc.tensor.transpose(psT[g * KD + k][:, t * P:(t + 1) * P],
                                                         xn[:, g, t, k * P:(k + 1) * P], C.ident[:])
                            mm.then_inc(turned, 1)
                    for g in range(G):
                        pe.wait_ge(xT_ready, (i * G + g + 1) * KD)
                        pe.wait_ge(logits_kept, i * G)
                        for t in range(CPB):
                            for k in range(KD):
                                mm = nc.tensor.matmul(psL[g][:, t], xT[:, g, k, t * P:(t + 1) * P], w[:, k],
                                                      start=(k == 0), stop=(k == KD - 1))
                        mm.then_inc(logits_ready, 1)

            @block.scalar
            def _(act):
                with act.Fori(0, TURNS) as i:
                    for g in range(G):
                        act.wait_ge(xT_kept[g], i * 16)
                        act.wait_ge(logits_ready, i * G)
                        for k in range(KD):
                            act.wait_ge(turned, (i * G + g) * KD + k + 1)
                            nc.scalar.copy(xT[:, g, k], psT[g * KD + k][:]).then_inc(xT_ready, 1)


class Scatter:

    def __init__(self, xn_all, slots, xs_d, rows, all_placed):
        self.xn_all, self.slots, self.xs_d, self.rows, self.all_placed = xn_all, slots, xs_d, rows, all_placed

    def start(self, nc, scattered):
        for t in range(NT):
            for slot in self.slots:
                nc.gpsimd.indirect_dma_start(
                    out=self.xs_d, out_offset=bass.IndirectOffsetOnAxis(ap=slot[:, t:t + 1], axis=0),
                    in_=self.xn_all[:, t, :], in_offset=None,
                    bounds_check=self.rows - 1, oob_is_err=self.all_placed).then_inc(scattered, 16)

    def finish(self, pool, scattered):
        pool.wait_ge(scattered, NT * len(self.slots) * 16)


def route(nc, C, name, logits, bias_bc, xn_all, xs_d, first_layer, out):
    rows = L0_ROWS if first_layer else L1_ROWS
    picks = 1 if first_layer else 2
    per_p = rows // P * D
    ZW = per_p // 4
    with Space(nc, name) as s:
        zeros = s.sb("zeros", [P, ZW])
        lb = s.sb("lb", [P, NT, NE])
        red = s.sb("red", [P, NT])
        total = s.sb("total", [P, NT])
        prob = s.sb("prob", [P, NT, NE])
        weight_i = s.sb("order_i", [P, NE], I32)
        order = s.sb("order", [P, NE])
        rowbase_i = s.sb("rowbase_i", [P, NE], I32)
        rowbase = s.sb("rowbase", [P, NE])
        tile_i = s.sb("tile_i", [P, L0_TILES], I32)
        tiles = s.sb("tiles", [P, L0_TILES])
        tmp = s.sb("tmp", [P, NT, NE])
        tmp2 = s.sb("tmp2", [P, NT, NE])
        hot = [s.sb(f"hot{k}", [P, NT, NE]) for k in range(picks)]
        mask = s.sb("mask", [P, NT, NE])
        best = [s.sb(f"best{k}", [P, NT]) for k in range(picks)]
        some = s.sb("some", [P, NT])
        rank = s.sb("rank", [P, NT, NE])
        per_tile = s.sb("per_tile", [P, NT, NE])
        upto = s.sb("upto", [P, NT, NE])
        over = s.sb("over", [P, NE, NT])
        n_tiles = s.sb("n_tiles", [P, NE])
        end_tile = s.sb("end_tile", [P, NE])
        start_row = s.sb("start_row", [P, NE])
        by_tile = s.sb("by_tile", [P, L0_TILES, NE])
        tile_expert = s.sb("tile_expert", [P, L0_TILES])
        slot = s.sb("slot", [P, NT])
        ps_rank = s.psum("ps_rank", [P, NT, NE])
        ps_tile = s.psum("ps_tile", [P, NT, NE])
        bias_in = s.sem("bias_in")
        bias = s.sb("bias", [P, NE])
        zeroed = s.sem("zeroed")
        filled = [s.sem(f"filled{q}") for q in range(4)]
        counted = s.sem("counted")
        shifted = s.sem("shifted")
        exped = s.sem("exped")
        chosen = s.sem("chosen")
        ranked = s.sem("ranked")
        chain = s.sem("chain")
        placed = s.sem("placed")
        xs_flat = xs_d.rearrange("(p r) d -> p (r d)", p=P)

        with nc.Block() as block:
            @block.sync
            def _(sp):
                sp.dma_start(bias[:], bias_bc).then_inc(bias_in, 16)
                sp.wait_ge(zeroed, 1)
                for q in range(4):
                    sp.dma_start(xs_flat[:, q * ZW:(q + 1) * ZW], zeros[:]).then_inc(filled[q], 16)
                for q in range(4):
                    sp.wait_ge(filled[q], 16)

            @block.gpsimd
            def _(pool):
                nc.gpsimd.memset(zeros[:], 0.0).then_inc(zeroed, 1)
                nc.gpsimd.iota(weight_i[:], pattern=[[-1, NE]], base=NE, channel_multiplier=0).then_inc(counted, 1)
                nc.gpsimd.iota(rowbase_i[:], pattern=[[CAP, NE]], base=-L1_ROWS, channel_multiplier=0).then_inc(counted, 1)
                nc.gpsimd.iota(tile_i[:], pattern=[[1, L0_TILES]], base=0, channel_multiplier=0).then_inc(counted, 1)

            @block.scalar
            def _(act):
                act.wait_ge(shifted, 1)
                nc.scalar.activation(prob[:], lb[:], ACT.Exp).then_inc(exped, 1)

            @block.tensor
            def _(pe):
                pe.wait_ge(chosen, 1)
                nc.tensor.matmul(ps_rank[:], C.before[:], mask[:], start=True, stop=True)
                nc.tensor.matmul(ps_tile[:], C.ones[:], mask[:], start=True, stop=True).then_inc(ranked, 1)

            @block.vector
            def _(dve):
                c = Chain(dve, chain)
                v = nc.vector

                def wide(ap):
                    return ap.unsqueeze(2).to_broadcast([P, NT, NE])

                def per_expert(ap):
                    return ap.unsqueeze(1).to_broadcast([P, NT, NE])

                dve.wait_ge(bias_in, 16)
                dve.wait_ge(counted, 3)
                c.step(v.tensor_copy(order[:], weight_i[:]))
                c.step(v.tensor_copy(rowbase[:], rowbase_i[:]))
                c.step(v.tensor_copy(tiles[:], tile_i[:]))
                c.step(v.tensor_tensor(lb[:], logits[:, :, 0:NE], per_expert(bias[:]), ALU.add))
                c.step(v.tensor_reduce(red[:], lb[:], AX_X, ALU.max))
                v.tensor_tensor(lb[:], lb[:], wide(red[:]), ALU.subtract).then_inc(shifted, 1)
                dve.wait_ge(exped, 1)
                c.step(v.tensor_reduce(total[:], prob[:], AX_X, ALU.add))
                c.step(v.reciprocal(total[:], total[:]))
                c.step(v.tensor_tensor(prob[:], prob[:], wide(total[:]), ALU.mult))
                for k in range(picks):
                    c.step(v.tensor_reduce(best[k][:], prob[:], AX_X, ALU.max))
                    c.step(v.tensor_tensor(tmp[:], prob[:], wide(best[k][:]), ALU.is_equal))
                    c.step(v.tensor_tensor(tmp[:], tmp[:], per_expert(order[:]), ALU.mult))
                    c.step(v.tensor_reduce(red[:], tmp[:], AX_X, ALU.max))
                    c.step(v.tensor_tensor(hot[k][:], tmp[:], wide(red[:]), ALU.is_equal))
                    if k + 1 < picks:
                        c.step(v.scalar_tensor_tensor(out=prob[:], in0=hot[k][:], scalar=-2.0, in1=prob[:],
                                                      op0=ALU.mult, op1=ALU.add))
                if first_layer:
                    v.tensor_copy(mask[:], hot[0][:]).then_inc(chosen, 1)
                    c.step(v.tensor_copy(out.gate[:], best[0][:]))
                else:
                    for k in range(picks):
                        c.step(v.tensor_scalar(some[:], best[k][:], LEAST_NORMAL, None, ALU.is_ge))
                        c.step(v.tensor_tensor(hot[k][:], hot[k][:], wide(some[:]), ALU.mult))
                    v.tensor_tensor(mask[:], hot[0][:], hot[1][:], ALU.add).then_inc(chosen, 1)
                dve.wait_ge(ranked, 1)
                c.step(v.tensor_copy(per_tile[:], ps_tile[:]))
                for e in range(NE):
                    c.link(v.tensor_tensor_scan(upto[:, :, e], C.ones[:, 0:NT], per_tile[:, :, e], 0.0, ALU.mult, ALU.add))
                c.wait()
                c.step(v.tensor_tensor(tmp[:], upto[:], per_tile[:], ALU.subtract))
                c.step(v.tensor_tensor(rank[:], ps_rank[:], tmp[:], ALU.add))
                if first_layer:
                    c.step(v.tensor_scalar(per_tile[:, :, 0], tiles[:, 0:NT], float(P), None, ALU.mult))
                    c.step(v.tensor_tensor(over[:], upto[:, NT - 1, :].unsqueeze(2).to_broadcast([P, NE, NT]),
                                           per_tile[:, :, 0].unsqueeze(1).to_broadcast([P, NE, NT]), ALU.is_gt))
                    c.step(v.tensor_reduce(n_tiles[:], over[:], AX_X, ALU.add))
                    c.step(v.tensor_tensor_scan(end_tile[:], C.ones[:, 0:NE], n_tiles[:], 0.0, ALU.mult, ALU.add))
                    c.step(v.tensor_tensor(start_row[:], end_tile[:], n_tiles[:], ALU.subtract))
                    c.step(v.tensor_scalar(start_row[:], start_row[:], float(P), None, ALU.mult))
                    c.step(v.tensor_tensor(rank[:], rank[:], per_expert(start_row[:]), ALU.add))
                    c.step(v.tensor_tensor(by_tile[:], tiles[:].unsqueeze(2).to_broadcast([P, L0_TILES, NE]),
                                           end_tile[:].unsqueeze(1).to_broadcast([P, L0_TILES, NE]), ALU.is_ge))
                    c.step(v.tensor_reduce(tile_expert[:], by_tile[:], AX_X, ALU.add))
                    c.step(v.tensor_scalar(tile_expert[:], tile_expert[:], float(NE - 1), None, ALU.min))
                    c.step(v.tensor_copy(out.tile_expert[:], tile_expert[:]))
                    c.step(v.tensor_tensor(tmp[:], hot[0][:], rank[:], ALU.mult))
                    c.step(v.tensor_reduce(slot[:], tmp[:], AX_X, ALU.add))
                    v.tensor_copy(out.slot[0][:], slot[:]).then_inc(placed, 1)
                else:
                    c.step(v.tensor_tensor(tmp2[:, :, 0], hot[0][:, :, NE - 1], best[0][:], ALU.mult))
                    c.step(v.tensor_tensor(tmp2[:, :, 1], hot[1][:, :, NE - 1], best[1][:], ALU.mult))
                    c.step(v.tensor_tensor(out.passed[:], tmp2[:, :, 0], tmp2[:, :, 1], ALU.add))
                    c.step(v.tensor_scalar(mask[:], rank[:], float(CAP), None, ALU.is_lt))
                    c.step(v.memset(mask[:, :, NE - 1], 0.0))
                    c.step(v.tensor_tensor(rank[:], rank[:], per_expert(rowbase[:]), ALU.add))
                    for k in range(picks):
                        c.step(v.tensor_tensor(hot[k][:], hot[k][:], mask[:], ALU.mult))
                        c.step(v.tensor_reduce(some[:], hot[k][:], AX_X, ALU.add))
                        c.step(v.tensor_tensor(out.weight[k][:], some[:], best[k][:], ALU.mult))
                        c.step(v.tensor_tensor(tmp[:], hot[k][:], rank[:], ALU.mult))
                        c.step(v.tensor_reduce(slot[:], tmp[:], AX_X, ALU.add))
                        c.step(v.tensor_scalar(slot[:], slot[:], float(L1_ROWS), None, ALU.add))
                        v.tensor_copy(out.slot[k][:], slot[:]).then_inc(placed, 1)
                        dve.wait_ge(placed, k + 1)
    return Scatter(xn_all, out.slot, xs_d, rows, first_layer)


def time_steps(nc, C, logits, dt_bias_bc, a_log_bc, dt, a):
    N2 = 2 * NH
    with Space(nc, "steps") as s:
        bias = s.sb("bias", [P, N2])
        neg_a = s.sb("neg_a", [P, N2])
        raw = s.sb("raw", [P, NT, N2])
        mag = s.sb("mag", [P, NT, N2])
        u = s.sb("u", [P, NT, N2])
        w = s.sb("w", [P, NT, N2])
        d = s.sb("d", [P, NT, N2])
        flat = s.sb("flat", [P, NT, N2])
        lw = s.sb("lw", [P, NT, N2])
        loaded = s.sem("loaded")
        mag_ready = s.sem("mag_ready")
        exped = s.sem("exped")
        w_ready = s.sem("w_ready")
        logged = s.sem("logged")
        chain = s.sem("chain")
        with nc.Block() as block:
            @block.sync
            def _(sp):
                sp.dma_start(bias[:], dt_bias_bc).then_inc(loaded, 16)
                sp.dma_start(neg_a[:], a_log_bc).then_inc(loaded, 16)

            @block.scalar
            def _(act):
                act.wait_ge(loaded, 32)
                nc.scalar.activation(neg_a[:], neg_a[:], ACT.Exp).then_inc(exped, 1)
                act.wait_ge(mag_ready, 1)
                nc.scalar.activation(u[:], mag[:], ACT.Exp, scale=-1.0).then_inc(exped, 1)
                act.wait_ge(w_ready, 1)
                nc.scalar.activation(lw[:], w[:], ACT.Ln).then_inc(logged, 1)

            @block.vector
            def _(dve):
                c = Chain(dve, chain)
                v = nc.vector
                dve.wait_ge(loaded, 32)
                c.step(v.tensor_tensor(raw[:], logits[:, :, NE:NE + N2],
                                       bias[:].unsqueeze(1).to_broadcast([P, NT, N2]), ALU.add))
                v.scalar_tensor_tensor(out=mag[:], in0=raw[:], scalar=-1.0, in1=raw[:],
                                       op0=ALU.mult, op1=ALU.max).then_inc(mag_ready, 1)
                dve.wait_ge(exped, 2)
                v.tensor_scalar(w[:], u[:], 1.0, None, ALU.add).then_inc(w_ready, 1)
                dve.wait_ge(w_ready, 1)
                c.step(v.tensor_scalar(d[:], w[:], -1.0, None, ALU.add))
                c.step(v.tensor_scalar(flat[:], d[:], 0.0, None, ALU.is_equal))
                c.step(v.tensor_tensor(d[:], d[:], flat[:], ALU.add))
                c.step(v.reciprocal(d[:], d[:]))
                c.step(v.tensor_tensor(d[:], d[:], u[:], ALU.mult))
                dve.wait_ge(logged, 1)
                c.step(v.tensor_tensor(d[:], d[:], lw[:], ALU.mult))
                c.step(v.tensor_tensor(flat[:], flat[:], u[:], ALU.mult))
                c.step(v.tensor_tensor(d[:], d[:], flat[:], ALU.add))
                c.step(v.scalar_tensor_tensor(out=dt[:], in0=raw[:], scalar=0.0, in1=d[:], op0=ALU.max, op1=ALU.add))
                c.step(v.scalar_tensor_tensor(out=a[:], in0=dt[:], scalar=-1.0,
                                              in1=neg_a[:].unsqueeze(1).to_broadcast([P, NT, N2]),
                                              op0=ALU.mult, op1=ALU.mult))


def mamba(nc, C, xT_d, x_d, w, dt, a, out_d, scatter):
    Z_AT = 0
    BT_AT = Z_AT + CPB
    XT_AT = BT_AT + 2
    TAIL_AT = XT_AT + CPB
    USES = TAIL_AT + 2 * CPB
    ORDER = [4, 5, 6, 7, 0, 1, 2, 3]
    XW = SEQ + 2
    U = 2 * CPB
    NA = 4

    with Space(nc, "mamba") as s:
        w_in = s.sb("w_in", [P, KD, DI + CONV])
        w_out = s.sb("w_out", [P, DI // P, D])
        norm_w = s.sb("norm_w", [P, DI // P])
        w_fcd = s.sb("w_fcd", [P, DI // P, NH])
        taps = s.sb("taps", [P, CT, TAPS])
        conv_b = s.sb("conv_b", [P, CT])
        d_bc = s.sb("d_bc", [P, NH])
        d_col = s.sb("d_col", [P, DI // P])
        d_diag = s.sb("d_diag", [P, DI // P, P])
        xT = s.sb("xT", [P, KD, SEQ])
        acc = s.sb("acc", [P, 4, SEQ])
        xc = s.sb("xc", [P, CT, XW])
        near = s.sb("near", [P, DI // P, SEQ])
        zs = s.sb("zs", [P, CPB, DI])
        Bl = s.sb("Bl", [P, 2, CPB, DS])
        xl = s.sb("xl", [P, CPB, DI])
        ab = s.sb("ab", [P, 2, CPB, NH])
        dtb = s.sb("dtb", [P, 2, CPB, NH])
        fac = s.sb("fac", [P, 3, 2, CPB, NH])
        dtdec = s.sb("dtdec", [P, 2, CPB, NH])
        fd = s.sb("fd", [P, CPB, NH])
        xdd = s.sb("xdd", [P, 2, DI])
        state = s.sb("state", [P, 2, CPB, DI])
        scaled = s.sb("scaled", [P, 2, DI])
        am = s.sb("am", [P, NA, NH, P])
        L = s.sb("L", [P, 2, NH, P])
        Gm = s.sb("Gm", [P, 2, P])
        xdt = s.sb("xdt", [P, 2, DI])
        xfd = s.sb("xfd", [P, 2, DI])
        yo = s.sb("yo", [P, 2, DI])
        y = s.sb("y", [P, 2, DI])
        sq = s.sb("sq", [P, DI])
        ssum = s.sb("ssum", [P, CPB])
        var = s.sb("var", [P, CPB])
        rstd = s.sb("rstd", [P, CPB])
        yT = s.sb("yT", [P, 2, DI // P, P])
        x = s.sb("x", [P, CPB, D])
        o = s.sb("o", [P, CPB, D])
        psA = [s.psum(f"psA{j}", [P, 512]) for j in range(2)]
        psS = [s.psum(f"psS{j}", [P, 4, P]) for j in range(2)]
        psG = s.psum("psG", [P, 512])
        psY = s.psum("psY", [P, DI])
        psO = [s.psum(f"psO{d}", [P, DI]) for d in range(2)]
        psC = [ps[:].rearrange("p a b -> p (a b)") for ps in psS] + [ps[:] for ps in psA]
        gT = psG[:, 0:2 * P].rearrange("p (d t) -> p d t", d=2)
        sums = psG[:, 256:448]
        fd_ps = psG[:, 448:480].rearrange("p (c h) -> p c h", c=CPB)
        tri = [C.before, C.after]

        weights_in = s.sem("weights_in")
        xT_in = s.sem("xT_in")
        x_in = s.sem("x_in")
        out_stored = s.sem("out_stored")
        padded = s.sem("padded")
        diag_ready = s.sem("diag_ready")
        wout_ready = s.sem("wout_ready")
        bank_ready = s.sem("bank_ready")
        conv_made = s.sem("conv_made")
        tap0 = s.sem("tap0")
        conv_done = s.sem("conv_done")
        xc_ready = s.sem("xc_ready")
        z_ready = s.sem("z_ready")
        tok_ready = s.sem("tok_ready")
        ab_ready = s.sem("ab_ready")
        sums_ready = s.sem("sums_ready")
        fac_ready = s.sem("fac_ready")
        dtdec_ready = s.sem("dtdec_ready")
        fd_done = s.sem("fd_done")
        fd_ready = s.sem("fd_ready")
        near_ready = s.sem("near_ready")
        xdd_ready = s.sem("xdd_ready")
        grown = s.sem("grown")
        state_ready = s.sem("state_ready")
        am_ready = s.sem("am_ready")
        seg_ready = s.sem("seg_ready")
        seg_exped = s.sem("seg_exped")
        g_ready = s.sem("g_ready")
        gm_ready = s.sem("gm_ready")
        L_ready = s.sem("L_ready")
        xdt_ready = s.sem("xdt_ready")
        diag_used = s.sem("diag_used")
        off_ready = s.sem("off_ready")
        off_scaled = s.sem("off_scaled")
        xfd_ready = s.sem("xfd_ready")
        y_read = s.sem("y_read")
        summed = s.sem("summed")
        gated = s.sem("gated")
        squared = s.sem("squared")
        var_ready = s.sem("var_ready")
        rstd_ready = s.sem("rstd_ready")
        yT_ready = s.sem("yT_ready")
        o_ready = s.sem("o_ready")
        chain = s.sem("chain")
        scattered = s.sem("scattered")

        def drained(eng, i, use):
            last = use - 2
            if last < BT_AT:
                eng.wait_ge(conv_done, (i + 1) * CT)
            elif last < TAIL_AT:
                eng.wait_ge(tok_ready, i * (2 + CPB) + last - BT_AT + 1)
            elif (last - TAIL_AT) % 2 == 0:
                eng.wait_ge(yT_ready, i * CPB + (last - TAIL_AT) // 2 + 1)
            else:
                eng.wait_ge(o_ready, i * CPB + (last - TAIL_AT) // 2 + 1)

        def heads(ap):
            return ap.unsqueeze(2).to_broadcast([P, NH, HD])

        def by_head(ap):
            return ap.rearrange("p (h e) -> p h e", h=NH)

        with nc.Block() as block:
            @block.sync
            def _(sp):
                sp.dma_start(w_in[:], w["in_T"].rearrange("(k p) n -> p k n", p=P)[:, :, 0:DI + CONV]).then_inc(weights_in, 16)
                sp.dma_start(w_out[:], w["out_T"].rearrange("(k p) n -> p k n", p=P)).then_inc(weights_in, 16)
                sp.dma_start(norm_w[:], w["norm_col"]).then_inc(weights_in, 16)
                sp.dma_start(w_fcd[:], w["fcd_T"].rearrange("(k p) n -> p k n", p=P)).then_inc(weights_in, 16)
                sp.dma_start(taps[:], w["taps"]).then_inc(weights_in, 16)
                sp.dma_start(conv_b[:], w["conv_b"]).then_inc(weights_in, 16)
                sp.dma_start(d_bc[:], w["d_bc"]).then_inc(weights_in, 16)
                sp.dma_start(d_col[:], w["d_col"]).then_inc(weights_in, 16)
                for i in range(BATCH):
                    if i:
                        sp.wait_ge(bank_ready, (i - 1) * USES + BT_AT)
                    sp.dma_start(xT[:], xT_d[:, i * SEQ:(i + 1) * SEQ].rearrange("(k p) t -> p k t", p=P)).then_inc(xT_in, 16)
                    if i:
                        sp.wait_ge(o_ready, i * CPB)
                        sp.dma_start(out_d[(i - 1) * SEQ:i * SEQ, :].rearrange("(c p) d -> p c d", p=P), o[:]).then_inc(out_stored, 16)
                    sp.dma_start(x[:], x_d[i * SEQ:(i + 1) * SEQ, :].rearrange("(c p) d -> p c d", p=P)).then_inc(x_in, 16)
                sp.wait_ge(o_ready, BATCH * CPB)
                sp.dma_start(out_d[(BATCH - 1) * SEQ:BATCH * SEQ, :].rearrange("(c p) d -> p c d", p=P), o[:]).then_inc(out_stored, 16)
                sp.wait_ge(out_stored, BATCH * 16)

            @block.tensor
            def _(pe):
                pe.wait_ge(weights_in, 8 * 16)
                pe.wait_ge(padded, 1)
                pe.wait_ge(diag_ready, DI // P)
                pe.wait_ge(wout_ready, DI // P)

                def conv(i, n):
                    m = ORDER[n]
                    if n == 0:
                        pe.wait_ge(xT_in, (i + 1) * 16)
                    if n < 2:
                        pe.wait_ge(seg_exped, i * U * 2)
                    elif n < 4:
                        pe.wait_ge(yT_ready, i * CPB)
                        pe.wait_ge(o_ready, i * CPB)
                    else:
                        pe.wait_ge(conv_done, i * CT + n - 3)
                    for k in range(KD):
                        mm = nc.tensor.matmul(psC[n % 4], w_in[:, k, DI + m * P:DI + (m + 1) * P], xT[:, k],
                                              start=(k == 0), stop=(k == KD - 1))
                    mm.then_inc(conv_made, 1)

                def turn(i, ahead):
                    for n in range(2, CT):
                        conv(i, n)
                    for t in range(CPB):
                        if t < 2:
                            pe.wait_ge(off_scaled, i * 6)
                        else:
                            pe.wait_ge(z_ready, i * CPB + t - 1)
                        for k in range(KD):
                            mm = nc.tensor.matmul(psO[t % 2][:], xT[:, k, t * P:(t + 1) * P], w_in[:, k, 0:DI],
                                                  start=(k == 0), stop=(k == KD - 1))
                        mm.then_inc(bank_ready, 1)
                    pe.wait_ge(ab_ready, i + 1)
                    pe.wait_ge(gm_ready, i * CPB)
                    for q in range(3):
                        for d in range(2):
                            lhs = C.ones if q == 2 else tri[d] if q == 0 else tri[1 - d]
                            at = (q * 2 + d) * CPB * NH
                            mm = nc.tensor.matmul(sums[:, at:at + CPB * NH], lhs[:], ab[:, d], start=True, stop=True)
                    mm.then_inc(sums_ready, 1)
                    pe.wait_ge(xc_ready, i * CT + 4)
                    for d in range(2):
                        use = BT_AT + d
                        drained(pe, i, use)
                        for t in range(CPB):
                            mm = nc.tensor.transpose(psA[use % 2][:, t * P:(t + 1) * P],
                                                     xc[:, 4 + 2 * d, 1 + t * P:1 + (t + 1) * P], C.ident[:])
                        mm.then_inc(bank_ready, 1)
                    pe.wait_ge(xc_ready, (i + 1) * CT)
                    for t in range(CPB):
                        use = XT_AT + t
                        drained(pe, i, use)
                        for m in range(DI // P):
                            mm = nc.tensor.transpose(psA[use % 2][:, m * P:(m + 1) * P],
                                                     xc[:, m, 1 + t * P:1 + (t + 1) * P], C.ident[:])
                        mm.then_inc(bank_ready, 1)
                    pe.wait_ge(fac_ready, i + 1)
                    for t in range(CPB):
                        for m in range(DI // P):
                            mm = nc.tensor.matmul(fd_ps[:, t], xc[:, m, 1 + t * P:1 + (t + 1) * P], w_fcd[:, m],
                                                  start=(m == 0), stop=(m == DI // P - 1))
                    mm.then_inc(fd_done, 1)

                    def grow(k):
                        for d in range(2):
                            n = 2 * k + d
                            t = k if d == 0 else CPB - 1 - k
                            pe.wait_ge(xdd_ready, i * 6 + n + 1)
                            if n >= 2:
                                pe.wait_ge(state_ready, i * 6 + n - 1)
                            else:
                                pe.wait_ge(z_ready, (i + 1) * CPB)
                            nc.tensor.matmul(psO[d][:], Bl[:, d, t], xdd[:, d], start=True, stop=True).then_inc(grown, 1)

                    def segment(u):
                        t, d = u // 2, u % 2
                        if d == 0:
                            pe.wait_ge(fd_ready, i + 1)
                            pe.wait_ge(gm_ready, i * CPB + t)
                            for e in range(2):
                                lo = t * P + (0 if e == 0 else 2)
                                mm = nc.tensor.matmul(gT[:, e], xc[:, 4 + 2 * e, 1 + t * P:1 + (t + 1) * P],
                                                      xc[:, 5 + 2 * e, lo:lo + P], start=True, stop=True)
                            mm.then_inc(g_ready, 1)
                        pe.wait_ge(am_ready, i * U + u + 1)
                        pe.wait_ge(seg_exped, (i * U + u) * 2)
                        for hf in range(2):
                            nc.tensor.matmul(psS[hf][:], tri[1 - d][:], am[:, u % NA, 4 * hf:4 * hf + 4],
                                             start=True, stop=True).then_inc(seg_ready, 1)

                    def diagonal(u):
                        t, d = u // 2, u % 2
                        if d == 0:
                            pe.wait_ge(y_read, i * CPB + t)
                            pe.wait_ge(near_ready, i + 1)
                            for m in range(DI // P):
                                nc.tensor.matmul(psY[:, m * P:(m + 1) * P], near[:, m, t * P:(t + 1) * P], d_diag[:, m],
                                                 start=(m == 0), stop=False, skip_group_check=True)
                        pe.wait_ge(L_ready, i * U + u + 1)
                        pe.wait_ge(xdt_ready, i * U + u + 1)
                        for h in range(NH):
                            mm = nc.tensor.matmul(psY[:, h * HD:(h + 1) * HD], L[:, u % 2, h], xdt[:, u % 2, h * HD:(h + 1) * HD],
                                                  start=False, stop=(d == 1), skip_group_check=True)
                        mm.then_inc(diag_used, 1)
                        if (d == 0 and t > 0) or (d == 1 and t < CPB - 1):
                            pe.wait_ge(state_ready, (i + 1) * 6)
                            done = [2 * (t - 1) if t > 1 else 0, 2 * t][d]
                            pe.wait_ge(off_scaled, i * 6 + done)
                            lo = t * P + (0 if d == 0 else 2)
                            nc.tensor.matmul(psO[d][:], xc[:, 5 + 2 * d, lo:lo + P], state[:, d, t],
                                             start=True, stop=True).then_inc(off_ready, 1)

                    def tail(t):
                        use = TAIL_AT + 2 * t
                        drained(pe, i, use)
                        pe.wait_ge(gated, i * CPB + t + 1)
                        for m in range(DI // P):
                            mm = nc.tensor.transpose(psA[use % 2][:, m * P:(m + 1) * P], y[:, t % 2, m * P:(m + 1) * P], C.ident[:])
                        mm.then_inc(bank_ready, 1)
                        drained(pe, i, use + 1)
                        pe.wait_ge(yT_ready, i * CPB + t + 1)
                        for m in range(DI // P):
                            mm = nc.tensor.matmul(psA[(use + 1) % 2][:, 0:D], yT[:, t % 2, m], w_out[:, m],
                                                  start=(m == 0), stop=(m == DI // P - 1))
                        mm.then_inc(bank_ready, 1)

                    segment(0)
                    grow(0)
                    segment(1)
                    grow(1)
                    grow(2)
                    diagonal(0)
                    for u in range(2, U + 1):
                        if u < U:
                            segment(u)
                        diagonal(u - 1)
                        if u >= 4 and u % 2 == 0:
                            tail(u // 2 - 2)
                    if ahead:
                        conv(i + 1, 0)
                        conv(i + 1, 1)
                    tail(CPB - 1)

                for n in range(2):
                    conv(0, n)
                with pe.Fori(0, BATCH - 1) as b:
                    turn(b, True)
                turn(BATCH - 1, False)

            @block.scalar
            def _(act):
                act.wait_ge(weights_in, 8 * 16)
                with act.Fori(0, BATCH) as i:
                    def silu(n):
                        act.wait_ge(conv_done, i * CT + n + 1)
                        if n == 0:
                            act.wait_ge(diag_used, i * U)
                            act.wait_ge(off_ready, i * 6)
                            act.wait_ge(near_ready, i)
                        nc.scalar.activation(xc[:, ORDER[n], 1:1 + SEQ], acc[:, n % 4], ACT.Silu).then_inc(xc_ready, 1)

                    for n in range(CT):
                        m = ORDER[n]
                        act.wait_ge(conv_made, i * CT + n + 1)
                        if n >= 4:
                            act.wait_ge(xc_ready, i * CT + n - 3)
                        else:
                            act.wait_ge(xc_ready, i * CT)
                        nc.scalar.activation(acc[:, n % 4], psC[n % 4], ACT.Identity, bias=conv_b[:, m:m + 1],
                                             scale=taps[:, m, TAPS - 1:TAPS]).then_inc(tap0, 1)
                        if n % 2 == 1 and n >= 3:
                            silu(n - 3)
                            silu(n - 2)
                    for t in range(CPB):
                        if t == 2:
                            silu(CT - 2)
                            silu(CT - 1)
                        act.wait_ge(bank_ready, i * USES + Z_AT + t + 1)
                        if t == 0:
                            act.wait_ge(gated, i * CPB)
                        nc.scalar.activation(zs[:, t], psO[t % 2][:], ACT.Silu).then_inc(z_ready, 1)
                    act.wait_ge(sums_ready, i + 1)
                    act.wait_ge(off_scaled, i * 6)
                    nc.scalar.activation(fac[:].rearrange("p a b c h -> p (a b c h)"), sums, ACT.Exp).then_inc(fac_ready, 1)
                    for d in range(2):
                        act.wait_ge(bank_ready, i * USES + BT_AT + d + 1)
                        act.wait_ge(grown, i * 6)
                        nc.scalar.copy(Bl[:, d], psA[(BT_AT + d) % 2][:].rearrange("p (t n) -> p t n", t=CPB)).then_inc(tok_ready, 1)
                    for t in range(CPB):
                        act.wait_ge(bank_ready, i * USES + XT_AT + t + 1)
                        act.wait_ge(xdt_ready, i * U)
                        act.wait_ge(xfd_ready, i * CPB)
                        nc.scalar.copy(xl[:, t], psA[(XT_AT + t) % 2][:]).then_inc(tok_ready, 1)

                    def tail(t):
                        act.wait_ge(gated, i * CPB + t + 1)
                        if t == 0:
                            act.wait_ge(rstd_ready, i * CPB)
                        act.wait_ge(squared, i * CPB + t)
                        nc.scalar.activation(sq[:], y[:, t % 2], ACT.Square, accum_out=ssum[:, t:t + 1]).then_inc(squared, 1)
                        act.wait_ge(squared, i * CPB + t + 1)
                        nc.scalar.activation(var[:, t:t + 1], ssum[:, t:t + 1], ACT.Copy, bias=EPS, scale=1.0 / DI).then_inc(var_ready, 1)
                        act.wait_ge(bank_ready, i * USES + TAIL_AT + 2 * t + 1)
                        if t >= 2:
                            act.wait_ge(bank_ready, i * USES + TAIL_AT + 2 * (t - 2) + 2)
                        else:
                            act.wait_ge(bank_ready, i * USES)
                        nc.scalar.copy(yT[:, t % 2], psA[(TAIL_AT + 2 * t) % 2][:].rearrange("p (m t) -> p m t", m=DI // P)).then_inc(yT_ready, 1)

                    for u in range(U):
                        if u >= 2:
                            act.wait_ge(diag_used, i * U + u - 1)
                        else:
                            act.wait_ge(diag_used, i * U)
                        for hf in range(2):
                            act.wait_ge(seg_ready, (i * U + u) * 2 + hf + 1)
                            nc.scalar.activation(L[:, u % 2, 4 * hf:4 * hf + 4], psS[hf][:], ACT.Exp).then_inc(seg_exped, 1)
                        if u >= 4 and u % 2 == 0:
                            tail(u // 2 - 2)
                    tail(CPB - 2)
                    tail(CPB - 1)

            @block.gpsimd
            def _(pool):
                nc.gpsimd.memset(xc[:, :, 0:1], 0.0)
                nc.gpsimd.memset(xc[:, :, XW - 1:XW], 0.0).then_inc(padded, 1)
                scatter.start(nc, scattered)
                with pool.Fori(0, BATCH) as i:
                    def masked_a(u):
                        t, d = u // 2, u % 2
                        if u == 0:
                            pool.wait_ge(ab_ready, i + 1)
                        if u >= NA:
                            pool.wait_ge(seg_ready, (i * U + u + 1 - NA) * 2)
                        else:
                            pool.wait_ge(seg_ready, i * U * 2)
                        nc.gpsimd.tensor_tensor(am[:, u % NA], tri[d][:].unsqueeze(1).to_broadcast([P, NH, P]),
                                                ab[:, d, t].unsqueeze(2).to_broadcast([P, NH, P]), ALU.mult).then_inc(am_ready, 1)

                    def rms(t):
                        pool.wait_ge(var_ready, i * CPB + t + 1)
                        nc.gpsimd.tensor_tensor(rstd[:, t:t + 1], var[:, t:t + 1], C.half[:, 0:1], ALU.pow).then_inc(rstd_ready, 1)

                    for u in range(NA):
                        masked_a(u)
                    pool.wait_ge(dtdec_ready, i + 1)
                    pool.wait_ge(tok_ready, (i + 1) * (2 + CPB))
                    for k in range(CPB - 1):
                        for d in range(2):
                            n = 2 * k + d
                            t = k if d == 0 else CPB - 1 - k
                            if n >= 2:
                                pool.wait_ge(grown, i * 6 + n - 1)
                            else:
                                pool.wait_ge(grown, i * 6)
                            nc.gpsimd.tensor_tensor(by_head(xdd[:, d]), by_head(xl[:, t]), heads(dtdec[:, d, t]), ALU.mult).then_inc(xdd_ready, 1)
                    for u in range(U):
                        t, d = u // 2, u % 2
                        if u >= 2:
                            pool.wait_ge(diag_used, i * U + u - 1)
                        else:
                            pool.wait_ge(diag_used, i * U)
                        nc.gpsimd.tensor_tensor(by_head(xdt[:, u % 2]), by_head(xl[:, t]), heads(dtb[:, d, t]), ALU.mult).then_inc(xdt_ready, 1)
                        if d == 0:
                            if t == 0:
                                pool.wait_ge(fd_ready, i + 1)
                            pool.wait_ge(y_read, i * CPB + max(t - 1, 0))
                            nc.gpsimd.tensor_tensor(by_head(xfd[:, t % 2]), by_head(xl[:, t]), heads(fd[:, t]), ALU.mult).then_inc(xfd_ready, 1)
                        if u + NA < U:
                            masked_a(u + NA)
                        if u >= 5 and d == 1:
                            rms((u - 5) // 2)
                    rms(CPB - 2)
                    rms(CPB - 1)
                scatter.finish(pool, scattered)

            @block.vector
            def _(dve):
                v = nc.vector
                dve.wait_ge(weights_in, 8 * 16)
                for m in range(DI // P):
                    v.tensor_scalar(d_diag[:, m], C.ident[:], d_col[:, m:m + 1], None, ALU.mult).then_inc(diag_ready, 1)
                    v.tensor_scalar(w_out[:, m], w_out[:, m], norm_w[:, m:m + 1], None, ALU.mult).then_inc(wout_ready, 1)
                LINKS = CT * 2 + 2 * (CPB - 2) + CPB - 2
                with dve.Fori(0, BATCH) as i:
                    c = Chain(dve, chain, i, LINKS)
                    dve.wait_ge(am_ready, i * U)
                    dve.wait_ge(xdt_ready, i * U)
                    for d in range(2):
                        v.tensor_copy(dtb[:, d], dt[:, bass.ds(i * CPB, CPB), d * NH:(d + 1) * NH])
                        cp = v.tensor_copy(ab[:, d], a[:, bass.ds(i * CPB, CPB), d * NH:(d + 1) * NH])
                    cp.then_inc(ab_ready, 1)
                    for n in range(0, CT, 2):
                        dve.wait_ge(tap0, i * CT + n + 2)
                        for j in range(1, TAPS):
                            for q in (n, n + 1):
                                ins = v.scalar_tensor_tensor(
                                    out=acc[:, q % 4, j:SEQ], in0=psC[q % 4][:, 0:SEQ - j],
                                    scalar=taps[:, ORDER[q], TAPS - 1 - j:TAPS - j], in1=acc[:, q % 4, j:SEQ],
                                    op0=ALU.mult, op1=ALU.add)
                                if j < TAPS - 1:
                                    c.link(ins)
                                else:
                                    ins.then_inc(conv_done, 1)
                            if j < TAPS - 1:
                                c.wait()
                    dve.wait_ge(ab_ready, i + 1)
                    dve.wait_ge(fac_ready, i + 1)
                    dve.wait_ge(xdd_ready, i * 6)
                    v.tensor_tensor(dtdec[:], dtb[:], fac[:, 1], ALU.mult).then_inc(dtdec_ready, 1)
                    dve.wait_ge(xc_ready, (i + 1) * CT)
                    dve.wait_ge(diag_used, i * U)
                    v.tensor_tensor(near[:], xc[:, 0:DI // P, 0:SEQ], xc[:, 0:DI // P, 2:2 + SEQ], ALU.add).then_inc(near_ready, 1)
                    dve.wait_ge(fd_done, i + 1)
                    dve.wait_ge(xfd_ready, i * CPB)
                    v.tensor_tensor(fd[:], fd_ps, d_bc[:].unsqueeze(1).to_broadcast([P, CPB, NH]), ALU.add).then_inc(fd_ready, 1)
                    def grow(k):
                        for d in range(2):
                            n = 2 * k + d
                            t = k if d == 0 else CPB - 1 - k
                            to = t + 1 if d == 0 else t - 1
                            if n == 0:
                                dve.wait_ge(off_ready, i * 6)
                            if k:
                                dve.wait_ge(state_ready, i * 6 + n - 1)
                                c.step(v.tensor_tensor(by_head(scaled[:, d]), by_head(state[:, d, t]), heads(fac[:, 2, d, t]), ALU.mult))
                            dve.wait_ge(grown, i * 6 + n + 1)
                            if k:
                                v.tensor_tensor(state[:, d, to], scaled[:, d], psO[d][:], ALU.add).then_inc(state_ready, 1)
                            else:
                                v.tensor_copy(state[:, d, to], psO[d][:]).then_inc(state_ready, 1)

                    def decays(u):
                        t, d = u // 2, u % 2
                        if d == 0:
                            dve.wait_ge(g_ready, i * CPB + t + 1)
                            dve.wait_ge(L_ready, i * U + u)
                            for e in range(2):
                                ins = v.tensor_tensor(Gm[:, e], gT[:, e], tri[e][:], ALU.mult)
                            ins.then_inc(gm_ready, 1)
                            dve.wait_ge(gm_ready, i * CPB + t + 1)
                        dve.wait_ge(seg_exped, (i * U + u + 1) * 2)
                        v.tensor_tensor(L[:, u % 2], L[:, u % 2], Gm[:, d].unsqueeze(1).to_broadcast([P, NH, P]), ALU.mult).then_inc(L_ready, 1)

                    def off(u, count):
                        t, d = u // 2, u % 2
                        if (d == 0 and t > 0) or (d == 1 and t < CPB - 1):
                            dve.wait_ge(off_ready, i * 6 + count + 1)
                            dve.wait_ge(summed, i * CPB + t)
                            v.tensor_tensor(by_head(yo[:, d]), by_head(psO[d][:]), heads(fac[:, 0, d, t]), ALU.mult).then_inc(off_scaled, 1)
                            return count + 1
                        return count

                    def finish(t):
                        b = t % 2
                        dve.wait_ge(diag_used, i * U + 2 * t + 2)
                        dve.wait_ge(xfd_ready, i * CPB + t + 1)
                        if t >= 2:
                            dve.wait_ge(bank_ready, i * USES + TAIL_AT + 2 * (t - 2) + 1)
                            dve.wait_ge(squared, i * CPB + t - 1)
                        else:
                            dve.wait_ge(bank_ready, i * USES)
                            dve.wait_ge(squared, i * CPB)
                        v.tensor_tensor(y[:, b], psY[:], xfd[:, b], ALU.add).then_inc(y_read, 1)
                        dve.wait_ge(y_read, i * CPB + t + 1)
                        dve.wait_ge(off_scaled, i * 6 + [1, 3, 5, 6][t])
                        if 0 < t < CPB - 1:
                            c.step(v.tensor_tensor(yo[:, 0], yo[:, 0], yo[:, 1], ALU.add))
                        v.tensor_tensor(y[:, b], y[:, b], yo[:, 1 if t == 0 else 0], ALU.add).then_inc(summed, 1)
                        dve.wait_ge(summed, i * CPB + t + 1)
                        v.tensor_tensor(y[:, b], y[:, b], zs[:, t], ALU.mult).then_inc(gated, 1)

                    def outputs(t):
                        dve.wait_ge(bank_ready, i * USES + TAIL_AT + 2 * t + 2)
                        dve.wait_ge(rstd_ready, i * CPB + t + 1)
                        if t == 0:
                            dve.wait_ge(x_in, (i + 1) * 16)
                            dve.wait_ge(out_stored, i * 16)
                        v.scalar_tensor_tensor(out=o[:, t], in0=psA[(TAIL_AT + 1) % 2][:, 0:D], scalar=rstd[:, t:t + 1],
                                               in1=x[:, t], op0=ALU.mult, op1=ALU.add).then_inc(o_ready, 1)

                    grow(0)
                    decays(0)
                    grow(1)
                    decays(1)
                    grow(2)
                    count = 0
                    for u in range(1, U + 1):
                        if 1 < u < U:
                            decays(u)
                        if u >= 1:
                            count = off(u - 1, count)
                        if u >= 2 and u % 2 == 0:
                            finish(u // 2 - 1)
                        if u >= 5 and u % 2 == 1:
                            outputs((u - 5) // 2)
                    outputs(CPB - 2)
                    outputs(CPB - 1)
                    c.end()


def one_expert_each(nc, C, w1_d, b1_bc, w2_d, b2_bc, tile_expert, xs_d, ys_d):
    N = L0_TILES
    W1N, W2N = KD * DFF, FT * D
    HALF = 512
    LAG = 3
    with Space(nc, "ffn0") as s:
        w1 = s.sb("w1", [P, NE * W1N])
        w2 = s.sb("w2", [P, NE * W2N])
        b1 = s.sb("b1", [P, NE * DFF])
        b2 = s.sb("b2", [P, NE * D])
        xs = s.sb("xs", [P, 2, D])
        xT = s.sb("xT", [P, 2, KD, P])
        h = s.sb("h", [P, 2, DFF])
        hT = s.sb("hT", [P, 2, FT, P])
        y = s.sb("y", [P, 2, D])
        psX = s.psum("psX", [P, KD, P])
        psH = [s.psum(f"psH{j}", [P, HALF]) for j in range(4)]
        psT = [s.psum(f"psT{j}", [P, 4, P]) for j in range(2)]
        psY = s.psum("psY", [P, D])
        loaded = [s.sem(f"loaded{e}") for e in range(NE)]
        marked = s.sb("marked", [P, NE])
        experts_in = s.sem("experts_in")
        xs_in = [s.sem(f"xs_in{b}") for b in range(2)]
        x_turned = s.sem("x_turned")
        xT_ready = s.sem("xT_ready")
        up_done = s.sem("up_done")
        h_ready = s.sem("h_ready")
        h_turned = s.sem("h_turned")
        hT_ready = s.sem("hT_ready")
        down_done = s.sem("down_done")
        y_ready = s.sem("y_ready")
        y_stored = [s.sem(f"y_stored{b}") for b in range(2)]

        def pairs(eng, first, last, step):
            n = (last - first) // 2
            with eng.Fori(0, n) as i:
                step(i * 2 + first, first % 2)
                step(i * 2 + first + 1, (first + 1) % 2)
            for j in range(first + 2 * n, last):
                step(j, j % 2)

        with nc.Block() as block:
            @block.sync
            def _(sp):
                for j in range(N + LAG):
                    if j < N:
                        if j >= 2:
                            sp.wait_ge(x_turned, j - 1)
                        sp.dma_start(xs[:, j % 2], xs_d[j * P:(j + 1) * P, :]).then_inc(xs_in[j % 2], 16)
                    done = j - LAG
                    if done >= 0:
                        sp.wait_ge(y_ready, done + 1)
                        sp.dma_start(ys_d[done * P:(done + 1) * P, :], y[:, done % 2]).then_inc(y_stored[done % 2], 16)
                sp.wait_ge(y_stored[0], (N + 1) // 2 * 16)
                sp.wait_ge(y_stored[1], N // 2 * 16)

            @block.gpsimd
            def _(pool):
                def load(e):
                    pool.dma_start(w1[:, e * W1N:(e + 1) * W1N].rearrange("p (k n) -> p k n", k=KD),
                                   w1_d[e].rearrange("(k p) n -> p k n", p=P)).then_inc(loaded[e], 16)
                    pool.dma_start(b1[:, e * DFF:(e + 1) * DFF], b1_bc[:, e * DFF:(e + 1) * DFF]).then_inc(loaded[e], 16)
                    pool.dma_start(w2[:, e * W2N:(e + 1) * W2N].rearrange("p (k n) -> p k n", k=FT),
                                   w2_d[e].rearrange("(k p) n -> p k n", p=P)).then_inc(loaded[e], 16)
                    pool.dma_start(b2[:, e * D:(e + 1) * D], b2_bc[:, e * D:(e + 1) * D]).then_inc(loaded[e], 16)

                load(0)
                for e in range(NE):
                    pool.wait_ge(loaded[e], 4 * 16)
                    if e + 1 < NE:
                        load(e + 1)
                    nc.gpsimd.memset(marked[:, e:e + 1], 0.0).then_inc(experts_in, 1)

            @block.tensor
            def _(pe):
                def turn_x(j, b):
                    pe.wait_ge(xs_in[b], ((j - b) // 2 + 1) * 16 if isinstance(j, int) else (j - b) * 8 + 16)
                    pe.wait_ge(xT_ready, j)
                    for k in range(KD):
                        mm = nc.tensor.transpose(psX[:, k], xs[:, b, k * P:(k + 1) * P], C.ident[:])
                    mm.then_inc(x_turned, 1)

                def up(j, b):
                    at = nc.tensor.value_load(tile_expert[0:1, bass.ds(j, 1)], min_val=0, max_val=NE - 1)
                    pe.wait_ge(experts_in, at + 1)
                    pe.wait_ge(xT_ready, j + 1)
                    if not isinstance(j, int) or j >= 2:
                        pe.wait_ge(h_ready, (j - 1) * 2)
                    for hf in range(2):
                        for k in range(KD):
                            mm = nc.tensor.matmul(psH[2 * b + hf][:], xT[:, b, k],
                                                  w1[:, bass.ds(at * W1N + (k * DFF + hf * HALF), HALF)],
                                                  start=(k == 0), stop=(k == KD - 1))
                        mm.then_inc(up_done, 1)

                def turn_h(j, b):
                    for hf in range(2):
                        pe.wait_ge(h_ready, j * 2 + hf + 1)
                        pe.wait_ge(hT_ready, j * 2)
                        for q in range(4):
                            mm = nc.tensor.transpose(psT[hf][:, q], h[:, b, hf * HALF + q * P:hf * HALF + (q + 1) * P], C.ident[:])
                        mm.then_inc(h_turned, 1)

                def down(j, b):
                    at = nc.tensor.value_load(tile_expert[0:1, bass.ds(j, 1)], min_val=0, max_val=NE - 1)
                    pe.wait_ge(hT_ready, j * 2 + 2)
                    pe.wait_ge(y_ready, j)
                    for f in range(FT):
                        mm = nc.tensor.matmul(psY[:], hT[:, b, f], w2[:, bass.ds(at * W2N + f * D, D)],
                                              start=(f == 0), stop=(f == FT - 1))
                    mm.then_inc(down_done, 1)

                turn_x(0, 0)
                turn_x(1, 1)
                up(0, 0)
                up(1, 1)
                turn_h(0, 0)

                def step(j, b):
                    turn_x(j + 1, 1 - b)
                    up(j + 1, 1 - b)
                    turn_h(j, b)
                    down(j - 1, 1 - b)

                pairs(pe, 1, N - 1, step)
                turn_h(N - 1, (N - 1) % 2)
                down(N - 2, N % 2)
                down(N - 1, (N - 1) % 2)

            @block.scalar
            def _(act):
                def x_out(j, b):
                    act.wait_ge(x_turned, j + 1)
                    if not isinstance(j, int) or j >= 2:
                        act.wait_ge(up_done, (j - 1) * 2)
                    nc.scalar.copy(xT[:, b], psX[:]).then_inc(xT_ready, 1)

                def relu(j, b):
                    if not isinstance(j, int) or j >= 2:
                        act.wait_ge(down_done, j - 1)
                    for hf in range(2):
                        act.wait_ge(h_turned, j * 2 + hf + 1)
                        nc.scalar.activation(hT[:, b, 4 * hf:4 * hf + 4], psT[hf][:], ACT.Relu).then_inc(hT_ready, 1)

                x_out(0, 0)
                x_out(1, 1)
                relu(0, 0)

                def step(j, b):
                    x_out(j + 1, 1 - b)
                    relu(j, b)

                pairs(act, 1, N - 1, step)
                relu(N - 1, (N - 1) % 2)

            @block.vector
            def _(dve):
                v = nc.vector

                def hidden(j, b):
                    at = v.value_load(tile_expert[0:1, bass.ds(j, 1)], min_val=0, max_val=NE - 1)
                    if not isinstance(j, int) or j >= 2:
                        dve.wait_ge(h_turned, (j - 1) * 2)
                    for hf in range(2):
                        dve.wait_ge(up_done, j * 2 + hf + 1)
                        v.tensor_tensor(h[:, b, hf * HALF:(hf + 1) * HALF], psH[2 * b + hf][:],
                                        b1[:, bass.ds(at * DFF + hf * HALF, HALF)], ALU.add).then_inc(h_ready, 1)

                def result(j, b):
                    at = v.value_load(tile_expert[0:1, bass.ds(j, 1)], min_val=0, max_val=NE - 1)
                    dve.wait_ge(down_done, j + 1)
                    if not isinstance(j, int) or j >= 2:
                        dve.wait_ge(y_stored[b], (j - b) * 8)
                    v.tensor_tensor(y[:, b], psY[:], b2[:, bass.ds(at * D, D)], ALU.add).then_inc(y_ready, 1)

                hidden(0, 0)
                hidden(1, 1)

                def step(j, b):
                    hidden(j + 1, 1 - b)
                    result(j - 1, 1 - b)

                pairs(dve, 1, N - 1, step)
                result(N - 2, N % 2)
                result(N - 1, (N - 1) % 2)


def full_experts(nc, C, w1_d, w2_d, xs_d, ys_d):
    RT = CAP // P
    with Space(nc, "ffn1") as s:
        w1 = s.sb("w1", [P, 2, KD, DFF])
        w2 = s.sb("w2", [P, 2, FT, D])
        xs = s.sb("xs", [P, 2, RT, D])
        xT = s.sb("xT", [P, 2, KD, CAP])
        hT = s.sb("hT", [P, FT, CAP])
        y = s.sb("y", [P, RT, D])
        psX = [s.psum(f"psX{k}", [P, CAP]) for k in range(KD)]
        psH = [s.psum(f"psH{j}", [P, CAP]) for j in range(4)]
        psY = [s.psum(f"psY{j}", [P, D]) for j in range(2)]
        w_in = [s.sem(f"w_in{b}") for b in range(2)]
        xs_in = [s.sem(f"xs_in{b}") for b in range(2)]
        x_turned = s.sem("x_turned")
        xT_ready = s.sem("xT_ready")
        up_done = s.sem("up_done")
        hT_ready = s.sem("hT_ready")
        down_done = s.sem("down_done")
        y_ready = s.sem("y_ready")
        y_stored = s.sem("y_stored")
        N = L1_EXPERTS

        def all_experts(eng, step):
            with eng.Fori(0, N // 2) as i:
                step(i * 2, 0)
                step(i * 2 + 1, 1)
            step(N - 1, 0)

        with nc.Block() as block:
            @block.sync
            def _(sp):
                for e in range(N):
                    b = e % 2
                    if e >= 2:
                        sp.wait_ge(down_done, (e - 1) * RT)
                    sp.dma_start(xs[:, b], xs_d[e * CAP:(e + 1) * CAP, :].rearrange("(t p) d -> p t d", p=P)).then_inc(xs_in[b], 16)
                    sp.dma_start(w1[:, b], w1_d[e].rearrange("(k p) n -> p k n", p=P)).then_inc(w_in[b], 16)
                    sp.dma_start(w2[:, b], w2_d[e].rearrange("(k p) n -> p k n", p=P)).then_inc(w_in[b], 16)

            @block.tensor
            def _(pe):
                def step(e, b):
                    turn = (e - b) * 8 + 16
                    pe.wait_ge(xs_in[b], turn)
                    for k in range(KD):
                        pe.wait_ge(xT_ready, e * KD)
                        for t in range(RT):
                            mm = nc.tensor.transpose(psX[k][:, t * P:(t + 1) * P], xs[:, b, t, k * P:(k + 1) * P], C.ident[:])
                        mm.then_inc(x_turned, 1)
                    pe.wait_ge(w_in[b], turn * 2)
                    pe.wait_ge(xT_ready, (e + 1) * KD)
                    for f in range(FT):
                        pe.wait_ge(hT_ready, e * FT + max(f - 3, 0))
                        for k in range(KD):
                            mm = nc.tensor.matmul(psH[f % 4][:], w1[:, b, k, f * P:(f + 1) * P], xT[:, b, k],
                                                  start=(k == 0), stop=(k == KD - 1))
                        mm.then_inc(up_done, 1)
                    for t in range(RT):
                        pe.wait_ge(hT_ready, (e + 1) * FT)
                        pe.wait_ge(y_ready, e * RT + max(t - 1, 0))
                        for f in range(FT):
                            mm = nc.tensor.matmul(psY[t % 2][:], hT[:, f, t * P:(t + 1) * P], w2[:, b, f],
                                                  start=(f == 0), stop=(f == FT - 1))
                        mm.then_inc(down_done, 1)

                all_experts(pe, step)

            @block.scalar
            def _(act):
                def step(e, b):
                    for k in range(KD):
                        act.wait_ge(x_turned, e * KD + k + 1)
                        act.wait_ge(up_done, e * FT)
                        nc.scalar.copy(xT[:, b, k], psX[k][:]).then_inc(xT_ready, 1)
                    for f in range(FT):
                        act.wait_ge(up_done, e * FT + f + 1)
                        act.wait_ge(down_done, e * RT)
                        nc.scalar.activation(hT[:, f], psH[f % 4][:], ACT.Relu).then_inc(hT_ready, 1)

                all_experts(act, step)

            @block.vector
            def _(dve):
                def step(e, b):
                    for t in range(RT):
                        dve.wait_ge(down_done, e * RT + t + 1)
                        if t == 0:
                            dve.wait_ge(y_stored, e * 16)
                        nc.vector.tensor_copy(y[:, t], psY[t % 2][:]).then_inc(y_ready, 1)

                all_experts(dve, step)

            @block.gpsimd
            def _(pool):
                for e in range(N):
                    pool.wait_ge(y_ready, (e + 1) * RT)
                    pool.dma_start(ys_d[e * CAP:(e + 1) * CAP, :].rearrange("(t p) d -> p t d", p=P), y[:]).then_inc(y_stored, 16)
                pool.wait_ge(y_stored, N * 16)



PAIRS = [(0, 0), (0, 1), (1, 0), (1, 1), (0, 2), (2, 0), (1, 2), (2, 1)]


def project(nc, C, xT_d, w, qp_d, kp_d, v_all, scatter):
    with Space(nc, "proj") as s:
        wq = s.sb("wq", [P, KD, D])
        wk = s.sb("wk", [P, KD, D])
        wv = s.sb("wv", [P, KD, D])
        wd = s.sb("wd", [P, KD, LAT])
        wuk = s.sb("wuk", [LAT, D])
        wuv = s.sb("wuv", [LAT, D])
        xT = s.sb("xT", [P, 2, KD, SEQ])
        kvT = s.sb("kvT", [P, KD, SEQ])
        latT = s.sb("latT", [LAT, SEQ])
        qk = s.sb("qk", [P, 2, 2, KD, SEQ])
        rest = s.sb("rest", [P, 2, 2, KD, SEQ])
        parts = s.sb("parts", [P, 2, 2, 3, KD, SEQ], BF16)
        psQK = [[s.psum(f"ps{n}{m}", [P, SEQ]) for m in range(KD)] for n in "QK"]
        psKV = [s.psum(f"psKV{m}", [P, SEQ]) for m in range(KD)]
        psL = s.psum("psL", [P, SEQ])
        psV = s.psum("psV", [P, 2, D])
        w_in = s.sem("w_in")
        xT_in = [s.sem(f"xT_in{b}") for b in range(2)]
        kv_done = s.sem("kv_done")
        kv_ready = s.sem("kv_ready")
        lat_done = s.sem("lat_done")
        lat_ready = s.sem("lat_ready")
        v_done = s.sem("v_done")
        v_ready = s.sem("v_ready")
        made = [s.sem(f"made{j}") for j in range(2)]
        taken = [s.sem(f"taken{j}") for j in range(2)]
        high = [s.sem(f"high{j}") for j in range(2)]
        rest_ready = [s.sem(f"rest_ready{j}") for j in range(2)]
        mid = [s.sem(f"mid{j}") for j in range(2)]
        low = [s.sem(f"low{j}") for j in range(2)]
        scattered = s.sem("scattered")
        stored = [[s.sem(f"stored{j}{b}") for b in range(2)] for j in range(2)]

        def steps(eng, step):
            step(0, 0, True, False)
            step(1, 1, True, True)
            with eng.Fori(1, BATCH // 2) as i:
                step(i * 2, 0, True, True)
                step(i * 2 + 1, 1, True, True)
            step(BATCH, 0, False, True)

        with nc.Block() as block:
            @block.sync
            def _(sp):
                def load(b):
                    sp.dma_start(xT[:, b % 2], xT_d[:, b * SEQ:(b + 1) * SEQ].rearrange("(k p) t -> p k t", p=P)).then_inc(xT_in[b % 2], 16)

                sp.dma_start(wq[:], w["wq"].rearrange("(k p) n -> p k n", p=P)).then_inc(w_in, 16)
                load(0)
                for dst, src in ((wk, w["wk"]), (wv, w["wv"]), (wd, w["wd"])):
                    sp.dma_start(dst[:], src.rearrange("(k p) n -> p k n", p=P)).then_inc(w_in, 16)
                sp.dma_start(wuk[:], w["wuk"]).then_inc(w_in, 16)
                sp.dma_start(wuv[:], w["wuv"]).then_inc(w_in, 16)
                load(1)
                for b in range(BATCH + 1):
                    for j, dst, of in ((0, qp_d, b), (1, kp_d, b - 1)):
                        if 0 <= of < BATCH:
                            sp.wait_ge(low[j], of + 1)
                            sp.dma_start(dst[of].rearrange("a (m p) t -> p (a m) t", p=P),
                                         parts[:, j, of % 2].rearrange("p a m t -> p (a m) t")).then_inc(stored[j][of % 2], 16)
                    if b + 2 < BATCH:
                        sp.wait_ge(made[0], b + 1)
                        sp.wait_ge(kv_done, (b + 1) * KD)
                        load(b + 2)
                for j in range(2):
                    for slot in range(2):
                        sp.wait_ge(stored[j][slot], BATCH // 2 * 16)

            @block.tensor
            def _(pe):
                pe.wait_ge(w_in, 6 * 16)

                def step(b, slot, new, old):
                    if new:
                        pe.wait_ge(xT_in[slot], (b - slot) * 8 + 16)
                        pe.wait_ge(taken[0], b)
                        for m in range(KD):
                            for k in range(KD):
                                mm = nc.tensor.matmul(psQK[0][m][:], wq[:, k, m * P:(m + 1) * P], xT[:, slot, k],
                                                      start=(k == 0), stop=(k == KD - 1))
                        mm.then_inc(made[0], 1)
                        pe.wait_ge(kv_ready, b * KD)
                        for m in range(KD):
                            for n, ww in enumerate((wk, wv)):
                                for k in range(KD):
                                    mm = nc.tensor.matmul(psKV[m][:], ww[:, k, m * P:(m + 1) * P], xT[:, slot, k],
                                                          start=(n == 0 and k == 0), stop=(n == 1 and k == KD - 1))
                            mm.then_inc(kv_done, 1)
                    if old:
                        pe.wait_ge(lat_ready, b)
                        pe.wait_ge(taken[1], b - 1)
                        for m in range(KD):
                            mm = nc.tensor.matmul(psQK[1][m][:], wuk[:, m * P:(m + 1) * P], latT[:], start=True, stop=True)
                        mm.then_inc(made[1], 1)
                        for g in range(2):
                            pe.wait_ge(v_ready, (b - 1) * 2 + g)
                            for t in range(2):
                                mm = nc.tensor.matmul(psV[:, t], latT[:, (2 * g + t) * P:(2 * g + t + 1) * P], wuv[:], start=True, stop=True)
                            mm.then_inc(v_done, 1)
                    if new:
                        pe.wait_ge(kv_ready, (b + 1) * KD)
                        pe.wait_ge(lat_ready, b)
                        for k in range(KD):
                            mm = nc.tensor.matmul(psL[0:LAT, :], wd[:, k], kvT[:, k], start=(k == 0), stop=(k == KD - 1))
                        mm.then_inc(lat_done, 1)

                steps(pe, step)

            @block.scalar
            def _(act):
                def take_high(j, b, slot):
                    act.wait_ge(taken[j], b + 1)
                    act.wait_ge(stored[j][slot], (b - slot) * 8)
                    nc.scalar.copy(parts[:, j, slot, 0], qk[:, j, slot]).then_inc(high[j], 1)

                def take_mid(j, b, slot):
                    act.wait_ge(rest_ready[j], b + 1)
                    nc.scalar.copy(parts[:, j, slot, 1], rest[:, j, slot]).then_inc(mid[j], 1)

                def keep_v(b, g):
                    act.wait_ge(v_done, b * 2 + g + 1)
                    nc.scalar.copy(v_all[:, bass.ds(b * CPB + 2 * g, 2), :], psV[:]).then_inc(v_ready, 1)

                def step(b, slot, new, old):
                    if new:
                        take_high(0, b, slot)
                        for m in range(KD):
                            act.wait_ge(kv_done, b * KD + m + 1)
                            act.wait_ge(lat_done, b)
                            nc.scalar.copy(kvT[:, m], psKV[m][:]).then_inc(kv_ready, 1)
                    if old:
                        for g in range(2):
                            keep_v(b - 1, g)
                        take_high(1, b - 1, 1 - slot)
                    if new:
                        act.wait_ge(lat_done, b + 1)
                        act.wait_ge(v_done, b * 2)
                        nc.scalar.copy(latT[:], psL[0:LAT, :]).then_inc(lat_ready, 1)
                        take_mid(0, b, slot)
                    if old:
                        take_mid(1, b - 1, 1 - slot)

                steps(act, step)

            @block.vector
            def _(dve):
                v = nc.vector

                def take(j, b, slot):
                    dve.wait_ge(made[j], b + 1)
                    if not isinstance(b, int) or b > 1:
                        dve.wait_ge(rest_ready[j], b - 1)
                        dve.wait_ge(high[j], b - 1)
                    for m in range(KD):
                        ins = v.tensor_scalar(qk[:, j, slot, m], psQK[j][m][:], (1.0 / 16.0, 1.0)[j], None, ALU.mult)
                    ins.then_inc(taken[j], 1)

                def subtract(j, b, slot):
                    dve.wait_ge(taken[j], b + 1)
                    dve.wait_ge(high[j], b + 1)
                    if not isinstance(b, int) or b > 1:
                        dve.wait_ge(mid[j], b - 1)
                        dve.wait_ge(low[j], b - 1)
                    v.tensor_tensor(rest[:, j, slot], qk[:, j, slot], parts[:, j, slot, 0], ALU.subtract).then_inc(rest_ready[j], 1)

                def take_low(j, b, slot):
                    dve.wait_ge(mid[j], b + 1)
                    v.tensor_tensor(parts[:, j, slot, 2], rest[:, j, slot], parts[:, j, slot, 1], ALU.subtract).then_inc(low[j], 1)

                def step(b, slot, new, old):
                    if new:
                        take(0, b, slot)
                        subtract(0, b, slot)
                    if old:
                        take(1, b - 1, 1 - slot)
                        subtract(1, b - 1, 1 - slot)
                    if new:
                        take_low(0, b, slot)
                    if old:
                        take_low(1, b - 1, 1 - slot)

                steps(dve, step)

            @block.gpsimd
            def _(pool):
                scatter.start(nc, scattered)
                scatter.finish(pool, scattered)


def attend(nc, C, qp_d, kp_d, v_all, wo_d, x_d, xn_d, ys_d, choice, out_d):
    U = 2 * CPB
    TURNS = AH // 2
    PAIRS_ALL = BATCH * TURNS
    SCORE, CLIP, FADE, EXP, MIX = 13, 12, 10, 5, -2
    BANK = [0, 1, 2, 0, 1, 2, 0, 1]
    NPT = 4
    NCL = 4
    TERMS = 3
    with Space(nc, "att") as s:
        wo = s.sb("wo", [P, KD, D])
        decay = s.sb("decay", [P, CPB, SEQ])
        dist_i = s.sb("dist_i", [P, CPB, SEQ], I32)
        dist = s.sb("dist", [P, CPB, SEQ])
        qs = s.sb("qs", [P, 2, AH, SEQ], BF16)
        ks = s.sb("ks", [P, 2, AH, SEQ], BF16)
        clipped = s.sb("clipped", [P, NCL, SEQ])
        scores = s.sb("scores", [P, U, SEQ])
        top = s.sb("top", [P, 2, CPB])
        shift = s.sb("shift", [P, 2, CPB])
        prob = s.sb("prob", [P, U, SEQ])
        total = s.sb("total", [P, 2, CPB])
        inv = s.sb("inv", [P, 2, CPB])
        pT = s.sb("pT", [P, NPT, CPB, P])
        heads = s.sb("heads", [P, CPB, D])
        hT = s.sb("hT", [P, KD, SEQ])
        res = s.sb("res", [P, CPB, D])
        xn = s.sb("xn", [P, CPB, D])
        got = s.sb("got", [P, 2, CPB, D])
        out = s.sb("out", [P, CPB, D])
        psS = [s.psum(f"psS{j}", [P, SEQ]) for j in range(3)]
        psT = [s.psum(f"psT{j}", [P, CPB, P]) for j in range(2)]
        psO = [s.psum(f"psO{j}", [P, CPB, HW]) for j in range(2)]
        psE = s.psum("psE", [P, SEQ])
        wo_in = s.sem("wo_in")
        counted = s.sem("counted")
        chain0 = s.sem("chain0")
        dist_ready = s.sem("dist_ready")
        decay_ready = s.sem("decay_ready")
        stacked = [s.sem(f"stacked{j}") for j in range(2)]
        res_in = s.sem("res_in")
        xn_in = s.sem("xn_in")
        cleared = s.sem("cleared")
        gathered = s.sem("gathered")
        weighted = s.sem("weighted")
        added = s.sem("added")
        scored = s.sem("scored")
        clip_done = s.sem("clip_done")
        decayed = s.sem("decayed")
        shift_ready = s.sem("shift_ready")
        exped = s.sem("exped")
        turned = s.sem("turned")
        pT_ready = s.sem("pT_ready")
        mixed = s.sem("mixed")
        inv_ready = s.sem("inv_ready")
        heads_ready = s.sem("heads_ready")
        h_turned = s.sem("h_turned")
        hT_ready = s.sem("hT_ready")
        out_done = s.sem("out_done")
        out_ready = s.sem("out_ready")
        out_stored = s.sem("out_stored")

        def first(n):
            return isinstance(n, int) and n == 0

        def over(n):
            return isinstance(n, int) and n >= PAIRS_ALL

        with nc.Block() as block:
            @block.sync
            def _(sp):
                sp.dma_start(wo[:], wo_d.rearrange("(k p) n -> p k n", p=P)).then_inc(wo_in, 16)
                for b in range(BATCH + 1):
                    if b < BATCH:
                        if b >= 2:
                            sp.wait_ge(scored, (b - 1) * AH * CPB)
                        for j, (qa, kb) in enumerate(PAIRS):
                            for dst, src, part in ((qs, qp_d, qa), (ks, kp_d, kb)):
                                sp.dma_start(dst[HW * j:HW * (j + 1), b % 2],
                                             src[b, part].rearrange("(h e) t -> e h t", e=HW)).then_inc(stacked[b % 2], 16)
                    if b:
                        sp.wait_ge(out_ready, b * CPB)
                        sp.dma_start(out_d[(b - 1) * SEQ:b * SEQ, :].rearrange("(c p) d -> p c d", p=P), out[:]).then_inc(out_stored, 16)
                    if b < BATCH:
                        if b:
                            sp.wait_ge(added, b * TERMS)
                        sp.dma_start(res[:], x_d[b * SEQ:(b + 1) * SEQ, :].rearrange("(c p) d -> p c d", p=P)).then_inc(res_in, 16)
                        sp.dma_start(xn[:], xn_d[b * SEQ:(b + 1) * SEQ, :].rearrange("(c p) d -> p c d", p=P)).then_inc(xn_in, 16)
                sp.wait_ge(out_stored, BATCH * 16)

            @block.gpsimd
            def _(pool):
                for t in range(CPB):
                    nc.gpsimd.iota(dist_i[:, t], pattern=[[-1, SEQ]], base=t * P, channel_multiplier=1).then_inc(counted, 1)
                for b in range(BATCH):
                    if b:
                        pool.wait_ge(added, b * TERMS)
                    nc.gpsimd.memset(got[:], 0.0).then_inc(cleared, 1)
                    pool.wait_ge(cleared, b + 1)
                    for k in range(2):
                        for t in range(CPB):
                            at = b * CPB + t
                            nc.gpsimd.indirect_dma_start(
                                out=got[:, k, t, :], out_offset=None, in_=ys_d,
                                in_offset=bass.IndirectOffsetOnAxis(ap=choice.slot[k][:, at:at + 1], axis=0),
                                bounds_check=L1_ROWS - 1, oob_is_err=False).then_inc(gathered, 16)
                    pool.wait_ge(res_in, (b + 1) * 16)
                    pool.wait_ge(xn_in, (b + 1) * 16)
                    pool.wait_ge(gathered, (b + 1) * 2 * CPB * 16)
                    terms = [(got[:, 0], choice.weight[0]), (got[:, 1], choice.weight[1]), (xn[:], choice.passed)]
                    for rows_of, factor in terms:
                        nc.gpsimd.tensor_tensor(rows_of, rows_of, factor[:, b * CPB:(b + 1) * CPB].unsqueeze(2).to_broadcast([P, CPB, D]),
                                                ALU.mult).then_inc(weighted, 1)
                    for n, (rows_of, factor) in enumerate(terms):
                        pool.wait_ge(weighted, b * TERMS + n + 1)
                        if n:
                            pool.wait_ge(added, b * TERMS + n)
                        nc.gpsimd.tensor_tensor(res[:], res[:], rows_of, ALU.add).then_inc(added, 1)

            @block.tensor
            def _(pe):
                def score(n, b, slot, hp, u):
                    g, t = u // CPB, u % CPB
                    if u >= 3:
                        pe.wait_ge(clip_done, n * U + u - 2)
                    elif not first(n):
                        pe.wait_ge(clip_done, n * U - 1 + min(u, 1))
                    if isinstance(hp, int) and hp == 0 and u == 0:
                        pe.wait_ge(stacked[slot], (b - slot) * (len(PAIRS) * 16) + 2 * len(PAIRS) * 16)
                    nc.tensor.matmul(psS[BANK[u]][:], qs[:, slot, bass.ds(hp * 2 + g, 1), t * P:(t + 1) * P].rearrange("p a t -> p (a t)"),
                                     ks[:, slot, bass.ds(hp * 2 + g, 1), :].rearrange("p a t -> p (a t)"),
                                     start=True, stop=True).then_inc(scored, 1)

                def turn(n, u):
                    pe.wait_ge(exped, n * U + u + 1)
                    if not first(n) or u >= 2:
                        pe.wait_ge(pT_ready, n * U + u - 1)
                    for q in range(CPB):
                        mm = nc.tensor.transpose(psT[u % 2][:, q], prob[:, u, q * P:(q + 1) * P], C.ident[:])
                    mm.then_inc(turned, 1)

                def mix(n, b, hp, u):
                    g, t = u // CPB, u % CPB
                    pe.wait_ge(pT_ready, n * U + u + 1)
                    if t == 0 and not first(n):
                        pe.wait_ge(heads_ready, n * 2 - 1 + g)
                    for q in range(CPB):
                        mm = nc.tensor.matmul(psO[g][:, t], pT[:, u % NPT, q],
                                              v_all[:, bass.ds(b * CPB + q, 1), bass.ds((hp * 2 + g) * HW, HW)].rearrange("p a e -> p (a e)"),
                                              start=(q == 0), stop=(q == CPB - 1))
                    mm.then_inc(mixed, 1)

                def turn_heads(b, k):
                    pe.wait_ge(heads_ready, (b + 1) * AH)
                    pe.wait_ge(hT_ready, b * KD + k)
                    pe.wait_ge(out_ready, b * CPB)
                    for t in range(CPB):
                        mm = nc.tensor.transpose(psE[:, t * P:(t + 1) * P], heads[:, t, k * P:(k + 1) * P], C.ident[:])
                    mm.then_inc(h_turned, 1)

                def project_out(b, t):
                    pe.wait_ge(hT_ready, (b + 1) * KD)
                    pe.wait_ge(out_ready, b * CPB + t)
                    for k in range(KD):
                        mm = nc.tensor.matmul(psE[:, 0:D], hT[:, k, t * P:(t + 1) * P], wo[:, k],
                                              start=(k == 0), stop=(k == KD - 1))
                    mm.then_inc(out_done, 1)

                def pair(b, slot, hp, extra=lambda u: None):
                    n = b * TURNS + hp
                    for u in range(U):
                        turn(n, u)
                        far, at = divmod(u + SCORE, U)
                        if not over(n + far):
                            if isinstance(hp, int) and hp + far >= TURNS:
                                score(n + far, b + 1, 1 - slot, hp + far - TURNS, at)
                            else:
                                score(n + far, b, slot, hp + far, at)
                        if u + MIX >= 0:
                            mix(n, b, hp, u + MIX)
                        elif isinstance(hp, int) and hp == 0:
                            if not first(n):
                                mix(n - 1, b - 1, TURNS - 1, u + MIX + U)
                        else:
                            mix(n - 1, b, hp - 1, u + MIX + U)
                        extra(u)

                def batch(b, slot):
                    def turn_last(u):
                        if u in (4, 6):
                            turn_heads(b - 1, (u - 4) // 2)

                    def project_last(u):
                        if u % 2 == 0:
                            project_out(b - 1, u // 2)

                    if first(b):
                        pair(b, slot, 0)
                        pair(b, slot, 1)
                    else:
                        pair(b, slot, 0, turn_last)
                        pair(b, slot, 1, project_last)
                    with pe.Fori(2, TURNS - 2) as hp:
                        pair(b, slot, hp)
                    pair(b, slot, TURNS - 2)
                    pair(b, slot, TURNS - 1)

                pe.wait_ge(wo_in, 16)
                for k in range(SCORE):
                    score(k // U, 0, 0, k // U, k % U)
                batch(0, 0)
                with pe.Fori(0, BATCH // 2 - 1) as i:
                    batch(i * 2 + 1, 1)
                    batch(i * 2 + 2, 0)
                batch(BATCH - 1, 1)
                for u in range(U + MIX, U):
                    mix(PAIRS_ALL - 1, BATCH - 1, TURNS - 1, u)
                for k in range(KD):
                    turn_heads(BATCH - 1, k)
                for t in range(CPB):
                    project_out(BATCH - 1, t)

            @block.scalar
            def _(act):
                def exp(n, u):
                    g, t = u // CPB, u % CPB
                    if t == 0:
                        if not first(n):
                            act.wait_ge(inv_ready, n * 2 - 1 + g)
                        act.wait_ge(shift_ready, n * 2 + g + 1)
                    if not first(n):
                        act.wait_ge(turned, (n - 1) * U + u + 1)
                    nc.scalar.activation(prob[:, u], scores[:, u], ACT.Exp, bias=shift[:, g, t:t + 1],
                                         accum_out=total[:, g, t:t + 1]).then_inc(exped, 1)

                def copy(n, u):
                    act.wait_ge(turned, n * U + u + 1)
                    if not first(n) or u >= NPT:
                        act.wait_ge(mixed, n * U + u + 1 - NPT)
                    nc.scalar.copy(pT[:, u % NPT], psT[u % 2][:]).then_inc(pT_ready, 1)

                def copy_heads(b, k):
                    act.wait_ge(h_turned, b * KD + k + 1)
                    act.wait_ge(out_done, b * CPB)
                    nc.scalar.copy(hT[:, k], psE[:]).then_inc(hT_ready, 1)

                def pair(n, b=None):
                    for u in range(U):
                        far, at = divmod(u + EXP, U)
                        if not over(n + far):
                            exp(n + far, at)
                        copy(n, u)
                        if b is not None and u in (5, 7):
                            copy_heads(b, (u - 5) // 2)

                act.wait_ge(dist_ready, 1)
                nc.scalar.activation(decay[:], dist[:], ACT.Exp, scale=-DECAY).then_inc(decay_ready, 1)
                for k in range(EXP):
                    exp(0, k)
                pair(0)
                with act.Fori(1, BATCH) as b:
                    with act.Fori(0, TURNS - 1) as hp:
                        pair((b - 1) * TURNS + 1 + hp)
                    pair(b * TURNS, b - 1)
                with act.Fori(0, TURNS - 2) as hp:
                    pair((BATCH - 1) * TURNS + 1 + hp)
                pair(PAIRS_ALL - 1)
                for k in range(KD):
                    copy_heads(BATCH - 1, k)

            @block.vector
            def _(dve):
                v = nc.vector

                def clip(n, u):
                    dve.wait_ge(scored, n * U + u + 1)
                    if not first(n) or u >= NCL:
                        dve.wait_ge(decayed, n * U + u + 1 - NCL)
                    v.tensor_scalar(clipped[:, u % NCL], psS[BANK[u]][:], -CLAMP, CLAMP, ALU.max, ALU.min).then_inc(clip_done, 1)

                def before_fade(n, u):
                    dve.wait_ge(clip_done, n * U + u + 1)
                    if not first(n):
                        dve.wait_ge(exped, (n - 1) * U + u + 1)

                def fade(n, u):
                    g, t = u // CPB, u % CPB
                    v.tensor_tensor_reduce(scores[:, u], clipped[:, u % NCL], decay[:, t], 1.0, -2.0 * CLAMP,
                                           ALU.mult, ALU.max, top[:, g, t:t + 1]).then_inc(decayed, 1)

                def negate(n, u):
                    g = u // CPB
                    if u % CPB == CPB - 1:
                        dve.wait_ge(decayed, n * U + u + 1)
                        v.tensor_scalar(shift[:, g], top[:, g], -1.0, None, ALU.mult).then_inc(shift_ready, 1)

                def reciprocals(n, g):
                    dve.wait_ge(exped, n * U + (g + 1) * CPB)
                    if not first(n):
                        dve.wait_ge(heads_ready, n * 2 - 1 + g)
                    v.reciprocal(inv[:, g], total[:, g]).then_inc(inv_ready, 1)

                def normalise_heads(n, b, hp, g):
                    dve.wait_ge(inv_ready, n * 2 + g + 1)
                    dve.wait_ge(mixed, n * U + (g + 1) * CPB)
                    if isinstance(hp, int) and hp == 0 and g == 0:
                        dve.wait_ge(h_turned, b * KD)
                    v.tensor_tensor(heads[:, :, bass.ds((hp * 2 + g) * HW, HW)], psO[g][:],
                                    inv[:, g].unsqueeze(2).to_broadcast([P, CPB, HW]), ALU.mult).then_inc(heads_ready, 1)

                def result(b, t):
                    if t == 0:
                        dve.wait_ge(added, (b + 1) * TERMS)
                        dve.wait_ge(out_stored, b * 16)
                    dve.wait_ge(out_done, b * CPB + t + 1)
                    v.tensor_tensor(out[:, t], psE[:, 0:D], res[:, t], ALU.add).then_inc(out_ready, 1)

                def pair(b, hp, results=False):
                    n = b * TURNS + hp
                    for u in range(U):
                        far_f, at_f = divmod(u + FADE, U)
                        far_c, at_c = divmod(u + CLIP, U)
                        far_s, at_s = divmod(u + FADE - 1, U)
                        if u == 3 and not first(n):
                            normalise_heads(n - 1, b, TURNS - 1 if isinstance(hp, int) and hp == 0 else hp - 1, 1)
                        if u == 7:
                            normalise_heads(n, b, hp, 0)
                        if u in (0, 4):
                            reciprocals(n, u // 4)
                        if not over(n + far_f):
                            before_fade(n + far_f, at_f)
                        if not over(n + far_c):
                            clip(n + far_c, at_c)
                        if not over(n + far_s):
                            negate(n + far_s, at_s)
                        if not over(n + far_f):
                            fade(n + far_f, at_f)
                        if results and u % 2 == 1:
                            result(b - 1, u // 2)

                c0 = Chain(dve, chain0)
                dve.wait_ge(counted, CPB)
                c0.step(v.tensor_copy(scores[:, 0:CPB], dist_i[:]))
                v.scalar_tensor_tensor(out=dist[:], in0=scores[:, 0:CPB], scalar=-1.0, in1=scores[:, 0:CPB],
                                       op0=ALU.mult, op1=ALU.max).then_inc(dist_ready, 1)
                dve.wait_ge(decay_ready, 1)
                dve.wait_ge(dist_ready, 1)
                lag = CLIP - FADE
                for k in range(lag):
                    clip(0, k)
                for k in range(FADE):
                    before_fade(k // U, k % U)
                    clip((k + lag) // U, (k + lag) % U)
                    if k:
                        negate((k - 1) // U, (k - 1) % U)
                    fade(k // U, k % U)
                pair(0, 0)
                pair(0, 1)
                with dve.Fori(2, TURNS) as hp:
                    pair(0, hp)
                with dve.Fori(1, BATCH - 1) as b:
                    pair(b, 0)
                    pair(b, 1, results=True)
                    with dve.Fori(2, TURNS) as hp:
                        pair(b, hp)
                pair(BATCH - 1, 0)
                pair(BATCH - 1, 1, results=True)
                with dve.Fori(2, TURNS - 2) as hp:
                    pair(BATCH - 1, hp)
                pair(BATCH - 1, TURNS - 2)
                pair(BATCH - 1, TURNS - 1)
                normalise_heads(PAIRS_ALL - 1, BATCH - 1, TURNS - 1, 1)
                for t in range(CPB):
                    result(BATCH - 1, t)




def build(nc, a, out_d):

    def dram(name, shape, dt=F32):
        return nc.dram_tensor(name, shape, dt).ap()

    xnT0_d, xnT1_d = dram("xnT0", (D, TOK)), dram("xnT1", (D, TOK))
    mixed_d, x1_d, xn1_d = dram("mixed", (TOK, D)), dram("x1", (TOK, D)), dram("xn1", (TOK, D))
    xs0_d, ys0_d = dram("xs0", (L0_ROWS, D)), dram("ys0", (L0_ROWS, D))
    xs1_d, ys1_d = dram("xs1", (L1_ROWS, D)), dram("ys1", (L1_ROWS, D))
    qp_d, kp_d = (dram(n, (BATCH, 3, D, SEQ), BF16) for n in ("q_parts", "k_parts"))
    N2 = 2 * NH

    with ExitStack() as kept:
        def keep(where, name, shape, dt=F32):
            return where.enter_context(nc.sbuf_tensor(name, shape, dt))

        C = Constants()
        constants(nc, kept, C)
        choice0 = Choice()
        choice0.slot = [keep(kept, "slot0", [P, NT], I32)]
        choice0.gate = keep(kept, "gate0", [P, NT])
        choice0.tile_expert = keep(kept, "tile_expert", [P, L0_TILES], I32)
        with ExitStack() as mem:
            dt, step_a = keep(mem, "dt", [P, NT, N2]), keep(mem, "step_a", [P, NT, N2])
            xn_all = keep(mem, "xn_all0", [P, NT, D])
            with ExitStack() as mem0:
                logits = keep(mem0, "logits0", [P, NT, NE + N2])
                normalise(nc, C, "norm0", a["u"], a["router_dt"], NE + N2, logits, xn_all, xnT0_d)
                scatter0 = route(nc, C, "route0", logits, a["br_bc"], xn_all, xs0_d, True, choice0)
                time_steps(nc, C, logits, a["dt_bias_bc"], a["a_log_bc"], dt, step_a)
            mamba(nc, C, xnT0_d, a["u"], a, dt, step_a, mixed_d, scatter0)
        one_expert_each(nc, C, a["w1"], a["b1_bc"], a["w2"], a["b2_bc"], choice0.tile_expert, xs0_d, ys0_d)
        choice1 = Choice()
        choice1.slot = [keep(kept, f"slot1{k}", [P, NT], I32) for k in range(2)]
        choice1.weight = [keep(kept, f"weight1{k}", [P, NT]) for k in range(2)]
        choice1.passed = keep(kept, "passed", [P, NT])
        v_all = keep(kept, "v_all", [P, NT, D])
        with ExitStack() as mem:
            logits = keep(mem, "logits1", [P, NT, NE])
            xn_all = keep(mem, "xn_all1", [P, NT, D])
            normalise(nc, C, "norm1", mixed_d, a["router1"], NE, logits, xn_all, xnT1_d,
                      merge=(ys0_d, choice0.slot[0], L0_ROWS, choice0.gate, x1_d, xn1_d))
            scatter1 = route(nc, C, "route1", logits, a["br1_bc"], xn_all, xs1_d, False, choice1)
            project(nc, C, xnT1_d, a, qp_d, kp_d, v_all, scatter1)
        full_experts(nc, C, a["inter"], a["outer"], xs1_d, ys1_d)
        attend(nc, C, qp_d, kp_d, v_all, a["wo"], x1_d, xn1_d, ys1_d, choice1, out_d)


def kernel(**inputs):
    import concourse.bacc as bacc
    import numpy as np
    from concourse.bass_utils import run_bass_kernel_spmd

    g = {n: np.asarray(x) for n, x in inputs.items()}

    def rows(x):
        return np.ascontiguousarray(np.broadcast_to(x.reshape(1, -1), (P, x.size)))

    def column(x):
        return np.ascontiguousarray(x.reshape(-1, P).T)

    in_T = np.ascontiguousarray(g["L0_attn_in_proj_w"].T)
    arrays = {
        "u": g["L0_attn_u"].reshape(TOK, D),
        "router_dt": np.ascontiguousarray(np.concatenate([g["L0_ffn_Wr"], in_T[:, DI + CONV:]], axis=1)),
        "in_T": in_T,
        "out_T": np.ascontiguousarray(g["L0_attn_out_proj_w"].T),
        "norm_col": column(g["L0_attn_norm_w"]),
        "fcd_T": np.ascontiguousarray(g["L0_attn_fc_D_w"].T),
        "taps": np.ascontiguousarray(g["L0_attn_conv_w"].reshape(CT, P, TAPS).transpose(1, 0, 2)),
        "conv_b": column(g["L0_attn_conv_b"]),
        "d_bc": rows(g["L0_attn_D"]),
        "d_col": column(np.repeat(g["L0_attn_D"], HD)),
        "dt_bias_bc": rows(np.concatenate([g["L0_attn_dt_bias"]] * 2)),
        "a_log_bc": rows(np.concatenate([g["L0_attn_A_log"]] * 2)),
        "br_bc": rows(g["L0_ffn_br"]),
        "w1": g["L0_ffn_W1"], "b1_bc": rows(g["L0_ffn_b1"]),
        "w2": g["L0_ffn_W2"], "b2_bc": rows(g["L0_ffn_b2"]),
        "wq": g["L1_attn_Wq"], "wk": g["L1_attn_Wk"], "wv": g["L1_attn_Wv"], "wo": g["L1_attn_Wo"],
        "wd": g["L1_attn_W_down_kv"], "wuk": g["L1_attn_W_up_k"], "wuv": g["L1_attn_W_up_v"],
        "router1": np.ascontiguousarray(g["L1_ffn_router_w"].T),
        "br1_bc": rows(g["L1_ffn_router_b"]),
        "inter": g["L1_ffn_experts_inter"], "outer": g["L1_ffn_experts_out"],
    }
    nc = bacc.Bacc("TRN2", target_bir_lowering=False, num_devices=1)
    a = {n: nc.dram_tensor(f"in_{n}", x.shape, mybir.dt.from_np(x.dtype), kind="ExternalInput").ap()
         for n, x in arrays.items()}
    out_d = nc.dram_tensor("out", (TOK, D), F32, kind="ExternalOutput").ap()
    build(nc, a, out_d)
    done = run_bass_kernel_spmd(nc, [{f"in_{n}": x for n, x in arrays.items()}], core_ids=[0])
    return done.results[0]["out"].reshape(BATCH, SEQ, D)
```
